# Optimizing a Trainium2 kernel written in Bass

```python
import numpy as np
import jax
import jax.numpy as jnp

def _softmax(x, axis=-1):
    return jax.nn.softmax(x, axis=axis)

def _gelu(x):
    return jax.nn.gelu(x, approximate=True)

def _silu(x):
    return jax.nn.silu(x)

def _sigmoid(x):
    return jax.nn.sigmoid(x)

def _layernorm(x, axis=-1, eps=1e-05):
    m = jnp.mean(x, axis=axis, keepdims=True)
    v = jnp.var(x, axis=axis, keepdims=True)
    return (x - m) / jnp.sqrt(v + eps)

def _scatter_add(tgt, idx, src, axis=0):
    return tgt.at[idx].add(src)

def _segment_sum(src, seg, n):
    return jax.ops.segment_sum(src, seg, n)
kernel_name = 'mk_decoder_preln_d1_seqx_r4_c51dd8'

def setup_inputs(seed: int=0):
    np.random.seed(seed)
    _w = jnp.asarray

    def _rec_inputs():
        import jax
        import jax.numpy as jnp
        _rk = jax.random.key(seed)
        x = -0.000125 + 0.9999 * jax.random.normal(jax.random.fold_in(_rk, 1), (8, 256, 256), jnp.float32)
        _lenS = 256 - jax.random.randint(jax.random.fold_in(_rk, 7), (8,), 0, max(1, 256 // 4) + 1, jnp.int32)
        _lenS2 = 256 - jax.random.randint(jax.random.fold_in(_rk, 8), (8,), 0, max(1, 256 // 4) + 1, jnp.int32)
        _ctx_768P = jax.random.normal(jax.random.fold_in(_rk, 11), (8, 16, 192), jnp.float32)
        _ctx_768c = jax.random.dirichlet(jax.random.fold_in(_rk, 511), 0.3 * jnp.ones((16,), jnp.float32), (8, 256))
        _ctx_768t = jnp.einsum('bsk,bkd->bsd', _ctx_768c, _ctx_768P)
        _ctx_768t = _ctx_768t * jax.lax.rsqrt(jnp.mean(jnp.square(_ctx_768t)) + 1e-12) * 0.953939
        ctx_768 = -7.36909e-05 + 0.999899 * (_ctx_768t + 0.3 * jax.random.normal(jax.random.fold_in(_rk, 611), (8, 256, 192), jnp.float32))
        return (x, ctx_768)
    x, ctx_768 = _rec_inputs()

    def _L0_attn_setup():
        import jax, jax.numpy as jnp
        import numpy as np
        D_MODEL = 256
        NUM_HEADS = 16
        DEPTH = D_MODEL // NUM_HEADS
        MAX_LEN = 1250
        EPS = 1e-06

        def _make_rel_pos_emb():
            pos = np.arange(-MAX_LEN, MAX_LEN + 1, dtype=np.float32)[:, None]
            dim = np.arange(D_MODEL, dtype=np.float32)[None, :]
            angle = pos / 2500 ** (2 * (dim // 2) / D_MODEL)
            pe = np.where(dim % 2 == 0, np.sin(angle), np.cos(angle)).astype(np.float32)
            return jnp.asarray(pe)

        def _rel_shift(x):
            B, H, L, _ = x.shape
            x_padded = jnp.pad(x, ((0, 0), (0, 0), (0, 0), (1, 0)))
            x_padded = x_padded.reshape(B, H, 2 * L, L)
            x_shifted = x_padded[:, :, 1:, :].reshape(B, H, L, 2 * L - 1)
            return x_shifted[:, :, :, :L]
        key = jax.random.key(seed)
        ks = jax.random.split(key, 8)
        B, L = (2, 256)
        s = 1.0 / np.sqrt(D_MODEL)
        return {'x': jax.random.normal(ks[0], (B, L, D_MODEL), jnp.float32), 'gamma': jnp.ones((D_MODEL,), jnp.float32), 'beta': jnp.zeros((D_MODEL,), jnp.float32), 'Wq': jax.random.normal(ks[1], (D_MODEL, D_MODEL), jnp.float32) * s, 'Wk': jax.random.normal(ks[2], (D_MODEL, D_MODEL), jnp.float32) * s, 'Wv': jax.random.normal(ks[3], (D_MODEL, D_MODEL), jnp.float32) * s, 'Wr': jax.random.normal(ks[4], (D_MODEL, D_MODEL), jnp.float32) * s, 'u_bias': jax.random.normal(ks[5], (NUM_HEADS, DEPTH), jnp.float32) * 0.02, 'v_bias': jax.random.normal(ks[6], (NUM_HEADS, DEPTH), jnp.float32) * 0.02, 'Wo': jax.random.normal(ks[7], (D_MODEL, D_MODEL), jnp.float32) * s, 'bo': jnp.zeros((D_MODEL,), jnp.float32), 'rel_pos_emb': _make_rel_pos_emb()}
    _L0_attn_all = _L0_attn_setup()
    _L0_attn_in = {k: v for k, v in _L0_attn_all.items() if k in ('gamma', 'beta', 'Wq', 'Wk', 'Wv', 'Wr', 'u_bias', 'v_bias', 'Wo', 'bo', 'rel_pos_emb')}
    del _L0_attn_all

    def _L0_xattn_setup():
        import jax, jax.numpy as jnp
        import numpy as np
        import math
        E = 256
        EV = 256
        FFN = 1024
        DINO = 192
        B, S, P = (64, 128, 64)

        def bitnet_linear(x, W, b):
            w_scale = jnp.maximum(jnp.mean(jnp.abs(W)), 1e-05)
            qW = jnp.sign(W) * (jnp.abs(W) > 0.5 * w_scale).astype(W.dtype)
            i_scale = jnp.maximum(jnp.max(jnp.abs(x)), 1e-08) / 127.0
            qx = jnp.clip(jnp.round(x / i_scale), -128.0, 127.0)
            out = jnp.einsum('...i,oi->...o', qx, qW) * (w_scale * i_scale)
            return out + b
        key = jax.random.key(seed)
        ks = iter(jax.random.split(key, 32))

        def lin_w(fin, fout):
            return jax.random.normal(next(ks), (fout, fin), jnp.float32) * math.sqrt(2.0 / fin)
        return {'text_embeddings': jax.random.normal(next(ks), (B, S, E), jnp.float32), 'dinov2_features': jax.random.normal(next(ks), (B, P, DINO), jnp.float32), 'W_d2v': lin_w(DINO, EV), 'b_d2v': jnp.zeros((EV,), jnp.float32), 'W_img': lin_w(EV, E), 'b_img': jnp.zeros((E,), jnp.float32), 'W_txt': lin_w(E, E), 'b_txt': jnp.zeros((E,), jnp.float32), 'W_att0': lin_w(E, E // 2), 'b_att0': jnp.zeros((E // 2,), jnp.float32), 'W_att1': lin_w(E, E // 2), 'b_att1': jnp.zeros((E // 2,), jnp.float32), 'W_f1': lin_w(2 * E, FFN), 'b_f1': jnp.zeros((FFN,), jnp.float32), 'W_f2': lin_w(FFN, E), 'b_f2': jnp.zeros((E,), jnp.float32)}
    _L0_xattn_all = _L0_xattn_setup()
    _L0_xattn_in = {k: v for k, v in _L0_xattn_all.items() if k in ('W_d2v', 'b_d2v', 'W_img', 'b_img', 'W_txt', 'b_txt', 'W_att0', 'b_att0', 'W_att1', 'b_att1', 'W_f1', 'b_f1', 'W_f2', 'b_f2')}
    del _L0_xattn_all

    def _L0_ffn_setup():
        import jax, jax.numpy as jnp
        import numpy as np
        D_MODEL, D_FF, N_EXP = (256, 1024, 8)
        key = jax.random.key(seed)
        ks = jax.random.split(key, 8)
        s = lambda fan_in: 1.0 / np.sqrt(fan_in)
        x = jax.random.normal(ks[0], (4, 512, D_MODEL), dtype=jnp.float32)
        Wr = jax.random.uniform(ks[1], (N_EXP, D_MODEL), jnp.float32, -s(D_MODEL), s(D_MODEL))
        br = jax.random.uniform(ks[2], (N_EXP,), jnp.float32, -s(D_MODEL), s(D_MODEL))
        W1 = jax.random.uniform(ks[3], (N_EXP, D_FF, D_MODEL), jnp.float32, -s(D_MODEL), s(D_MODEL))
        b1 = jax.random.uniform(ks[4], (N_EXP, D_FF), jnp.float32, -s(D_MODEL), s(D_MODEL))
        W2 = jax.random.uniform(ks[5], (N_EXP, D_MODEL, D_FF), jnp.float32, -s(D_FF), s(D_FF))
        b2 = jax.random.uniform(ks[6], (N_EXP, D_MODEL), jnp.float32, -s(D_FF), s(D_FF))
        return {'x': x, 'Wr': Wr, 'br': br, 'W1': W1, 'b1': b1, 'W2': W2, 'b2': b2}
    _L0_ffn_all = _L0_ffn_setup()
    _L0_ffn_in = {k: v for k, v in _L0_ffn_all.items() if k in ('Wr', 'br', 'W1', 'b1', 'W2', 'b2')}
    del _L0_ffn_all
    return {'x': x, 'ctx_768': ctx_768, 'L0_attn_gamma': _L0_attn_in['gamma'], 'L0_attn_beta': _L0_attn_in['beta'], 'L0_attn_Wq': _L0_attn_in['Wq'], 'L0_attn_Wk': _L0_attn_in['Wk'], 'L0_attn_Wv': _L0_attn_in['Wv'], 'L0_attn_Wr': _L0_attn_in['Wr'], 'L0_attn_u_bias': _L0_attn_in['u_bias'], 'L0_attn_v_bias': _L0_attn_in['v_bias'], 'L0_attn_Wo': _L0_attn_in['Wo'], 'L0_attn_bo': _L0_attn_in['bo'], 'L0_attn_rel_pos_emb': _L0_attn_in['rel_pos_emb'], 'L0_xattn_W_d2v': _L0_xattn_in['W_d2v'], 'L0_xattn_b_d2v': _L0_xattn_in['b_d2v'], 'L0_xattn_W_img': _L0_xattn_in['W_img'], 'L0_xattn_b_img': _L0_xattn_in['b_img'], 'L0_xattn_W_txt': _L0_xattn_in['W_txt'], 'L0_xattn_b_txt': _L0_xattn_in['b_txt'], 'L0_xattn_W_att0': _L0_xattn_in['W_att0'], 'L0_xattn_b_att0': _L0_xattn_in['b_att0'], 'L0_xattn_W_att1': _L0_xattn_in['W_att1'], 'L0_xattn_b_att1': _L0_xattn_in['b_att1'], 'L0_xattn_W_f1': _L0_xattn_in['W_f1'], 'L0_xattn_b_f1': _L0_xattn_in['b_f1'], 'L0_xattn_W_f2': _L0_xattn_in['W_f2'], 'L0_xattn_b_f2': _L0_xattn_in['b_f2'], 'L0_ffn_Wr': _L0_ffn_in['Wr'], 'L0_ffn_br': _L0_ffn_in['br'], 'L0_ffn_W1': _L0_ffn_in['W1'], 'L0_ffn_b1': _L0_ffn_in['b1'], 'L0_ffn_W2': _L0_ffn_in['W2'], 'L0_ffn_b2': _L0_ffn_in['b2']}

def reference(x, ctx_768, L0_attn_gamma, L0_attn_beta, L0_attn_Wq, L0_attn_Wk, L0_attn_Wv, L0_attn_Wr, L0_attn_u_bias, L0_attn_v_bias, L0_attn_Wo, L0_attn_bo, L0_attn_rel_pos_emb, L0_xattn_W_d2v, L0_xattn_b_d2v, L0_xattn_W_img, L0_xattn_b_img, L0_xattn_W_txt, L0_xattn_b_txt, L0_xattn_W_att0, L0_xattn_b_att0, L0_xattn_W_att1, L0_xattn_b_att1, L0_xattn_W_f1, L0_xattn_b_f1, L0_xattn_W_f2, L0_xattn_b_f2, L0_ffn_Wr, L0_ffn_br, L0_ffn_W1, L0_ffn_b1, L0_ffn_W2, L0_ffn_b2):
    import jax
    import jax.numpy as jnp

    def _L0_attn_ref(x, gamma, beta, Wq, Wk, Wv, Wr, u_bias, v_bias, Wo, bo, rel_pos_emb):
        import jax, jax.numpy as jnp
        import numpy as np
        D_MODEL = 256
        NUM_HEADS = 16
        DEPTH = D_MODEL // NUM_HEADS
        MAX_LEN = 1250
        EPS = 1e-06

        def _make_rel_pos_emb():
            pos = np.arange(-MAX_LEN, MAX_LEN + 1, dtype=np.float32)[:, None]
            dim = np.arange(D_MODEL, dtype=np.float32)[None, :]
            angle = pos / 2500 ** (2 * (dim // 2) / D_MODEL)
            pe = np.where(dim % 2 == 0, np.sin(angle), np.cos(angle)).astype(np.float32)
            return jnp.asarray(pe)

        def _rel_shift(x):
            B, H, L, _ = x.shape
            x_padded = jnp.pad(x, ((0, 0), (0, 0), (0, 0), (1, 0)))
            x_padded = x_padded.reshape(B, H, 2 * L, L)
            x_shifted = x_padded[:, :, 1:, :].reshape(B, H, L, 2 * L - 1)
            return x_shifted[:, :, :, :L]
        B, L, _ = x.shape
        mu = jnp.mean(x, axis=-1, keepdims=True)
        var = jnp.mean(jnp.square(x - mu), axis=-1, keepdims=True)
        xn = (x - mu) * jax.lax.rsqrt(var + EPS) * gamma + beta

        def heads(t):
            return t.reshape(B, L, NUM_HEADS, DEPTH).transpose(0, 2, 1, 3)
        q = heads(xn @ Wq)
        k = heads(xn @ Wk)
        v = heads(xn @ Wv)
        idx = jnp.arange(2 * L - 1) - (L - 1) + MAX_LEN
        r_emb = rel_pos_emb[idx]
        r = (r_emb @ Wr).reshape(2 * L - 1, NUM_HEADS, DEPTH).transpose(1, 0, 2)
        AC = jnp.einsum('bhld,bhmd->bhlm', q + u_bias[None, :, None, :], k)
        BD = jnp.einsum('bhld,hrd->bhlr', q + v_bias[None, :, None, :], r)
        score = (AC + _rel_shift(BD)) / jnp.sqrt(jnp.float32(DEPTH))
        attn = jax.nn.softmax(score, axis=-1)
        out = jnp.einsum('bhlm,bhmd->bhld', attn, v)
        out = out.transpose(0, 2, 1, 3).reshape(B, L, D_MODEL)
        return out @ Wo + bo

    def _L0_xattn_ref(text_embeddings, dinov2_features, W_d2v, b_d2v, W_img, b_img, W_txt, b_txt, W_att0, b_att0, W_att1, b_att1, W_f1, b_f1, W_f2, b_f2):
        import jax, jax.numpy as jnp
        import numpy as np
        import math
        E = 256
        EV = 256
        FFN = 1024
        DINO = 192
        B, S, P = (64, 128, 64)

        def bitnet_linear(x, W, b):
            w_scale = jnp.maximum(jnp.mean(jnp.abs(W)), 1e-05)
            qW = jnp.sign(W) * (jnp.abs(W) > 0.5 * w_scale).astype(W.dtype)
            i_scale = jnp.maximum(jnp.max(jnp.abs(x)), 1e-08) / 127.0
            qx = jnp.clip(jnp.round(x / i_scale), -128.0, 127.0)
            out = jnp.einsum('...i,oi->...o', qx, qW) * (w_scale * i_scale)
            return out + b
        b, s, e = text_embeddings.shape
        vis = bitnet_linear(dinov2_features, W_d2v, b_d2v)
        image_embeds = bitnet_linear(vis, W_img, b_img)
        fused = bitnet_linear(text_embeddings, W_txt, b_txt)
        inv_sqrt_e = 1.0 / math.sqrt(e)
        for Wa, ba in ((W_att0, b_att0), (W_att1, b_att1)):
            kv = bitnet_linear(image_embeds, Wa, ba)
            k = jnp.concatenate([kv, kv], axis=-1)
            scores = jnp.einsum('bse,bpe->bsp', fused, k) * inv_sqrt_e
            attn = jax.nn.softmax(scores, axis=-1)
            fused = fused + 0.1 * jnp.einsum('bsp,bpe->bse', attn, k)
        avg_img = jnp.mean(image_embeds, axis=1, keepdims=True)
        concatenated = jnp.concatenate([fused, jnp.broadcast_to(avg_img, (b, s, e))], axis=-1)
        h = jax.nn.relu(bitnet_linear(concatenated, W_f1, b_f1))
        return bitnet_linear(h, W_f2, b_f2)

    def _L0_ffn_ref(x, Wr, br, W1, b1, W2, b2):
        import jax, jax.numpy as jnp
        import numpy as np
        D_MODEL, D_FF, N_EXP = (256, 1024, 8)
        B, S, D = x.shape
        xf = x.reshape(-1, D)
        logits = xf @ Wr.T + br
        expert_idx = jnp.argmax(logits, axis=-1)
        h = jax.nn.relu(jnp.einsum('td,efd->etf', xf, W1) + b1[:, None, :])
        y = jnp.einsum('etf,edf->etd', h, W2) + b2[:, None, :]
        out = y[expert_idx, jnp.arange(xf.shape[0])]
        return out.reshape(B, S, D)
    x = x + _L0_attn_ref(_layernorm(x, axis=-1), L0_attn_gamma, L0_attn_beta, L0_attn_Wq, L0_attn_Wk, L0_attn_Wv, L0_attn_Wr, L0_attn_u_bias, L0_attn_v_bias, L0_attn_Wo, L0_attn_bo, L0_attn_rel_pos_emb)
    x = x + _L0_xattn_ref(_layernorm(x, axis=-1), ctx_768, L0_xattn_W_d2v, L0_xattn_b_d2v, L0_xattn_W_img, L0_xattn_b_img, L0_xattn_W_txt, L0_xattn_b_txt, L0_xattn_W_att0, L0_xattn_b_att0, L0_xattn_W_att1, L0_xattn_b_att1, L0_xattn_W_f1, L0_xattn_b_f1, L0_xattn_W_f2, L0_xattn_b_f2)
    x = x + _L0_ffn_ref(_layernorm(x, axis=-1), L0_ffn_Wr, L0_ffn_br, L0_ffn_W1, L0_ffn_b1, L0_ffn_W2, L0_ffn_b2)
    return x

_drawn_inputs = setup_inputs


def setup_inputs(seed=0):
    import zlib

    import numpy as np

    out = dict(_drawn_inputs(seed))
    spreads = {'L0_attn_gamma': (1.0, 0.2),
     'L0_attn_beta': (0.0, 0.1),
     'L0_attn_bo': (0.0, 0.1),
     'L0_xattn_b_d2v': (0.0, 0.1),
     'L0_xattn_b_img': (0.0, 0.1),
     'L0_xattn_b_txt': (0.0, 0.1),
     'L0_xattn_b_att0': (0.0, 0.326),
     'L0_xattn_b_att1': (0.0, 0.285),
     'L0_xattn_b_f1': (0.0, 0.1),
     'L0_xattn_b_f2': (0.0, 0.1)}
    factors = {'L0_attn_u_bias': 2.737, 'L0_attn_v_bias': 3.316, 'L0_ffn_b1': 4.496, 'L0_ffn_b2': 3.506}
    for name, (base, spread) in spreads.items():
        noise = np.random.default_rng([zlib.crc32(name.encode()), seed]).standard_normal(out[name].shape)
        drawn = base * np.exp(spread * noise) if base else spread * noise
        out[name] = jnp.asarray(drawn.astype(out[name].dtype))
    for name, factor in factors.items():
        out[name] = (out[name] * factor).astype(out[name].dtype)
    return out
```

```python
from contextlib import ExitStack

import concourse.bass as bass
from concourse import mybir

F32 = mybir.dt.float32
BF16 = mybir.dt.bfloat16
U32 = mybir.dt.uint32
ALU = mybir.AluOpType
ACT = mybir.ActivationFunctionType
X = mybir.AxisListType.X

P = 128
B, L, D = 8, 256, 256
T = B * L
NT = T // P
DC = D // P
H, DH = 16, 16
MAXLEN = 1250
NR = 2 * L - 1
BANK = 512

IB = 32
NIB = L // IB
GAM = 4
HP = H // GAM
U = HP * B
WIN = L + IB - 1


class Mem:

    sems = None

    def __init__(self, nc):
        self.nc, self.stack = nc, ExitStack()

    def __enter__(self):
        self.stack.__enter__()
        return self

    def __exit__(self, *a):
        return self.stack.__exit__(*a)

    def sb(self, name, shape, dt=F32):
        return self.stack.enter_context(self.nc.sbuf_tensor(name, shape, dt))

    def sem(self, name):
        return Mem.sems.enter_context(self.nc.semaphore(name))


def bc(ap, *shape):
    return ap.to_broadcast(list(shape))


def project_phase(nc, ps, io, keep):
    qu, qv, kT, vt, rT, ident, mask8 = (keep[n] for n in ("qu", "qv", "kT", "vt", "rT", "ident", "mask8"))
    NTB = T // BANK
    with Mem(nc) as m:
        x = m.sb("x_a", [P, NT, D])
        z = m.sb("z_a", [P, NT, D])
        xnT = m.sb("xnT", [P, DC, T])
        w = {n: m.sb(f"w{n}", [P, DC, D]) for n in "qkvr"}
        rel = m.sb("rel", [P, 4, D])
        relT = m.sb("relT", [P, DC, BANK])
        gcol, bcol, ucol, vcol = (m.sb(n, [P, DC]) for n in ("gcol", "bcol", "ucol", "vcol"))
        ones8 = m.sb("ones8", [P, 8])
        st = m.sb("st", [P, NT, 6])
        mv = m.sb("mv", [P, NT, 2])
        ve = m.sb("ve", [P, NT])
        sd = m.sb("sd", [P, NT])
        rs = m.sb("rs", [P, NT])
        x_in = [m.sem(f"x_in{i}") for i in range(4)]
        rel_in, wr_in, vec_in, wqkv_in = m.sem("rel_in"), m.sem("wr_in"), m.sem("vec_in"), m.sem("wqkv_in")
        setup_step, consts_ready = m.sem("setup_step"), m.sem("consts_ready")
        norm_step, var_ready, std_ready = m.sem("norm_step"), m.sem("var_ready"), m.sem("std_ready")
        xn_ready, rel_T, rel_copied, r_done, r_kept = (m.sem(n) for n in ("xn_ready", "rel_T", "rel_copied", "r_done", "r_kept"))
        xT_done, xnT_ready, job_done = m.sem("xT_done"), m.sem("xnT_ready"), m.sem("job_done")
        kept_dve, kept_act = m.sem("kept_dve"), m.sem("kept_act")

        jobs = [(what, n) for n in range(NTB * DC) for what in "qkv"]
        by_dve = [sum(1 for w_, _ in jobs[:n + 1] if w_ == "q") for n in range(len(jobs))]
        by_act = [sum(1 for w_, _ in jobs[:n + 1] if w_ != "q") for n in range(len(jobs))]

        block = m.stack.enter_context(nc.Block())

        @block.sync
        def _(sp):
            xv = io["x"].rearrange("b s d -> (b s) d").rearrange("(t p) d -> p t d", p=P)
            for i in range(4):
                sp.dma_start(x[:, 4 * i:4 * i + 4], xv[:, 4 * i:4 * i + 4]).then_inc(x_in[i], 16)
            r0 = MAXLEN - (L - 1)
            rr = io["L0_attn_rel_pos_emb"]
            sp.dma_start(rel[:, 0:3], rr[r0:r0 + 3 * P].rearrange("(t p) d -> p t d", p=P)).then_inc(rel_in, 16)
            sp.dma_start(rel[0:P - 1, 3], rr[r0 + 3 * P:r0 + NR]).then_inc(rel_in, 16)
            sp.dma_start(w["r"][:], io["L0_attn_Wr"].rearrange("(c p) n -> p c n", p=P)).then_inc(wr_in, 16)
            for n in "qkv":
                sp.dma_start(w[n][:], io[f"L0_attn_W{n}"].rearrange("(c p) n -> p c n", p=P)).then_inc(wqkv_in, 16)

        @block.gpsimd
        def _(pool):
            with nc.allow_non_contiguous_dma(reason="four columns of 128 words"):
                pool.dma_start(gcol[:], io["L0_attn_gamma"].rearrange("(c p) -> p c", p=P)).then_inc(vec_in, 16)
                pool.dma_start(bcol[:], io["L0_attn_beta"].rearrange("(c p) -> p c", p=P)).then_inc(vec_in, 16)
                pool.dma_start(ucol[:], io["L0_attn_u_bias"].rearrange("h d -> (h d)").rearrange("(c p) -> p c", p=P)).then_inc(vec_in, 16)
                pool.dma_start(vcol[:], io["L0_attn_v_bias"].rearrange("h d -> (h d)").rearrange("(c p) -> p c", p=P)).then_inc(vec_in, 16)
            nc.gpsimd.memset(ident[:], 0.0).then_inc(setup_step, 1)
            nc.gpsimd.memset(ones8[:], 1.0).then_inc(setup_step, 1)
            pool.wait_ge(setup_step, 2)
            nc.gpsimd.affine_select(out=ident[:], in_=ident[:], compare_op=ALU.not_equal, fill=1.0, base=0,
                                    pattern=[[-1, P]], channel_multiplier=1).then_inc(consts_ready, 1)
            nc.gpsimd.affine_select(out=ones8[:], in_=ones8[:], compare_op=ALU.is_ge, fill=0.0, base=0,
                                    pattern=[[-DH, 8]], channel_multiplier=1).then_inc(setup_step, 1)
            pool.wait_ge(setup_step, 3)
            nc.gpsimd.affine_select(out=mask8[:], in_=ones8[:], compare_op=ALU.is_ge, fill=0.0, base=DH - 1,
                                    pattern=[[DH, 8]], channel_multiplier=-1).then_inc(consts_ready, 1)

        @block.vector
        def _(dve):
            def normalize(src, dst, eps, first, turn, steps):
                for t in range(NT):
                    if first and t % 4 == 0:
                        dve.wait_ge(x_in[t // 4], 16)
                    i = nc.vector.bn_stats(st[:, t], src[:, t])
                i.then_inc(norm_step, 1)
                dve.wait_ge(norm_step, steps + 1)
                for t in range(NT):
                    i = nc.vector.bn_aggr(mv[:, t], st[:, t])
                i.then_inc(norm_step, 1)
                dve.wait_ge(norm_step, steps + 2)
                nc.vector.tensor_scalar_add(ve[:], mv[:, :, 1], eps).then_inc(var_ready, 1)
                dve.wait_ge(std_ready, turn)
                nc.vector.reciprocal(rs[:], sd[:]).then_inc(norm_step, 1)
                dve.wait_ge(norm_step, steps + 3)
                for t in range(NT):
                    i = nc.vector.tensor_scalar(dst[:, t], src[:, t], mv[:, t, 0:1], rs[:, t:t + 1], ALU.subtract, ALU.mult)
                    if not first:
                        i.then_inc(xn_ready, 1)
                if first:
                    i.then_inc(norm_step, 1)
                    dve.wait_ge(norm_step, steps + 4)

            normalize(x, z, 1e-5, True, 1, 0)
            normalize(z, x, 1e-6, False, 2, 4)
            for n, (what, i) in enumerate(jobs):
                if what != "q":
                    continue
                if n == 0:
                    dve.wait_ge(vec_in, 64)
                dve.wait_ge(job_done, n + 1)
                bank = ps[n % 4]
                tb, hg = divmod(i, DC)
                cols = slice(tb * BANK, (tb + 1) * BANK)
                nc.vector.tensor_scalar_add(qu[:, hg, cols], bank[:], ucol[:, hg:hg + 1])
                nc.vector.tensor_scalar_add(qv[:, hg, cols], bank[:], vcol[:, hg:hg + 1]).then_inc(kept_dve, 1)

        @block.scalar
        def _(act):
            for c in range(DC):
                act.wait_ge(rel_T, c + 1)
                nc.scalar.activation(relT[:, c, 0:NR], ps[c][:, 0:NR], ACT.Copy).then_inc(rel_copied, 1)
            for hg in range(DC):
                act.wait_ge(r_done, hg + 1)
                nc.scalar.activation(rT[:, hg, 0:NR], ps[2 + hg][:, 0:NR], ACT.Copy).then_inc(r_kept, 1)
            for turn in range(2):
                act.wait_ge(var_ready, turn + 1)
                nc.scalar.activation(sd[:], ve[:], ACT.Sqrt).then_inc(std_ready, 1)
            act.wait_ge(vec_in, 64)
            for n in range(NTB * DC):
                tb, c = divmod(n, DC)
                act.wait_ge(xT_done, n + 1)
                nc.scalar.activation(xnT[:, c, tb * BANK:(tb + 1) * BANK], ps[4 + n % 4][:], ACT.Identity,
                                     bias=bcol[:, c:c + 1], scale=gcol[:, c:c + 1]).then_inc(xnT_ready, 1)
            for n, (what, i) in enumerate(jobs):
                if what == "q":
                    continue
                act.wait_ge(job_done, n + 1)
                bank = ps[n % 4]
                if what == "v":
                    nc.scalar.activation(vt[:, 2 * i:2 * i + 2], bank[:].rearrange("p (t d) -> p t d", t=2), ACT.Copy).then_inc(kept_act, 1)
                else:
                    tb, hg = divmod(i, DC)
                    nc.scalar.activation(kT[:, hg, tb * BANK:(tb + 1) * BANK], bank[:], ACT.Copy).then_inc(kept_act, 1)

        @block.tensor
        def _(pe):
            pe.wait_ge(consts_ready, 2)
            pe.wait_ge(rel_in, 32)
            for c in range(DC):
                for t in range(4):
                    n = P if t < 3 else P - 1
                    i = nc.tensor.transpose(ps[c][:, t * P:t * P + n], rel[0:n, t, c * P:(c + 1) * P], ident[0:n, 0:n])
                i.then_inc(rel_T, 1)
            pe.wait_ge(rel_copied, DC)
            pe.wait_ge(wr_in, 16)
            for hg in range(DC):
                for c in range(DC):
                    i = nc.tensor.matmul(ps[2 + hg][:, 0:NR], w["r"][:, c, hg * P:(hg + 1) * P], relT[:, c, 0:NR],
                                         start=c == 0, stop=c == DC - 1)
                i.then_inc(r_done, 1)
            for n in range(NTB * DC):
                tb, c = divmod(n, DC)
                if n >= 4:
                    pe.wait_ge(xnT_ready, n - 3)
                for t in range(4):
                    if c == 0:
                        pe.wait_ge(xn_ready, 4 * tb + t + 1)
                    i = nc.tensor.transpose(ps[4 + n % 4][:, t * P:(t + 1) * P], x[:, 4 * tb + t, c * P:(c + 1) * P], ident[:])
                i.then_inc(xT_done, 1)
            pe.wait_ge(wqkv_in, 48)
            pe.wait_ge(r_kept, DC)
            for n, (what, i) in enumerate(jobs):
                if n >= 4:
                    pe.wait_ge(kept_dve, by_dve[n - 4])
                    pe.wait_ge(kept_act, by_act[n - 4])
                pe.wait_ge(xnT_ready, DC * (i // 2 + 1))
                bank = ps[n % 4]
                if what == "v":
                    for t in range(2):
                        for c in range(DC):
                            tile = 2 * i + t
                            j = nc.tensor.matmul(bank[:, t * D:(t + 1) * D], xnT[:, c, tile * P:(tile + 1) * P], w["v"][:, c],
                                                 start=c == 0, stop=c == DC - 1)
                else:
                    tb, hg = divmod(i, DC)
                    for c in range(DC):
                        j = nc.tensor.matmul(bank[:], w[what][:, c, hg * P:(hg + 1) * P], xnT[:, c, tb * BANK:(tb + 1) * BANK],
                                             start=c == 0, stop=c == DC - 1)
                j.then_inc(job_done, 1)


def attention_phase(nc, ps, io, keep):
    qu, qv, kT, vt, rT, ident, mask8, aT = (keep[n] for n in ("qu", "qv", "kT", "vt", "rT", "ident", "mask8", "aT"))
    LEAD = 12
    CH = 4
    RING = 4
    ROW = CH * WIN + IB
    LT, LV, LO = 3, 6, 12
    pos = nc.dram_tensor("position_scores", [RING, P * ROW], F32).ap()
    with Mem(nc) as m:
        bds = m.sb("bds", [P, RING, CH, L])
        bdp = m.sb("bdp", [P, RING, CH * WIN])
        qa = m.sb("qa", [P, HP, 2, B, 2, IB])
        qb = m.sb("qb", [P, HP, 2, B, 2, IB])
        rwin = m.sb("rwin", [P, 2, 2, WIN])
        sc = m.sb("sc", [P, 4, L])
        pr = m.sb("pr", [P, 8, L])
        prT = m.sb("prT", [P, 4, BANK])
        nmax = m.sb("nmax", [P, U])
        rsum = m.sb("rsum", [P, U])
        rinv = m.sb("rinv", [P, U])
        osb = m.sb("osb", [P, B, HP, DH])
        ac_banks, bd_banks, pt_banks, o_banks = ps[0:2], ps[2:4], ps[4:6], ps[6:8]

        qa_ready, qb_ready, rwin_ready = m.sem("qa_ready"), m.sem("qb_ready"), m.sem("rwin_ready")
        ac_done, s_done, exp_done = m.sem("ac_done"), m.sem("s_done"), m.sem("exp_done")
        bd_done, bd_kept = m.sem("bd_done"), m.sem("bd_kept")
        pos_out = [m.sem(f"pos_out{i}") for i in range(RING)]
        pos_in = [m.sem(f"pos_in{i}") for i in range(RING)]
        pt_done, pt_kept, pv_done = m.sem("pt_done"), m.sem("pt_kept"), m.sem("pv_done")
        rinv_step, o_kept, ot_done, ot_kept = m.sem("rinv_step"), m.sem("o_kept"), m.sem("ot_done"), m.sem("ot_kept")

        NC = U // CH
        TURNS = NC // RING

        def place(ib, s, shift):
            s += shift
            ib, s = (ib - 1, s + U) if s < 0 else (ib + 1, s - U) if s >= U else (ib, s)
            return None if isinstance(ib, int) and not 0 <= ib < NIB else (ib, s)

        def past(ib, n):
            return not isinstance(ib, int) or ib >= n

        def run_turns(eng, step):
            for s in range(U):
                step(0, s, 0)
            with eng.Fori(0, NIB // 2 - 1) as pair:
                for odd in (1, 0):
                    for s in range(U):
                        step(2 * pair + 2 - odd, s, odd)
            for s in range(U):
                step(NIB - 1, s, 1)
            for s in range(LO):
                step(NIB, s, None)

        block = m.stack.enter_context(nc.Block())

        @block.sync
        def _(sp):
            def shift_chunk(ib, c):
                slot, turn = c % RING, TURNS * ib + c // RING
                sp.wait_ge(bd_kept, U * ib + CH * (c + 1))
                sp.nop(nofuse=True)
                if c >= RING or past(ib, 1):
                    sp.wait_ge(pos_in[slot], 16 * turn)
                    sp.nop(nofuse=True)
                sp.dma_start(bass.AP(pos.tensor, slot * P * ROW, [[IB * (ROW - 1), GAM], [ROW, IB], [1, CH * WIN]]),
                             bdp[:, slot]).then_inc(pos_out[slot], 16)
                sp.wait_ge(pos_out[slot], 16 * turn + 16)
                sp.nop(nofuse=True)
                if c >= RING or past(ib, 1):
                    sp.wait_ge(s_done, U * ib + CH * (c + 1 - RING))
                    sp.nop(nofuse=True)
                sp.dma_start(bds[:, slot], bass.AP(pos.tensor, slot * P * ROW + IB - 1, [[ROW - 1, P], [WIN, CH], [1, L]])
                             ).then_inc(pos_in[slot], 16)

            for c in range(NC):
                shift_chunk(0, c)
            with sp.Fori(1, NIB) as ib:
                for c in range(NC):
                    shift_chunk(ib, c)

        @block.gpsimd
        def _(pool):
            def operands(ib, odd):
                if past(ib, 2):
                    pool.wait_ge(bd_done, U * (ib - 1))
                    pool.nop(nofuse=True)
                nc.gpsimd.tensor_copy(rwin[:, odd], rT[:, :, bass.ds(L - IB - IB * ib, WIN)]).then_inc(rwin_ready, 1)
                for hp in range(HP):
                    for dst, src, used, ready in ((qb, qv, bd_done, qb_ready), (qa, qu, ac_done, qa_ready)):
                        if past(ib, 1):
                            pool.wait_ge(used, U * (ib - 1) + (hp + 1) * B)
                            pool.nop(nofuse=True)
                        for hg in range(2):
                            q = src[:, hg].rearrange("p (b i) -> p b i", b=B)[:, :, bass.ds(IB * ib, IB)].unsqueeze(2)
                            k = mask8[:, hp:2 * HP:HP].unsqueeze(1).unsqueeze(3)
                            nc.gpsimd.tensor_tensor(out=dst[:, hp, hg], in0=bc(q, P, B, 2, IB), in1=bc(k, P, B, 2, IB),
                                                    op=ALU.mult).then_inc(ready, 1)

            operands(0, 0)
            operands(1, 1)
            with pool.Fori(1, NIB // 2) as pair:
                operands(2 * pair, 0)
                operands(2 * pair + 1, 1)

        @block.vector
        def _(dve):
            def step(ib, s, odd):
                if odd is not None:
                    c = s // CH
                    if s % CH == 0:
                        dve.wait_ge(pos_in[c % RING], 16 * (TURNS * ib + c // RING + 1))
                    dve.wait_ge(ac_done, U * ib + s + 1)
                    if s >= 4 or past(ib, 1):
                        dve.wait_ge(exp_done, U * ib + s - 3)
                    dve.nop(nofuse=True)
                    nc.vector.tensor_tensor_reduce(
                        out=sc[:, s % 4], in0=ac_banks[s % 2][:, 0:L], in1=bds[:, c % RING, s % CH],
                        scale=-1.0 / DH ** 0.5, scalar=3.0e38, op0=ALU.add, op1=ALU.min,
                        accum_out=nmax[:, s:s + 1]).then_inc(s_done, 1)
                t = place(ib, s, -LT)
                if t and t[1] % 2:
                    tb, pair = t[0], t[1] // 2
                    dve.wait_ge(pt_done, U // 2 * tb + pair + 1)
                    if pair >= 4 or past(tb, 1):
                        dve.wait_ge(pv_done, U // 2 * tb + pair - 3)
                    nc.vector.tensor_copy(prT[:, pair % 4], pt_banks[pair % 2][:]).then_inc(pt_kept, 1)
                t = place(ib, s, -LV - 1)
                if t and t[1] % B == B - 1:
                    tb, hp = t[0], t[1] // B
                    part = slice(hp * B, (hp + 1) * B)
                    dve.wait_ge(exp_done, U * tb + t[1] + 1)
                    nc.vector.reciprocal(rinv[:, part], rsum[:, part]).then_inc(rinv_step, 1)
                    dve.wait_ge(rinv_step, HP * tb + hp + 1)
                    dve.wait_ge(pv_done, U // 2 * tb + (t[1] + 1) // 2)
                    if hp == 0 and past(tb, 1):
                        dve.wait_ge(ot_done, tb)
                    bank = o_banks[hp % 2][:].rearrange("p (b g d) -> p b g d", b=B, g=GAM)
                    for g in range(GAM):
                        rows = slice(g * IB, (g + 1) * IB)
                        i = nc.vector.tensor_tensor(out=osb[rows, :, hp], in0=bank[rows, :, g],
                                                    in1=bc(rinv[rows, part].unsqueeze(2), IB, B, DH), op=ALU.mult)
                    i.then_inc(o_kept, 1)

            run_turns(dve, step)

        @block.scalar
        def _(act):
            def keep_positions(ib, s):
                c = s // CH
                act.wait_ge(bd_done, U * ib + s + 1)
                if s % CH == 0 and (c >= RING or past(ib, 1)):
                    act.wait_ge(pos_out[c % RING], 16 * (TURNS * ib + c // RING))
                nc.scalar.activation(bdp[:, c % RING, s % CH * WIN:(s % CH + 1) * WIN], bd_banks[s % 2][:, 0:WIN], ACT.Copy).then_inc(bd_kept, 1)

            def step(ib, s, odd):
                if odd is not None:
                    act.wait_ge(s_done, U * ib + s + 1)
                    if s % 2 == 0 and (s >= 8 or past(ib, 1)):
                        act.wait_ge(pt_done, U // 2 * ib + s // 2 - 3)
                    nc.scalar.activation(pr[:, s % 8], sc[:, s % 4], ACT.Exp, bias=nmax[:, s:s + 1], scale=-1.0,
                                         accum_out=rsum[:, s:s + 1]).then_inc(exp_done, 1)
                    if place(ib, s, LEAD):
                        keep_positions(*place(ib, s, LEAD))
                if s == LO - 1 and past(ib, 1):
                    act.wait_ge(ot_done, ib)
                    nc.scalar.activation(aT[:, :, :, bass.ds(IB * ib - IB, IB)], o_banks[1][:].rearrange("p (a g i) -> p a g i", a=B // 2, g=GAM),
                                         ACT.Copy).then_inc(ot_kept, 1)

            for s in range(LEAD):
                keep_positions(0, s)
            run_turns(act, step)

        @block.tensor
        def _(pe):
            def position_scores(ib, s, odd):
                hp, b = divmod(s, B)
                if b == 0:
                    pe.wait_ge(qb_ready, 2 * (HP * ib + hp) + 2)
                    if hp == 0:
                        pe.wait_ge(rwin_ready, ib + 1)
                if s >= 2 or past(ib, 1):
                    pe.wait_ge(bd_kept, U * ib + s - 1)
                for hg in range(2):
                    i = nc.tensor.matmul(bd_banks[s % 2][64 * hg:64 * hg + 64, 0:WIN], qb[:, hp, hg, b].rearrange("p g i -> p (g i)"),
                                         rwin[:, odd, hg], start=True, stop=True)
                i.then_inc(bd_done, 1)

            def content_scores(ib, s):
                hp, b = divmod(s, B)
                if b == 0:
                    pe.wait_ge(qa_ready, 2 * (HP * ib + hp) + 2)
                if s >= 2 or past(ib, 1):
                    pe.wait_ge(s_done, U * ib + s - 1)
                for hg in range(2):
                    i = nc.tensor.matmul(ac_banks[s % 2][64 * hg:64 * hg + 64, 0:L], qa[:, hp, hg, b].rearrange("p g i -> p (g i)"),
                                         kT[:, hg, b * L:(b + 1) * L], start=True, stop=True)
                i.then_inc(ac_done, 1)

            def transposes(ib, s):
                pe.wait_ge(exp_done, U * ib + s + 1)
                if s % 2 == 0 and (s >= 4 or past(ib, 1)):
                    pe.wait_ge(pt_kept, U // 2 * ib + s // 2 - 1)
                for jc in range(2):
                    i = nc.tensor.transpose(pt_banks[s // 2 % 2][:, s % 2 * L + jc * P:s % 2 * L + (jc + 1) * P],
                                            pr[:, s % 8, jc * P:(jc + 1) * P], ident[:])
                if s % 2:
                    i.then_inc(pt_done, 1)

            def values(ib, s):
                hp, b = divmod(s, B)
                if s % 2 == 0:
                    pe.wait_ge(pt_kept, U // 2 * ib + s // 2 + 1)
                if b == 0 and (hp >= 2 or past(ib, 1)):
                    if hp == 1:
                        pe.wait_ge(ot_kept, ib)
                    else:
                        pe.wait_ge(o_kept, HP * ib + hp - 1)
                for jc in range(2):
                    v = vt[:, 2 * b + jc].rearrange("p (g h d) -> p g h d", g=GAM, h=HP)[:, :, hp]
                    i = nc.tensor.matmul(o_banks[hp % 2][:, b * 64:(b + 1) * 64],
                                         prT[:, s // 2 % 4, s % 2 * L + jc * P:s % 2 * L + (jc + 1) * P], v,
                                         start=jc == 0, stop=jc == 1)
                if s % 2:
                    i.then_inc(pv_done, 1)

            def step(ib, s, odd):
                if odd is not None:
                    content_scores(ib, s)
                    if place(ib, s, LEAD):
                        position_scores(*place(ib, s, LEAD), odd ^ (s + LEAD >= U))
                if place(ib, s, -LT):
                    transposes(*place(ib, s, -LT))
                if place(ib, s, -LV):
                    values(*place(ib, s, -LV))
                if s == LO - 1 and past(ib, 1):
                    pe.wait_ge(o_kept, HP * ib)
                    for a in range(B // 2):
                        i = nc.tensor.transpose(o_banks[1][:, a * P:(a + 1) * P], osb[:, 2 * a:2 * a + 2].rearrange("p b h d -> p (b h d)"), ident[:])
                    i.then_inc(ot_done, 1)

            for s in range(LEAD):
                position_scores(0, s, 0)
            run_turns(pe, step)


MAGIC = 12582912.0
XW = ("d2v", "img", "txt", "att0", "att1", "f1", "f2")
XSHAPE = {"d2v": (256, 192), "img": (256, 256), "txt": (256, 256), "att0": (128, 256), "att1": (128, 256),
          "f1": (1024, 512), "f2": (256, 1024)}
RMAX = bass.bass_isa.ReduceOp.max
RADD = bass.bass_isa.ReduceOp.add


def chunks(n):
    return [(i, min(P, n - i)) for i in range(0, n, P)]


class Chain:

    def __init__(self, eng, sem):
        self.eng, self.sem, self.n = eng, sem, 0

    def __call__(self, ins):
        self.n += 1
        ins.then_inc(self.sem, 1)
        self.eng.wait_ge(self.sem, self.n)


def activation_scale(nc, link, am, isc, inv):
    link(nc.vector.tensor_scalar(isc, am, 1e-8, 1.0 / 127.0, ALU.max, ALU.mult))
    link(nc.vector.reciprocal(inv, isc))


def context_phase(nc, ps, io, keep):
    ident, qwT, ws, bias = keep["ident"], keep["qwT"], keep["ws"], keep["bias"]
    kvT, kvt, avg = keep["kvT"], keep["kvt"], keep["avg"]
    aT, x1 = keep["aT"], keep["x1"]
    NB = 4
    CW = 192
    NTB = T // BANK
    with Mem(nc) as m:
        wo = m.sb("wo", [P, GAM, D])
        bo = m.sb("bo", [P, D])
        wo_in, x_in, bo_in = m.sem("wo_in"), m.sem("x1_in"), m.sem("bo_in")
        y_done, xb_done, x1_done = m.sem("y_done"), m.sem("xb_done"), m.sem("x1_done")
        raw = {n: m.sb(f"raw_{n}", [P, XSHAPE[n][0] // P, XSHAPE[n][1]]) for n in XW}
        junk = m.sb("junk", [P, 8 * BANK], BF16)
        qn = {n: m.sb(f"qn_{n}", [P, XSHAPE[n][0] // P, XSHAPE[n][1]], BF16) for n in XW}
        identb = m.sb("identb", [P, P], BF16)
        cx = m.sb("cx", [P, NT, CW])
        cq = m.sb("cq", [P, NT, CW], BF16)
        cqT = m.sb("cqT", [P, 2, T], BF16)
        act_f = {"vis": m.sb("vis", [P, DC, T]), "img": m.sb("img", [P, DC, T])}
        act_q = m.sb("act_q", [P, DC, T], BF16)
        sums, cnt, thr, nthr = (m.sb(n, [P, len(XW)]) for n in ("sums", "cnt", "thr", "nthr"))
        part = m.sb("part", [P, 8])
        loc, am, isc, inv = (m.sb(n, [P, 3]) for n in ("loc", "am", "isc", "inv"))
        sc = m.sb("sc_d", [P, 4])
        small_in = m.sem("w_in_small")
        w_in = {n: small_in if n in ("img", "txt", "att0", "att1") else m.sem(f"w_in_{n}") for n in XW}
        cx_in, bias_in = m.sem("cx_in"), m.sem("bias_in")
        dve_step, pool_step, cnt_ready, abs_summed, sums_ready, idb_ready = (
            m.sem(n) for n in ("dve_step", "pool_step", "cnt_ready", "abs_summed", "sums_ready", "idb_ready"))
        w_quant, loc_ready, am_ready, scale_ready = (m.sem(n) for n in ("w_quant", "loc_ready", "am_ready", "scale_ready"))
        c_quant, a_quant = m.sem("c_quant"), {n: m.sem(f"quant_{n}") for n in ("vis", "img")}
        bank_done, bank_kept = m.sem("bank_done"), m.sem("bank_kept")

        WB = {"d2v": 1, "img": 1, "txt": 1, "att0": 1, "att1": 1, "f1": 4, "f2": 2}
        J = {}
        n = 0
        J["d2v"] = n; n += 1
        J["ctx"] = n; n += 4
        J["vis"] = n; n += 8
        J["img"] = n; n += 1
        J["image"] = n; n += 8
        for w in ("att0", "att1"):
            J[w] = n; n += 1
        J["kv"] = n; n += 8
        J["kvt"] = n; n += 8
        for w in ("txt", "f1", "f2"):
            J[w] = n; n += WB[w]
        NJ = n
        block = m.stack.enter_context(nc.Block())

        @block.sync
        def _(sp):
            for half in range(2):
                sp.dma_start(wo[64 * half:64 * half + 64], io["L0_attn_Wo"].rearrange("(g q) n -> q g n", g=GAM)).then_inc(wo_in, 16)
            sp.dma_start(x1[:], io["x"].rearrange("b s d -> (b s) d").rearrange("(t p) d -> p t d", p=P)).then_inc(x_in, 16)
            sp.dma_start(bo[:], bc(io["L0_attn_bo"].unsqueeze(0), P, D)).then_inc(bo_in, 16)
            for w in XW:
                if w == "img":
                    sp.dma_start(cx[:], io["ctx_768"].rearrange("b s d -> (b s) d").rearrange("(t p) d -> p t d", p=P)).then_inc(cx_in, 16)
                sp.dma_start(raw[w][:], io[f"L0_xattn_W_{w}"].rearrange("(c p) n -> p c n", p=P)).then_inc(w_in[w], 16)

        @block.gpsimd
        def _(pool):
            with nc.allow_non_contiguous_dma(reason="bias columns"):
                for w in XW:
                    pool.dma_start(bias[w][:], io[f"L0_xattn_b_{w}"].rearrange("(c p) -> p c", p=P)).then_inc(bias_in, 16)
            nc.gpsimd.tensor_copy(identb[:], ident[:]).then_inc(idb_ready, 1)
            for k, w in enumerate(XW):
                i = nc.gpsimd.memset(cnt[:, k:k + 1], 1.0 / (XSHAPE[w][0] * XSHAPE[w][1]))
            i.then_inc(cnt_ready, 1)
            pool.wait_ge(x_in, 16)
            pool.wait_ge(bo_in, 16)
            for t in range(0, NT, 2):
                nc.gpsimd.tensor_tensor(out=x1[:, t:t + 2], in0=x1[:, t:t + 2], in1=bc(bo[:].unsqueeze(1), P, 2, D), op=ALU.add).then_inc(xb_done, 1)
            pool.wait_ge(abs_summed, len(XW))
            nc.gpsimd.partition_all_reduce(thr[:], sums[:], P, RADD).then_inc(sums_ready, 1)
            for a in range(3):
                pool.wait_ge(loc_ready, a + 1)
                nc.gpsimd.partition_all_reduce(am[:, a:a + 1], loc[:, a:a + 1], P, RMAX).then_inc(am_ready, 1)
            pool.wait_ge(bias_in, 16 * len(XW))

        @block.vector
        def _(dve):
            link = Chain(dve, dve_step)

            def keep_rows(pairs):
                for k in pairs:
                    dve.wait_ge(xb_done, k + 1)
                    dve.wait_ge(y_done, k + 1)
                    nc.vector.tensor_tensor(out=x1[:, 2 * k:2 * k + 2], in0=ps[NB + k % 4][:].rearrange("p (t d) -> p t d", t=2),
                                            in1=x1[:, 2 * k:2 * k + 2], op=ALU.add).then_inc(x1_done, 1)

            dve.wait_ge(cx_in, 16)
            nc.vector.tensor_reduce(loc[:, 0:1], cx[:].rearrange("p t d -> p (t d)"), X, ALU.max, apply_absolute_value=True).then_inc(loc_ready, 1)
            keep_rows((0, 1, 2))
            dve.wait_ge(sums_ready, 1)
            dve.wait_ge(cnt_ready, 1)
            link(nc.vector.tensor_tensor(out=ws[:], in0=thr[:], in1=cnt[:], op=ALU.mult))
            link(nc.vector.tensor_scalar_max(ws[:], ws[:], 1e-5))
            link(nc.vector.tensor_scalar_mul(thr[:], ws[:], 0.5))
            link(nc.vector.tensor_scalar_mul(nthr[:], ws[:], -0.5))

            def ternary(w):
                k = XW.index(w)
                link(nc.vector.tensor_scalar(qn[w][:], raw[w][:], nthr[:, k:k + 1], None, ALU.is_lt))
                nc.vector.scalar_tensor_tensor(out=qn[w][:], in0=raw[w][:], scalar=thr[:, k:k + 1], in1=qn[w][:],
                                               op0=ALU.is_gt, op1=ALU.subtract).then_inc(w_quant, 1)

            ternary("d2v")
            keep_rows((3,))
            dve.wait_ge(am_ready, 1)
            activation_scale(nc, link, am[:, 0:1], isc[:, 0:1], inv[:, 0:1])
            nc.vector.tensor_tensor(out=sc[:, 0:1], in0=isc[:, 0:1], in1=ws[:, 0:1], op=ALU.mult).then_inc(scale_ready, 1)
            for g in range(2):
                tiles = slice(8 * g, 8 * g + 8)
                link(nc.vector.tensor_scalar(cx[:, tiles], cx[:, tiles], inv[:, 0:1], MAGIC, ALU.mult, ALU.add))
                nc.vector.tensor_scalar(cq[:, tiles], cx[:, tiles], MAGIC, None, ALU.subtract).then_inc(c_quant, 1)
            ternary("img")
            keep_rows((4,))

            def measure(a, name, j0):
                for tb in range(NTB):
                    for oc in range(DC):
                        dve.wait_ge(bank_kept, J[j0] + tb * DC + oc + 1)
                        i = nc.vector.tensor_reduce(part[:, tb * DC + oc:tb * DC + oc + 1], act_f[name][:, oc, tb * BANK:(tb + 1) * BANK],
                                                    X, ALU.max, apply_absolute_value=True)
                link(i)
                nc.vector.tensor_reduce(loc[:, a:a + 1], part[:], X, ALU.max).then_inc(loc_ready, 1)

            def quantize(a, name):
                src = act_f[name]
                for tb in range(NTB):
                    cols = slice(tb * BANK, (tb + 1) * BANK)
                    link(nc.vector.tensor_scalar(src[:, :, cols], src[:, :, cols], inv[:, a:a + 1], MAGIC, ALU.mult, ALU.add))
                    nc.vector.tensor_scalar(act_q[:, :, cols], src[:, :, cols], MAGIC, None, ALU.subtract).then_inc(a_quant[name], 1)

            measure(1, "vis", "vis")
            ternary("att0")
            ternary("att1")
            keep_rows((5,))
            dve.wait_ge(am_ready, 2)
            activation_scale(nc, link, am[:, 1:2], isc[:, 1:2], inv[:, 1:2])
            nc.vector.tensor_tensor(out=sc[:, 1:2], in0=isc[:, 1:2], in1=ws[:, 1:2], op=ALU.mult).then_inc(scale_ready, 1)
            quantize(1, "vis")
            keep_rows((6,))
            measure(2, "img", "image")
            link(nc.vector.reduce_sum(avg[:], act_f["img"][:].rearrange("p c (b s) -> p c b s", b=B), X))
            nc.vector.tensor_scalar_mul(avg[:], avg[:], 1.0 / L)
            keep_rows((7,))
            dve.wait_ge(am_ready, 3)
            activation_scale(nc, link, am[:, 2:3], isc[:, 2:3], inv[:, 2:3])
            nc.vector.tensor_scalar(sc[:, 2:4], ws[:, 3:5], isc[:, 2:3], None, ALU.mult).then_inc(scale_ready, 1)
            dve.wait_ge(bank_kept, J["image"] + 8)
            dve.wait_ge(bank_done, J["image"] + 8)
            quantize(2, "img")
            ternary("txt")
            ternary("f1")
            ternary("f2")

        def keep_weight(w):
            rows, cols = XSHAPE[w]
            blocks = [(ic, oc) for ic in range(len(chunks(cols))) for oc in range(rows // P)]
            per = -(-len(blocks) // WB[w])
            return [blocks[i:i + per] for i in range(0, len(blocks), per)]

        @block.scalar
        def _(act):
            for k, w in enumerate(XW):
                act.wait_ge(w_in[w], 64 if w_in[w] is small_in else 16)
                n = XSHAPE[w][0] // P * XSHAPE[w][1]
                if k:
                    act.wait_ge(abs_summed, k)
                nc.scalar.activation(junk[:, 0:n], raw[w][:].rearrange("p c n -> p (c n)"), ACT.Abs,
                                     accum_out=sums[:, k:k + 1]).then_inc(abs_summed, 1)
            act.wait_ge(bias_in, 16 * len(XW))

            def weight(w):
                for q, blocks in enumerate(keep_weight(w)):
                    j = J[w] + q
                    act.wait_ge(bank_done, j + 1)
                    (i0, o0) = blocks[0]
                    bank = ps[j % NB][:].bitcast(BF16)
                    rows = min(c[1] for c in chunks(XSHAPE[w][1]))
                    if rows == P:
                        o = qwT[w][:].rearrange("p i n -> p (i n)")
                        s = (i0 * (XSHAPE[w][0] // P) + o0) * P
                        nc.scalar.activation(o[:, s:s + len(blocks) * P], bank[:, 0:len(blocks) * P], ACT.Copy).then_inc(bank_kept, 1)
                    else:
                        half = len(blocks) // 2 * P
                        nc.scalar.activation(qwT[w][:, 0], bank[:, 0:half], ACT.Copy)
                        nc.scalar.activation(qwT[w][0:rows, 1], bank[0:rows, half:2 * half], ACT.Copy).then_inc(bank_kept, 1)

            weight("d2v")
            for c, (c0, cn) in enumerate(chunks(CW)):
                for g in range(2):
                    j = J["ctx"] + 2 * c + g
                    act.wait_ge(bank_done, j + 1)
                    nc.scalar.activation(cqT[0:cn, c, g * 1024:(g + 1) * 1024], ps[j % NB][0:cn, :].bitcast(BF16), ACT.Copy).then_inc(bank_kept, 1)

            def linear(j0, a, out, w):
                act.wait_ge(scale_ready, a + 1)
                for tb in range(NTB):
                    for oc in range(DC):
                        j = J[j0] + tb * DC + oc
                        act.wait_ge(bank_done, j + 1)
                        nc.scalar.activation(out[:, oc, tb * BANK:(tb + 1) * BANK], ps[j % NB][:], ACT.Identity,
                                             scale=sc[:, a:a + 1], bias=bias[w][:, oc:oc + 1]).then_inc(bank_kept, 1)

            linear("vis", 0, act_f["vis"], "d2v")
            weight("img")
            linear("image", 1, act_f["img"], "img")
            weight("att0")
            weight("att1")
            act.wait_ge(scale_ready, 3)
            for tb in range(NTB):
                for a in range(2):
                    j = J["kv"] + 2 * tb + a
                    act.wait_ge(bank_done, j + 1)
                    nc.scalar.activation(kvT[:, a, tb * BANK:(tb + 1) * BANK], ps[j % NB][:], ACT.Identity,
                                         scale=sc[:, 2 + a:3 + a], bias=bias[f"att{a}"][:, 0:1]).then_inc(bank_kept, 1)
            for tb in range(NTB):
                for a in range(2):
                    j = J["kvt"] + 2 * tb + a
                    act.wait_ge(bank_done, j + 1)
                    nc.scalar.activation(kvt[:, a, 4 * tb:4 * tb + 4], ps[j % NB][:].rearrange("p (t o) -> p t o", t=4), ACT.Copy).then_inc(bank_kept, 1)
            for w in ("txt", "f1", "f2"):
                weight(w)

        @block.tensor
        def _(pe):
            def bank(j):
                if j >= NB:
                    pe.wait_ge(bank_kept, j - NB + 1)
                return ps[j % NB]

            def weight(w, order):
                pe.wait_ge(w_quant, order)
                for q, blocks in enumerate(keep_weight(w)):
                    out = bank(J[w] + q)[:].bitcast(BF16)
                    for k, (ic, oc) in enumerate(blocks):
                        c0, cn = chunks(XSHAPE[w][1])[ic]
                        i = nc.tensor.transpose(out[0:cn, k * P:(k + 1) * P], qn[w][:, oc, c0:c0 + cn], identb[:])
                    i.then_inc(bank_done, 1)

            def project(pairs):
                for k in pairs:
                    if k >= 4:
                        pe.wait_ge(x1_done, k - 3)
                    rows = slice(64 * (k % 2), 64 * (k % 2) + 64)
                    for ic in range(2):
                        for g in range(GAM):
                            i = nc.tensor.matmul(ps[NB + k % 4][:, ic * D:(ic + 1) * D], aT[rows, k // 2, g, ic * P:(ic + 1) * P],
                                                 wo[rows, g], start=g == 0, stop=g == GAM - 1)
                    i.then_inc(y_done, 1)

            pe.wait_ge(wo_in, 32)
            project((0, 1, 2, 3))
            pe.wait_ge(idb_ready, 1)
            weight("d2v", 1)
            for c, (c0, cn) in enumerate(chunks(CW)):
                for g in range(2):
                    pe.wait_ge(c_quant, g + 1)
                    out = bank(J["ctx"] + 2 * c + g)[:].bitcast(BF16)
                    for t in range(8):
                        i = nc.tensor.transpose(out[0:cn, t * P:(t + 1) * P], cq[:, 8 * g + t, c0:c0 + cn], identb[:])
                    i.then_inc(bank_done, 1)
            pe.wait_ge(bank_kept, J["ctx"] + 4)

            def linear(j0, w, src, widths, ready):
                for tb in range(NTB):
                    if ready is not None:
                        pe.wait_ge(ready, tb + 1)
                    for oc in range(XSHAPE[w][0] // P):
                        o = bank(J[j0] + tb * DC + oc)
                        for c, (c0, cn) in enumerate(widths):
                            i = nc.tensor.matmul(o[:], qwT[w][0:cn, c, oc * P:(oc + 1) * P], src[0:cn, c, tb * BANK:(tb + 1) * BANK],
                                                 start=c == 0, stop=c == len(widths) - 1)
                        i.then_inc(bank_done, 1)

            project((4,))
            linear("vis", "d2v", cqT, chunks(CW), None)
            weight("img", 2)
            pe.wait_ge(bank_kept, J["img"] + 1)
            project((5, 6))
            linear("image", "img", act_q, chunks(D), a_quant["vis"])
            weight("att0", 3)
            weight("att1", 4)
            project((7,))
            pe.wait_ge(bank_kept, J["att1"] + 1)
            for tb in range(NTB):
                pe.wait_ge(a_quant["img"], tb + 1)
                for a in range(2):
                    o = bank(J["kv"] + 2 * tb + a)
                    for c in range(DC):
                        i = nc.tensor.matmul(o[:], qwT[f"att{a}"][:, c], act_q[:, c, tb * BANK:(tb + 1) * BANK], start=c == 0, stop=c == DC - 1)
                    i.then_inc(bank_done, 1)
            for tb in range(NTB):
                for a in range(2):
                    pe.wait_ge(bank_kept, J["kv"] + 2 * tb + a + 1)
                    o = bank(J["kvt"] + 2 * tb + a)
                    for t in range(4):
                        s = tb * BANK + t * P
                        i = nc.tensor.transpose(o[:, t * P:(t + 1) * P], kvT[:, a, s:s + P], ident[:])
                    i.then_inc(bank_done, 1)
            for k, w in enumerate(("txt", "f1", "f2")):
                weight(w, 5 + k)


def cross_phase(nc, ps, io, keep):
    ident, qwT, ws, bias, x1 = (keep[n] for n in ("ident", "qwT", "ws", "bias", "x1"))
    kvT, kvt, fused = keep["kvT"], keep["kvt"], keep["fused"]
    NTB = T // BANK
    with Mem(nc) as m:
        z = m.sb("z_c", [P, NT, D])
        zq = m.sb("zq", [P, NT, D], BF16)
        zqT = m.sb("zqT", [P, DC, T], BF16)
        identb = m.sb("identb_c", [P, P], BF16)
        fsum = m.sb("fsum", [P, 2, T])
        pr = m.sb("pr_c", [P, 4, 2, L])
        prT = m.sb("prT_c", [P, 2, BANK])
        st = m.sb("st_c", [P, NT, 6])
        mv = m.sb("mv_c", [P, NT, 2])
        ve, sd, rs = (m.sb(n, [P, NT]) for n in ("ve_c", "sd_c", "rs_c"))
        loc, am, isc, inv, sc = (m.sb(n, [P, 1]) for n in ("loc_c", "am_c", "isc_c", "inv_c", "sc_c"))
        nmax, rsum, rinv = (m.sb(n, [P, 32]) for n in ("nmax_c", "rsum_c", "rinv_c"))
        part = m.sb("part_c", [P, NT])
        dve_step, idb_ready, var_ready, std_ready, loc_ready, am_ready, scale_ready, z_quant = (
            m.sem(f"c_{n}") for n in ("dve_step", "idb_ready", "var_ready", "std_ready", "loc_ready", "am_ready", "scale_ready", "z_quant"))
        zT_done, zT_kept, txt_done, txt_kept, fsum_ready = (m.sem(f"c_{n}") for n in ("zT_done", "zT_kept", "txt_done", "txt_kept", "fsum_ready"))
        pool_step, fold_ready, rinv_ready = m.sem("c_pool_step"), m.sem("fold_ready"), m.sem("rinv_ready")
        s_done, max_ready, exp_done, pr_ready, pt_done, pt_kept, pv_done, pv_kept = (
            m.sem(f"c_{n}") for n in ("s_done", "max_ready", "exp_done", "pr_ready", "pt_done", "pt_kept", "pv_done", "pv_kept"))
        block = m.stack.enter_context(nc.Block())
        UN = 2 * B

        @block.gpsimd
        def _(pool):
            nc.gpsimd.tensor_copy(identb[:], ident[:]).then_inc(idb_ready, 1)
            pool.wait_ge(loc_ready, 1)
            nc.gpsimd.partition_all_reduce(am[:], loc[:], P, RMAX).then_inc(am_ready, 1)
            for n in range(UN + 3):
                if n < UN:
                    pool.wait_ge(rinv_ready, n + 1)
                    for a in range(2):
                        i = nc.gpsimd.tensor_scalar(pr[:, n % 4, a], pr[:, n % 4, a], rinv[:, 2 * n + a:2 * n + a + 1], None, ALU.mult)
                    i.then_inc(pr_ready, 1)
                k = n - 3
                if 0 <= k < B:
                    pool.wait_ge(pv_kept, k + 1)
                    cols = slice(k * L, (k + 1) * L)
                    nc.gpsimd.tensor_tensor(out=fsum[:, 1, cols], in0=fused[:, 0, cols], in1=fused[:, 1, cols], op=ALU.add).then_inc(pool_step, 1)
                    pool.wait_ge(pool_step, k + 1)
                    nc.gpsimd.tensor_scalar(fsum[:, 1, cols], fsum[:, 1, cols], 1.0 / 16.0, None, ALU.mult).then_inc(fold_ready, 1)

        @block.vector
        def _(dve):
            link = Chain(dve, dve_step)
            for t in range(NT):
                i = nc.vector.bn_stats(st[:, t], x1[:, t])
            link(i)
            for t in range(NT):
                i = nc.vector.bn_aggr(mv[:, t], st[:, t])
            link(i)
            nc.vector.tensor_scalar_add(ve[:], mv[:, :, 1], 1e-5).then_inc(var_ready, 1)
            dve.wait_ge(std_ready, 1)
            link(nc.vector.reciprocal(rs[:], sd[:]))
            for t in range(NT):
                i = nc.vector.tensor_scalar(z[:, t], x1[:, t], mv[:, t, 0:1], rs[:, t:t + 1], ALU.subtract, ALU.mult)
            link(i)
            nc.vector.tensor_reduce(loc[:], z[:].rearrange("p t d -> p (t d)"), X, ALU.max, apply_absolute_value=True).then_inc(loc_ready, 1)
            dve.wait_ge(am_ready, 1)
            activation_scale(nc, link, am[:], isc[:], inv[:])
            nc.vector.tensor_tensor(out=sc[:], in0=isc[:], in1=ws[:, 2:3], op=ALU.mult).then_inc(scale_ready, 1)
            for g in range(4):
                tiles = slice(4 * g, 4 * g + 4)
                link(nc.vector.tensor_scalar(z[:, tiles], z[:, tiles], inv[:], MAGIC, ALU.mult, ALU.add))
                nc.vector.tensor_scalar(zq[:, tiles], z[:, tiles], MAGIC, None, ALU.subtract).then_inc(z_quant, 1)

            def fold(cols):
                link(nc.vector.tensor_tensor(out=fsum[:, 0, cols], in0=fused[:, 0, cols], in1=fused[:, 1, cols], op=ALU.add))
                nc.vector.tensor_scalar_mul(fsum[:, 0, cols], fsum[:, 0, cols], 1.0 / 16.0).then_inc(fsum_ready, 1)

            for tb in range(NTB):
                dve.wait_ge(txt_kept, 2 * tb + 2)
                for b in (2 * tb, 2 * tb + 1):
                    fold(slice(b * L, (b + 1) * L))
            for n in range(UN + 3):
                if n < UN:
                    dve.wait_ge(s_done, n + 1)
                    nc.vector.tensor_reduce(nmax[:, 2 * n:2 * n + 2], ps[n % 2][:].rearrange("p (a j) -> p a j", a=2), X, ALU.max,
                                            negate=True).then_inc(max_ready, 1)
                k = n - 1
                if 0 <= k < UN:
                    dve.wait_ge(exp_done, k + 1)
                    nc.vector.reciprocal(rinv[:, 2 * k:2 * k + 2], rsum[:, 2 * k:2 * k + 2]).then_inc(rinv_ready, 1)
                k = n - 3
                if 0 <= k < UN:
                    layer, b = divmod(k, B)
                    cols = slice(b * L, (b + 1) * L)
                    dve.wait_ge(pv_done, k + 1)
                    for c in range(DC):
                        i = nc.vector.scalar_tensor_tensor(out=fused[:, c, cols], in0=ps[4 + k % 2][:, 0:L], scalar=0.1,
                                                           in1=fused[:, c, cols], op0=ALU.mult, op1=ALU.add)
                    i.then_inc(pv_kept, 1)

        @block.scalar
        def _(act):
            act.wait_ge(var_ready, 1)
            nc.scalar.activation(sd[:], ve[:], ACT.Sqrt).then_inc(std_ready, 1)
            for n in range(4):
                g, c = divmod(n, 2)
                act.wait_ge(zT_done, n + 1)
                nc.scalar.activation(zqT[:, c, g * 1024:(g + 1) * 1024], ps[n][:].bitcast(BF16), ACT.Copy).then_inc(zT_kept, 1)
            act.wait_ge(scale_ready, 1)
            for n in range(8):
                tb, oc = divmod(n, DC)
                act.wait_ge(txt_done, n + 1)
                nc.scalar.activation(fused[:, oc, tb * BANK:(tb + 1) * BANK], ps[4 + n % 4][:], ACT.Identity,
                                     scale=sc[:], bias=bias["txt"][:, oc:oc + 1]).then_inc(txt_kept, 1)
            for n in range(UN + 3):
                if n < UN:
                    act.wait_ge(max_ready, n + 1)
                    if n >= 4:
                        act.wait_ge(pt_done, n - 3)
                    for a in range(2):
                        i = nc.scalar.activation(pr[:, n % 4, a], ps[n % 2][:, a * L:(a + 1) * L], ACT.Exp,
                                                 bias=nmax[:, 2 * n + a:2 * n + a + 1], accum_out=rsum[:, 2 * n + a:2 * n + a + 1])
                    i.then_inc(exp_done, 1)
                k = n - 2
                if 0 <= k < UN:
                    act.wait_ge(pt_done, k + 1)
                    if k >= 2:
                        act.wait_ge(pv_done, k - 1)
                    nc.scalar.activation(prT[:, k % 2], ps[2 + k % 2][:], ACT.Copy).then_inc(pt_kept, 1)

        @block.tensor
        def _(pe):
            pe.wait_ge(idb_ready, 1)
            for n in range(4):
                g, c = divmod(n, 2)
                pe.wait_ge(z_quant, 2 * g + 2)
                for t in range(8):
                    i = nc.tensor.transpose(ps[n][:].bitcast(BF16)[:, t * P:(t + 1) * P], zq[:, 8 * g + t, c * P:(c + 1) * P], identb[:])
                i.then_inc(zT_done, 1)
            for n in range(8):
                tb, oc = divmod(n, DC)
                pe.wait_ge(zT_kept, 2 * (tb // 2) + 2)
                if n >= 4:
                    pe.wait_ge(txt_kept, n - 3)
                for c in range(DC):
                    i = nc.tensor.matmul(ps[4 + n % 4][:], qwT["txt"][:, c, oc * P:(oc + 1) * P], zqT[:, c, tb * BANK:(tb + 1) * BANK],
                                         start=c == 0, stop=c == DC - 1)
                i.then_inc(txt_done, 1)
            pe.wait_ge(txt_kept, 8)
            for n in range(UN + 3):
                if n < UN:
                    layer, b = divmod(n, B)
                    if layer:
                        pe.wait_ge(fold_ready, b + 1)
                    else:
                        pe.wait_ge(fsum_ready, b + 1)
                    if n >= 2:
                        pe.wait_ge(exp_done, n - 1)
                    for a in range(2):
                        s = b * L + a * P
                        i = nc.tensor.matmul(ps[n % 2][:, a * L:(a + 1) * L], fsum[:, layer, s:s + P], kvT[:, layer, b * L:(b + 1) * L],
                                             start=True, stop=True)
                    i.then_inc(s_done, 1)
                k = n - 2
                if 0 <= k < UN:
                    pe.wait_ge(pr_ready, k + 1)
                    if k >= 2:
                        pe.wait_ge(pt_kept, k - 1)
                    for a in range(2):
                        for jc in range(2):
                            i = nc.tensor.transpose(ps[2 + k % 2][:, jc * L + a * P:jc * L + (a + 1) * P], pr[:, k % 4, a, jc * P:(jc + 1) * P], ident[:])
                    i.then_inc(pt_done, 1)
                k = n - 3
                if 0 <= k < UN:
                    layer, b = divmod(k, B)
                    pe.wait_ge(pt_kept, k + 1)
                    if k >= 2:
                        pe.wait_ge(pv_kept, k - 1)
                    for jc in range(2):
                        i = nc.tensor.matmul(ps[4 + k % 2][:, 0:L], kvt[:, layer, 2 * b + jc], prT[:, k % 2, jc * L:(jc + 1) * L],
                                             start=jc == 0, stop=jc == 1)
                    i.then_inc(pv_done, 1)


def feed_phase(nc, ps, io, keep):
    ident, qwT, ws, bias, x1 = (keep[n] for n in ("ident", "qwT", "ws", "bias", "x1"))
    fused, avg = keep["fused"], keep["avg"]
    NTB = T // BANK
    FC = 8
    with Mem(nc) as m:
        h = m.sb("h", [P, FC, T])
        hq = m.sb("hq", [P, FC, T], BF16)
        qf = m.sb("qf", [P, DC, T], BF16)
        oT = m.sb("oT", [P, DC, T])
        qavg = m.sb("qavg", [P, DC, B], BF16)
        avm = m.sb("avm", [P, DC, B])
        part = m.sb("part_f", [P, 40])
        loc, am, isc, inv, sc = (m.sb(n, [P, 2]) for n in ("loc_f", "am_f", "isc_f", "inv_f", "sc_f"))
        dve_step, loc_ready, am_ready, scale_ready, f_quant, h_quant = (
            m.sem(f"f_{n}") for n in ("dve_step", "loc_ready", "am_ready", "scale_ready", "f_quant", "h_quant"))
        h_done, h_kept, o_done, o_kept, t_done, t_kept = (m.sem(f"f_{n}") for n in ("h_done", "h_kept", "o_done", "o_kept", "t_done", "t_kept"))
        block = m.stack.enter_context(nc.Block())

        @block.gpsimd
        def _(pool):
            for a in range(2):
                pool.wait_ge(loc_ready, a + 1)
                nc.gpsimd.partition_all_reduce(am[:, a:a + 1], loc[:, a:a + 1], P, RMAX).then_inc(am_ready, 1)

        @block.vector
        def _(dve):
            link = Chain(dve, dve_step)
            nc.vector.tensor_reduce(part[:, 0:1], fused.rearrange("p c t -> p (c t)"), X, ALU.max, apply_absolute_value=True)
            link(nc.vector.tensor_reduce(part[:, 1:2], avg[:].rearrange("p c b -> p (c b)"), X, ALU.max, apply_absolute_value=True))
            nc.vector.tensor_reduce(loc[:, 0:1], part[:, 0:2], X, ALU.max).then_inc(loc_ready, 1)
            dve.wait_ge(am_ready, 1)
            activation_scale(nc, link, am[:, 0:1], isc[:, 0:1], inv[:, 0:1])
            nc.vector.tensor_tensor(out=sc[:, 0:1], in0=isc[:, 0:1], in1=ws[:, 5:6], op=ALU.mult).then_inc(scale_ready, 1)
            link(nc.vector.tensor_scalar(avm[:], avg[:], inv[:, 0:1], MAGIC, ALU.mult, ALU.add))
            nc.vector.tensor_scalar(qavg[:], avm[:], MAGIC, None, ALU.subtract)
            for tb in range(NTB):
                cols = slice(tb * BANK, (tb + 1) * BANK)
                link(nc.vector.tensor_scalar(fused[:, :, cols], fused[:, :, cols], inv[:, 0:1], MAGIC, ALU.mult, ALU.add))
                nc.vector.tensor_scalar(qf[:, :, cols], fused[:, :, cols], MAGIC, None, ALU.subtract).then_inc(f_quant, 1)
            for n in range(NTB * FC):
                tb, fc = divmod(n, FC)
                dve.wait_ge(h_kept, n + 1)
                i = nc.vector.reduce_max(part[:, 2 + n:3 + n], h[:, fc, tb * BANK:(tb + 1) * BANK], X)
            link(i)
            nc.vector.reduce_max(loc[:, 1:2], part[:, 2:2 + NTB * FC], X).then_inc(loc_ready, 1)
            dve.wait_ge(am_ready, 2)
            activation_scale(nc, link, am[:, 1:2], isc[:, 1:2], inv[:, 1:2])
            nc.vector.tensor_tensor(out=sc[:, 1:2], in0=isc[:, 1:2], in1=ws[:, 6:7], op=ALU.mult).then_inc(scale_ready, 1)
            for tb in range(NTB):
                cols = slice(tb * BANK, (tb + 1) * BANK)
                link(nc.vector.tensor_scalar(h[:, :, cols], h[:, :, cols], inv[:, 1:2], MAGIC, ALU.mult, ALU.add))
                nc.vector.tensor_scalar(hq[:, :, cols], h[:, :, cols], MAGIC, None, ALU.subtract).then_inc(h_quant, 1)
            for n in range(NT // 2):
                dve.wait_ge(t_done, n + 1)
                nc.vector.tensor_tensor(out=x1[:, 2 * n:2 * n + 2], in0=ps[n % 4][:].rearrange("p (t d) -> p t d", t=2),
                                        in1=x1[:, 2 * n:2 * n + 2], op=ALU.add).then_inc(t_kept, 1)

        @block.scalar
        def _(act):
            act.wait_ge(scale_ready, 1)
            for n in range(NTB * FC):
                tb, fc = divmod(n, FC)
                act.wait_ge(h_done, n + 1)
                nc.scalar.activation(h[:, fc, tb * BANK:(tb + 1) * BANK], ps[n % 8][:], ACT.Relu,
                                     scale=sc[:, 0:1], bias=bias["f1"][:, fc:fc + 1]).then_inc(h_kept, 1)
            act.wait_ge(scale_ready, 2)
            for n in range(NTB * DC):
                tb, oc = divmod(n, DC)
                act.wait_ge(o_done, n + 1)
                nc.scalar.activation(oT[:, oc, tb * BANK:(tb + 1) * BANK], ps[4 + n % 4][:], ACT.Identity,
                                     scale=sc[:, 1:2], bias=bias["f2"][:, oc:oc + 1]).then_inc(o_kept, 1)

        @block.tensor
        def _(pe):
            for n in range(NTB * FC):
                tb, fc = divmod(n, FC)
                pe.wait_ge(f_quant, tb + 1)
                if n >= 8:
                    pe.wait_ge(h_kept, n - 7)
                for c in range(DC):
                    nc.tensor.matmul(ps[n % 8][:], qwT["f1"][:, c, fc * P:(fc + 1) * P], qf[:, c, tb * BANK:(tb + 1) * BANK],
                                     start=c == 0, stop=False)
                for c in range(DC):
                    i = nc.tensor.matmul(ps[n % 8][:], qwT["f1"][:, DC + c, fc * P:(fc + 1) * P],
                                         bc(qavg[:, c, 2 * tb:2 * tb + 2].unsqueeze(2), P, 2, L), start=False, stop=c == DC - 1)
                i.then_inc(h_done, 1)
            pe.wait_ge(h_kept, NTB * FC)
            for tb in range(NTB):
                pe.wait_ge(h_quant, tb + 1)
                for oc in range(DC):
                    n = tb * DC + oc
                    if n >= 4:
                        pe.wait_ge(o_kept, n - 3)
                    for fc in range(FC):
                        i = nc.tensor.matmul(ps[4 + n % 4][:], qwT["f2"][:, fc, oc * P:(oc + 1) * P], hq[:, fc, tb * BANK:(tb + 1) * BANK],
                                             start=fc == 0, stop=fc == FC - 1)
                    i.then_inc(o_done, 1)
                pe.wait_ge(o_kept, 2 * tb + 2)
                for k in (2 * tb, 2 * tb + 1):
                    if k >= 4:
                        pe.wait_ge(t_kept, k - 3)
                    for t in range(2):
                        for c in range(DC):
                            s = (2 * k + t) * P
                            i = nc.tensor.transpose(ps[k % 4][:, t * D + c * P:t * D + (c + 1) * P], oT[:, c, s:s + P], ident[:])
                    i.then_inc(t_done, 1)


NE, FF = 8, 1024
FFC = FF // P
SLOTS = T // P + NE - 1
I32 = mybir.dt.int32


def route_phase(nc, ps, io, keep):
    ident, x2, slot, tile_e = (keep[n] for n in ("ident", "x1", "slot", "tile_e"))
    w1T, w2T, stage, rows = keep["w1T"], keep["w2T"], keep["stage"], keep["rows"]
    with Mem(nc) as m:
        y = m.sb("y", [P, NT, D])
        yT = m.sb("yT", [P, DC, T])
        st = m.sb("st_e", [P, NT, 6])
        mv = m.sb("mv_e", [P, NT, 2])
        ve, sd, rs = (m.sb(n, [P, NT]) for n in ("ve_e", "sd_e", "rs_e"))
        wr = m.sb("router", [NE, D])
        wrT = m.sb("routerT", [P, DC, NE])
        br = m.sb("br", [P, NE])
        lg, eq, hot = (m.sb(n, [P, NT, NE]) for n in ("lg", "eq", "hot"))
        hotb = m.sb("hotb", [P, NT, NE], BF16)
        tri, ones = m.sb("tri", [P, P], BF16), m.sb("ones", [P, P], BF16)
        zero = m.sb("zero", [P, 1, D])
        iota8 = m.sb("iota8", [P, NE])
        iotat = m.sb("iotat", [1, SLOTS])
        best, first, slotf = (m.sb(n, [P, NT]) for n in ("best", "first", "slotf"))
        cnt, tiles, ends, base = (m.sb(n, [P, NE]) for n in ("cnt_e", "tiles", "ends", "base"))
        cnti = m.sb("cnti", [P, NE], I32)
        cmp = m.sb("cmp", [1, SLOTS, NE - 1])
        tef = m.sb("tef", [1, SLOTS])
        w1_in, w2_in = [m.sem("w1_in0"), m.sem("w1_in1")], [m.sem("w2_in0"), m.sem("w2_in1")]
        wr_in, br_in, zero_sent, row_sent = (m.sem(n) for n in ("wr_in_e", "br_in", "zero_sent", "row_sent"))
        pool_step, consts_ready, dve_step, var_ready, std_ready, y_ready = (
            m.sem(f"e_{n}") for n in ("pool_step", "consts_ready", "dve_step", "var_ready", "std_ready", "y_ready"))
        wT_done, wT_kept, yT_done, yT_kept, wrT_done, wrT_kept, lg_done, hot_ready, pos_done, slot_ready = (
            m.sem(f"e_{n}") for n in ("wT_done", "wT_kept", "yT_done", "yT_kept", "wrT_done", "wrT_kept", "lg_done", "hot_ready", "pos_done", "slot_ready"))
        w_banks = ps[0:4]
        y_banks, lg_bank, pos_bank = ps[4:6], ps[6], ps[7]
        stages = [stage, yT[:].rearrange("p c t -> p (c t)")]
        s1 = [x[:, 0:FFC * D].rearrange("p (f d) -> p f d", d=D) for x in stages]
        s2 = [x[:, FFC * D:2 * FFC * D].rearrange("p (c f) -> p c f", f=FF) for x in stages]
        block = m.stack.enter_context(nc.Block())

        @block.sync
        def _(sp):
            sp.dma_start(wr[:], io["L0_ffn_Wr"]).then_inc(wr_in, 16)
            sp.dma_start(br[:], bc(io["L0_ffn_br"].unsqueeze(0), P, NE)).then_inc(br_in, 16)
            w1 = io["L0_ffn_W1"].rearrange("e (f p) d -> p (e f) d", p=P)
            w2 = io["L0_ffn_W2"].rearrange("e (c p) f -> p (e c) f", p=P)

            def load(e, place, w1_used, w2_used):
                if w2_used is not None:
                    sp.wait_ge(wT_done, w1_used)
                    sp.nop(nofuse=True)
                sp.dma_start(s1[place], w1[:, bass.ds(e * FFC, FFC)]).then_inc(w1_in[place], 16)
                if w2_used is not None:
                    sp.wait_ge(wT_done, w2_used)
                    sp.nop(nofuse=True)
                sp.dma_start(s2[place], w2[:, bass.ds(e * DC, DC)]).then_inc(w2_in[place], 16)

            load(0, 0, None, None)
            load(1, 0, 4, 8)
            sp.wait_ge(lg_done, 1)
            load(2, 1, None, None)
            load(3, 0, 12, 16)
            with sp.Fori(2, NE // 2) as j:
                load(2 * j, 1, 16 * j - 12, 16 * j - 8)
                load(2 * j + 1, 0, 16 * j - 4, 16 * j)
            sp.wait_ge(zero_sent, 16)
            sp.wait_ge(row_sent, 16 * NT)

        @block.gpsimd
        def _(pool):
            nc.gpsimd.memset(zero[:], 0.0).then_inc(pool_step, 1)
            pool.wait_ge(pool_step, 1)
            pool.dma_start(rows.rearrange("(k p) d -> p k d", p=P), bc(zero[:], P, SLOTS, D)).then_inc(zero_sent, 16)
            nc.gpsimd.memset(ones[:], 1.0).then_inc(pool_step, 1)
            pool.wait_ge(pool_step, 2)
            nc.gpsimd.affine_select(out=tri[:], in_=ones[:], compare_op=ALU.is_gt, fill=0.0, base=0,
                                    pattern=[[1, P]], channel_multiplier=-1).then_inc(consts_ready, 1)
            nc.gpsimd.iota(iota8[:], pattern=[[1, NE]], base=-NE, channel_multiplier=0,
                           allow_small_or_imprecise_dtypes=True).then_inc(consts_ready, 1)
            nc.gpsimd.iota(iotat[:], pattern=[[1, SLOTS]], base=0, channel_multiplier=0,
                           allow_small_or_imprecise_dtypes=True).then_inc(consts_ready, 1)
            pool.wait_ge(zero_sent, 16)
            pool.wait_ge(slot_ready, 1)
            for t in range(NT):
                pool.indirect_dma_start(out=rows, out_offset=bass.IndirectOffsetOnAxis(ap=slot[:, t:t + 1], axis=0),
                                        in_=y[:, t], in_offset=None).then_inc(row_sent, 16)

        @block.vector
        def _(dve):
            link = Chain(dve, dve_step)
            for t in range(NT):
                i = nc.vector.bn_stats(st[:, t], x2[:, t])
            link(i)
            for t in range(NT):
                i = nc.vector.bn_aggr(mv[:, t], st[:, t])
            link(i)
            nc.vector.tensor_scalar_add(ve[:], mv[:, :, 1], 1e-5).then_inc(var_ready, 1)
            dve.wait_ge(std_ready, 1)
            link(nc.vector.reciprocal(rs[:], sd[:]))
            for t in range(NT):
                nc.vector.tensor_scalar(y[:, t], x2[:, t], mv[:, t, 0:1], rs[:, t:t + 1], ALU.subtract, ALU.mult).then_inc(y_ready, 1)
            dve.wait_ge(wrT_done, 1)
            nc.vector.tensor_copy(wrT[:].rearrange("p c e -> p (c e)"), lg_bank[:, 0:DC * NE]).then_inc(wrT_kept, 1)
            for n in range(8):
                tb, c = divmod(n, DC)
                dve.wait_ge(yT_done, n + 1)
                nc.vector.tensor_copy(yT[:, c, tb * BANK:(tb + 1) * BANK], y_banks[n % 2][:]).then_inc(yT_kept, 1)
            dve.wait_ge(consts_ready, 3)
            dve.wait_ge(br_in, 16)
            dve.wait_ge(lg_done, 1)
            link(nc.vector.tensor_tensor(out=lg[:], in0=lg_bank[:, 0:NT * NE].rearrange("p (t e) -> p t e", e=NE),
                                         in1=bc(br[:].unsqueeze(1), P, NT, NE), op=ALU.add))
            link(nc.vector.tensor_reduce(best[:], lg[:], X, ALU.max))
            link(nc.vector.tensor_tensor(out=eq[:], in0=lg[:], in1=bc(best[:].unsqueeze(2), P, NT, NE), op=ALU.is_ge))
            link(nc.vector.tensor_tensor(out=eq[:], in0=eq[:], in1=bc(iota8[:].unsqueeze(1), P, NT, NE), op=ALU.mult))
            link(nc.vector.tensor_reduce(first[:], eq[:], X, ALU.min))
            link(nc.vector.tensor_tensor(out=hot[:], in0=bc(iota8[:].unsqueeze(1), P, NT, NE),
                                         in1=bc(first[:].unsqueeze(2), P, NT, NE), op=ALU.is_equal))
            nc.vector.tensor_copy(hotb[:], hot[:]).then_inc(hot_ready, 1)
            dve.wait_ge(pos_done, 1)
            link(nc.vector.tensor_scalar_add(cnt[:], pos_bank[:, NT * NE:(NT + 1) * NE], float(P - 1)))
            link(nc.vector.tensor_copy(cnti[:], cnt[:]))
            link(nc.vector.tensor_single_scalar(cnti[:], cnti[:], 7, op=ALU.logical_shift_right))
            link(nc.vector.tensor_copy(tiles[:], cnti[:]))
            link(nc.vector.tensor_copy(ends[:, 0:1], tiles[:, 0:1]))
            for e in range(1, NE):
                link(nc.vector.tensor_tensor(out=ends[:, e:e + 1], in0=ends[:, e - 1:e], in1=tiles[:, e:e + 1], op=ALU.add))
            link(nc.vector.tensor_tensor(out=base[:], in0=ends[:], in1=tiles[:], op=ALU.subtract))
            link(nc.vector.tensor_scalar_mul(base[:], base[:], float(P)))
            link(nc.vector.tensor_tensor(out=eq[:], in0=pos_bank[:, 0:NT * NE].rearrange("p (t e) -> p t e", e=NE),
                                         in1=bc(base[:].unsqueeze(1), P, NT, NE), op=ALU.add))
            link(nc.vector.tensor_tensor(out=eq[:], in0=eq[:], in1=hot[:], op=ALU.mult))
            link(nc.vector.tensor_reduce(slotf[:], eq[:], X, ALU.add))
            nc.vector.tensor_copy(slot[:], slotf[:]).then_inc(slot_ready, 1)
            link(nc.vector.tensor_tensor(out=cmp[:], in0=bc(iotat[:].unsqueeze(2), 1, SLOTS, NE - 1),
                                         in1=bc(ends[0:1, 0:NE - 1].unsqueeze(1), 1, SLOTS, NE - 1), op=ALU.is_ge))
            link(nc.vector.tensor_reduce(tef[:], cmp[:], X, ALU.add))
            link(nc.vector.tensor_copy(tile_e[:], tef[:]))

        @block.scalar
        def _(act):
            act.wait_ge(var_ready, 1)
            nc.scalar.activation(sd[:], ve[:], ACT.Sqrt).then_inc(std_ready, 1)
            with act.Fori(0, NE) as e:
                for n in range(8):
                    act.wait_ge(wT_done, 8 * e + n + 1)
                    if n < 4:
                        c, half = divmod(n, 2)
                        dst = w1T[:].rearrange("p (e c f) -> p e c f", e=NE, c=DC)[:, bass.ds(e, 1), c, half * BANK:(half + 1) * BANK]
                    else:
                        dst = w2T[:].rearrange("p (e q j) -> p e q j", e=NE, q=4)[:, bass.ds(e, 1), n - 4]
                    nc.scalar.activation(dst, w_banks[n % 4][:].unsqueeze(1), ACT.Copy).then_inc(wT_kept, 1)

        @block.tensor
        def _(pe):
            def weights(e, place, loads):
                for n in range(8):
                    if n == 0:
                        pe.wait_ge(w1_in[place], 16 * loads)
                    if n == 4:
                        pe.wait_ge(w2_in[place], 16 * loads)
                    if n >= 4 or not isinstance(e, int) or e:
                        pe.wait_ge(wT_kept, 8 * e + n - 3)
                    for k in range(4):
                        if n < 4:
                            c, half = divmod(n, 2)
                            src = s1[place][:, 4 * half + k, c * P:(c + 1) * P]
                        else:
                            fc, c = divmod(4 * (n - 4) + k, DC)
                            src = s2[place][:, c, fc * P:(fc + 1) * P]
                        i = nc.tensor.transpose(w_banks[n % 4][:, k * P:(k + 1) * P], src, ident[:])
                    i.then_inc(wT_done, 1)

            weights(0, 0, 1)
            pe.wait_ge(wr_in, 16)
            for c in range(DC):
                i = nc.tensor.transpose(lg_bank[:, c * NE:(c + 1) * NE], wr[:, c * P:(c + 1) * P], ident[0:NE, 0:NE])
            i.then_inc(wrT_done, 1)
            for n in range(8):
                tb, c = divmod(n, DC)
                pe.wait_ge(y_ready, 4 * tb + 4)
                if n >= 2:
                    pe.wait_ge(yT_kept, n - 1)
                for t in range(4):
                    i = nc.tensor.transpose(y_banks[n % 2][:, t * P:(t + 1) * P], y[:, 4 * tb + t, c * P:(c + 1) * P], ident[:])
                i.then_inc(yT_done, 1)
            pe.wait_ge(wrT_kept, 1)
            pe.wait_ge(yT_kept, 8)
            for t in range(NT):
                for c in range(DC):
                    i = nc.tensor.matmul(lg_bank[:, t * NE:(t + 1) * NE], yT[:, c, t * P:(t + 1) * P], wrT[:, c], start=c == 0, stop=c == DC - 1)
            i.then_inc(lg_done, 1)
            weights(1, 0, 2)
            pe.wait_ge(hot_ready, 1)
            nc.tensor.matmul(pos_bank[:, 0:NT * NE], tri[:], hotb[:].rearrange("p t e -> p (t e)"), start=True, stop=False)
            for t in range(NT - 1):
                nc.tensor.matmul(pos_bank[:, (t + 1) * NE:NT * NE].rearrange("p (t e) -> p t e", e=NE), ones[:],
                                 bc(hotb[:, t:t + 1], P, NT - 1 - t, NE), start=False, stop=t == NT - 2)
            for t in range(NT):
                i = nc.tensor.matmul(pos_bank[:, NT * NE:(NT + 1) * NE], ones[:], hotb[:, t], start=t == 0, stop=t == NT - 1)
            i.then_inc(pos_done, 1)
            with pe.Fori(1, NE // 2) as j:
                weights(2 * j, 1, j)
                weights(2 * j + 1, 0, j + 2)


def expert_phase(nc, ps, io, keep):
    ident, tile_e, w1T, w2T = (keep[n] for n in ("ident", "tile_e", "w1T", "w2T"))
    rows, outs = keep["rows"], keep["outs"]
    with Mem(nc) as m:
        b1T = m.sb("b1T", [P, NE * FFC])
        b1n = m.sb("b1n", [NE * FFC, P])
        b2 = m.sb("b2", [P, NE * D])
        yt = m.sb("yt", [P, 2, D])
        yTt = m.sb("yTt", [P, 2, DC, P])
        hs = m.sb("hs", [P, FF])
        hT = m.sb("hT", [P, 2, FFC, P])
        ot = m.sb("ot", [P, 2, D])
        b1_in, b2_in, y_in = m.sem("b1_in"), m.sem("b2_in"), [m.sem("y_in0"), m.sem("y_in1")]
        b1T_done, b1T_kept, yT_done, yT_kept, h_done, h_kept, hT_done, hT_kept, o_done, o_kept = (
            m.sem(f"x_{n}") for n in ("b1T_done", "b1T_kept", "yT_done", "yT_kept", "h_done", "h_kept", "hT_done", "hT_kept", "o_done", "o_kept"))
        o_sent = [m.sem("o_sent0"), m.sem("o_sent1")]
        yT_bank, h_banks, hT_banks, o_bank = ps[0], ps[1:3], ps[3:5], ps[5]
        N2 = (SLOTS - 1) // 2
        assert SLOTS % 2
        rv = rows.rearrange("(k p) d -> k p d", p=P)
        ov = outs.rearrange("(k p) d -> k p d", p=P)

        def past(j, c, n):
            return not isinstance(j, int) or 2 * j + c >= n

        block = m.stack.enter_context(nc.Block())

        @block.sync
        def _(sp):
            sp.dma_start(b1n[:], io["L0_ffn_b1"].rearrange("e (c p) -> (e c) p", p=P)).then_inc(b1_in, 16)
            sp.dma_start(b2[:], bc(io["L0_ffn_b2"].rearrange("e d -> (e d)").unsqueeze(0), P, NE * D)).then_inc(b2_in, 16)

            def fetch(j, c):
                if past(j, c, 2):
                    sp.wait_ge(yT_done, 2 * j + c - 1)
                sp.dma_start(yt[:, c % 2], rv[bass.ds(2 * j + c, 1)].rearrange("k p d -> p (k d)")).then_inc(y_in[c % 2], 16)

            def store(j, c):
                sp.wait_ge(o_kept, 2 * j + c + 1)
                sp.dma_start(ov[bass.ds(2 * j + c, 1)].rearrange("k p d -> p (k d)"), ot[:, c % 2]).then_inc(o_sent[c % 2], 16)

            fetch(0, 0)
            fetch(0, 1)
            fetch(0, 2)

            def turn(j):
                fetch(j, 3)
                store(j, 0)
                fetch(j, 4)
                store(j, 1)

            turn(0)
            with sp.Fori(1, N2 - 1) as j:
                turn(j)
            for c in range(3):
                store(N2 - 1, c)
            sp.wait_ge(o_sent[0], 16 * (N2 + 1))
            sp.wait_ge(o_sent[1], 16 * N2)

        @block.vector
        def _(dve):
            dve.wait_ge(b1T_done, 1)
            nc.vector.tensor_copy(b1T[:], o_bank[:, 0:NE * FFC]).then_inc(b1T_kept, 1)
            dve.wait_ge(b2_in, 16)

            def keep_yT(j, c):
                dve.wait_ge(yT_done, 2 * j + c + 1)
                if past(j, c, 2):
                    dve.wait_ge(h_done, 2 * j + c - 1)
                nc.vector.tensor_copy(yTt[:, c % 2], yT_bank[:, 0:DC * P].rearrange("p (c t) -> p c t", c=DC)).then_inc(yT_kept, 1)

            def keep_h(j, c):
                dve.wait_ge(h_done, 2 * j + c + 1)
                if past(j, c, 1):
                    dve.wait_ge(hT_done, 2 * j + c)
                nc.vector.tensor_copy(hs[:, 0:BANK], h_banks[0][:])
                nc.vector.tensor_copy(hs[:, BANK:FF], h_banks[1][:]).then_inc(h_kept, 1)

            def keep_o(j, c):
                e = dve.value_load(tile_e[0:1, bass.ds(2 * j + c, 1)], min_val=0, max_val=NE - 1)
                dve.wait_ge(o_done, 2 * j + c + 1)
                if past(j, c, 2):
                    dve.wait_ge(o_sent[c % 2], 16 * (j + c // 2))
                nc.vector.tensor_tensor(out=ot[:, c % 2], in0=o_bank[:, 0:D], in1=b2[:, bass.ds(e * D, D)], op=ALU.add).then_inc(o_kept, 1)

            keep_yT(0, 0)
            keep_yT(0, 1)
            keep_h(0, 0)

            def turn(j, c, last):
                if not last:
                    keep_yT(j, c + 1)
                keep_h(j, c)
                keep_o(j, c - 1)

            turn(0, 1, False)
            turn(0, 2, False)
            with dve.Fori(1, N2 - 1) as j:
                turn(j, 1, False)
                turn(j, 2, False)
            turn(N2 - 1, 1, False)
            turn(N2 - 1, 2, True)
            keep_o(N2 - 1, 2)

        @block.scalar
        def _(act):
            act.wait_ge(b1T_kept, 1)

            def relu(j, c):
                e = act.value_load(tile_e[0:1, bass.ds(2 * j + c, 1)], min_val=0, max_val=NE - 1)
                act.wait_ge(hT_done, 2 * j + c + 1)
                if past(j, c, 2):
                    act.wait_ge(o_done, 2 * j + c - 1)
                for fc in range(FFC):
                    i = nc.scalar.activation(hT[:, c % 2, fc], hT_banks[fc // 4][:, fc % 4 * P:(fc % 4 + 1) * P], ACT.Relu,
                                             bias=b1T[:, bass.ds(e * FFC + fc, 1)])
                i.then_inc(hT_kept, 1)

            for c in range(3):
                relu(0, c)
            with act.Fori(1, N2) as j:
                relu(j, 1)
                relu(j, 2)

        @block.tensor
        def _(pe):
            pe.wait_ge(b1_in, 16)
            nc.tensor.transpose(o_bank[:, 0:NE * FFC], b1n[:], ident[0:NE * FFC, 0:NE * FFC]).then_inc(b1T_done, 1)
            pe.wait_ge(b1T_kept, 1)

            def turn_y(j, c):
                pe.wait_ge(y_in[c % 2], 16 * (j + c // 2 + 1))
                if past(j, c, 1):
                    pe.wait_ge(yT_kept, 2 * j + c)
                for k in range(DC):
                    i = nc.tensor.transpose(yT_bank[:, k * P:(k + 1) * P], yt[:, c % 2, k * P:(k + 1) * P], ident[:])
                i.then_inc(yT_done, 1)

            def layer1(j, c):
                e = pe.value_load(tile_e[0:1, bass.ds(2 * j + c, 1)], min_val=0, max_val=NE - 1)
                pe.wait_ge(yT_kept, 2 * j + c + 1)
                if past(j, c, 1):
                    pe.wait_ge(h_kept, 2 * j + c)
                for half in range(2):
                    for k in range(DC):
                        i = nc.tensor.matmul(h_banks[half][:], yTt[:, c % 2, k], w1T[:, bass.ds(e * (DC * FF) + k * FF + half * BANK, BANK)],
                                             start=k == 0, stop=k == DC - 1)
                i.then_inc(h_done, 1)

            def turn_h(j, c):
                pe.wait_ge(h_kept, 2 * j + c + 1)
                if past(j, c, 1):
                    pe.wait_ge(hT_kept, 2 * j + c)
                for fc in range(FFC):
                    i = nc.tensor.transpose(hT_banks[fc // 4][:, fc % 4 * P:(fc % 4 + 1) * P], hs[:, fc * P:(fc + 1) * P], ident[:])
                i.then_inc(hT_done, 1)

            def layer2(j, c):
                e = pe.value_load(tile_e[0:1, bass.ds(2 * j + c, 1)], min_val=0, max_val=NE - 1)
                pe.wait_ge(hT_kept, 2 * j + c + 1)
                if past(j, c, 1):
                    pe.wait_ge(o_kept, 2 * j + c)
                for fc in range(FFC):
                    i = nc.tensor.matmul(o_bank[:, 0:D], hT[:, c % 2, fc], w2T[:, bass.ds(e * (FFC * D) + fc * D, D)],
                                         start=fc == 0, stop=fc == FFC - 1)
                i.then_inc(o_done, 1)

            turn_y(0, 0)
            turn_y(0, 1)
            layer1(0, 0)
            turn_h(0, 0)

            def turn(j, c, last):
                if not last:
                    turn_y(j, c + 1)
                layer1(j, c)
                layer2(j, c - 1)
                turn_h(j, c)

            turn(0, 1, False)
            turn(0, 2, False)
            with pe.Fori(1, N2 - 1) as j:
                turn(j, 1, False)
                turn(j, 2, False)
            turn(N2 - 1, 1, False)
            turn(N2 - 1, 2, True)
            layer2(N2 - 1, 2)


def final_phase(nc, ps, io, keep, out):
    x2, slot, outs = keep["x1"], keep["slot"], keep["outs"]
    with Mem(nc) as m:
        g = m.sb("g", [P, NT, D])
        row_in = [m.sem(f"row_in{k}") for k in range(4)]
        sum_ready, out_sent = m.sem("sum_ready"), m.sem("out_sent")
        block = m.stack.enter_context(nc.Block())

        @block.gpsimd
        def _(pool):
            for t in range(NT):
                pool.indirect_dma_start(out=g[:, t], out_offset=None, in_=outs,
                                        in_offset=bass.IndirectOffsetOnAxis(ap=slot[:, t:t + 1], axis=0)).then_inc(row_in[t // 4], 16)

        @block.vector
        def _(dve):
            for k in range(4):
                dve.wait_ge(row_in[k], 64)
                nc.vector.tensor_tensor(out=g[:, 4 * k:4 * k + 4], in0=g[:, 4 * k:4 * k + 4], in1=x2[:, 4 * k:4 * k + 4], op=ALU.add).then_inc(sum_ready, 1)

        @block.sync
        def _(sp):
            ov = out.rearrange("b s d -> (b s) d").rearrange("(t p) d -> p t d", p=P)
            for k in range(4):
                sp.wait_ge(sum_ready, k + 1)
                sp.dma_start(ov[:, 4 * k:4 * k + 4], g[:, 4 * k:4 * k + 4]).then_inc(out_sent, 16)
            sp.wait_ge(out_sent, 64)


def build(nc, io, out):
    with ExitStack() as sems, Mem(nc) as top:
        Mem.sems = sems
        ps = [top.stack.enter_context(nc.psum_tensor(f"bank{i}", [P, BANK], F32)) for i in range(8)]
        keep = {"ident": top.sb("ident", [P, P]), "aT": top.sb("aT", [P, B // 2, GAM, L])}
        with Mem(nc) as m2:
            for n in ("qu", "qv", "kT"):
                keep[n] = m2.sb(n, [P, DC, T])
            keep["vt"] = m2.sb("vt", [P, NT, D])
            keep["rT"] = m2.sb("rT", [P, DC, NR + 1])
            keep["mask8"] = m2.sb("mask8", [P, 8])
            project_phase(nc, ps, io, keep)
            attention_phase(nc, ps, io, keep)
        keep["x1"] = top.sb("x1", [P, NT, D])
        with Mem(nc) as m:
            keep["qwT"] = {w: m.sb(f"qwT_{w}", [P, len(chunks(XSHAPE[w][1])), XSHAPE[w][0]], BF16) for w in XW}
            keep["ws"] = m.sb("ws", [P, len(XW)])
            keep["bias"] = {w: m.sb(f"bias_{w}", [P, XSHAPE[w][0] // P]) for w in XW}
            keep["avg"] = m.sb("avg", [P, DC, B])
            keep["fused"] = keep["aT"][:].rearrange("p a g i -> p (a g i)").rearrange("p (c t) -> p c t", c=DC)
            with Mem(nc) as m2:
                keep["kvT"] = m2.sb("kvT", [P, 2, T])
                keep["kvt"] = m2.sb("kvt", [P, 2, NT, P])
                context_phase(nc, ps, io, keep)
                cross_phase(nc, ps, io, keep)
            feed_phase(nc, ps, io, keep)
        with Mem(nc) as m:
            keep["slot"] = m.sb("slot", [P, NT], U32)
            keep["tile_e"] = m.sb("tile_e", [1, SLOTS], I32)
            keep["rows"] = nc.dram_tensor("expert_rows", [SLOTS * P, D], F32).ap()
            keep["outs"] = nc.dram_tensor("expert_outs", [SLOTS * P, D], F32).ap()
            with Mem(nc) as m2:
                keep["w1T"] = m2.sb("w1T", [P, NE * DC * FF])
                keep["w2T"] = m2.sb("w2T", [P, NE * FFC * D])
                keep["stage"] = keep["aT"][:].rearrange("p a g i -> p (a g i)")
                route_phase(nc, ps, io, keep)
                expert_phase(nc, ps, io, keep)
            final_phase(nc, ps, io, keep, out)


_INS = ("x", "ctx_768") + tuple(f"L0_attn_{n}" for n in ("gamma", "beta", "Wq", "Wk", "Wv", "Wr", "u_bias", "v_bias", "Wo", "bo", "rel_pos_emb")) \
    + tuple(f"L0_xattn_{k}_{n}" for n in XW for k in ("W", "b")) \
    + tuple(f"L0_ffn_{n}" for n in ("Wr", "br", "W1", "b1", "W2", "b2"))


def kernel(**inputs):
    import numpy as _np
    import concourse.bacc as _bacc
    from concourse import mybir as _mybir
    from concourse.bass_utils import run_bass_kernel_spmd as _run

    nc = _bacc.Bacc("TRN2", target_bir_lowering=False, num_devices=1)
    arrays, io = {}, {}
    for name in _INS:
        a = _np.ascontiguousarray(inputs[name])
        arrays[f"in_{name}_dram"] = a
        io[name] = nc.dram_tensor(f"in_{name}_dram", a.shape, _mybir.dt.from_np(a.dtype), kind="ExternalInput").ap()
    out = nc.dram_tensor("out_0_dram", (B, L, D), F32, kind="ExternalOutput").ap()
    build(nc, io, out)
    r = _run(nc, [arrays], core_ids=[0])
    return r.results[0]["out_0_dram"]
```

```python
from contextlib import ExitStack

import concourse.bass as bass
from concourse import mybir

F32 = mybir.dt.float32
F32R = mybir.dt.float32r
BF16 = mybir.dt.bfloat16
U32 = mybir.dt.uint32
ALU = mybir.AluOpType
ACT = mybir.ActivationFunctionType
X, XY = mybir.AxisListType.X, mybir.AxisListType.XY

P = 128
B, L, D = 8, 256, 256
T = B * L
NT = T // P
DC = D // P
H, DH = 16, 16
MAXLEN = 1250
NR = 2 * L - 1
BANK = 512

IB = 32
NIB = L // IB
GAM = 4
HP = H // GAM
U = HP * B
WIN = L + IB
HIGH = 0xFFFFF000


class Mem:

    sems = None

    def __init__(self, nc):
        self.nc, self.stack = nc, ExitStack()

    def __enter__(self):
        self.stack.__enter__()
        return self

    def __exit__(self, *a):
        return self.stack.__exit__(*a)

    def sb(self, name, shape, dt=F32):
        return self.stack.enter_context(self.nc.sbuf_tensor(name, shape, dt))

    def sem(self, name):
        return Mem.sems.enter_context(self.nc.semaphore(name))


def bc(ap, *shape):
    return ap.to_broadcast(list(shape))


def project_phase(nc, ps, io, keep):
    q2, k2, vt, r2, qs0, ident, ucol, vcol = (keep[n] for n in ("q2", "k2", "vt", "r2", "qs0", "ident", "ucol", "vcol"))
    NTB = T // BANK
    with Mem(nc) as m:
        x = m.sb("x_a", [P, NT, D])
        z = m.sb("z_a", [P, NT, D])
        xnT = keep["aT"][:].rearrange("p a g i -> p (a g i)").rearrange("p (c t) -> p c t", c=DC)
        w = {n: m.sb(f"w{n}", [P, DC, D]) for n in "qkvr"}
        rel = m.sb("rel", [P, 4, D])
        relT = m.sb("relT", [P, DC, BANK])
        w2 = {n: m.sb(f"w2{n}", [P, DC, HP, GAM, 2, DH]) for n in "qkr"}
        rf = m.sb("rf", [P, HP, BANK])
        rh = z[:].rearrange("p t d -> p (t d)")[:, 0:HP * BANK].rearrange("p (h r) -> p h r", h=HP)
        kh = z[:].rearrange("p t d -> p (t d)")[:, HP * BANK:HP * BANK + 2 * BANK].rearrange("p (a t) -> p a t", a=2)
        gcol, bcol = (m.sb(n, [P, DC]) for n in ("gcol", "bcol"))
        low, sign, zero = (m.sb(n, [P, 1]) for n in ("low", "sign", "project_zero"))
        mask8 = m.sb("mask8", [P, 8])
        ones8 = m.sb("ones8", [P, 8])
        st = m.sb("st", [P, NT, 6])
        mv = m.sb("mv", [P, NT, 2])
        ve = m.sb("ve", [P, NT])
        sd = m.sb("sd", [P, NT])
        rs = m.sb("rs", [P, NT])
        x_in = [m.sem(f"x_in{i}") for i in range(4)]
        rel_in, wr_in, vec_in, wqkv_in = m.sem("rel_in"), m.sem("wr_in"), m.sem("vec_in"), m.sem("wqkv_in")
        setup_step, consts_ready = m.sem("setup_step"), m.sem("consts_ready")
        norm_step, var_ready, std_ready = m.sem("norm_step"), m.sem("var_ready"), m.sem("std_ready")
        xn_ready, rel_T, rel_copied, r_done, r_kept = (m.sem(n) for n in ("xn_ready", "rel_T", "rel_copied", "r_done", "r_kept"))
        xT_done, xnT_ready, job_done = m.sem("xT_done"), m.sem("xnT_ready"), m.sem("job_done")
        kept_dve, kept_act = m.sem("kept_dve"), m.sem("kept_act")

        pad_ready, w2_ready, split_step = m.sem("pad_ready"), m.sem("w2_ready"), m.sem("split_step")

        jobs = [job for n in range(NTB * DC) for job in (("k", 2 * n), ("v", n), ("q", 2 * n), ("k", 2 * n + 1), ("q", 2 * n + 1))]
        by_dve = [sum(1 for w_, _ in jobs[:n + 1] if w_ == "k") for n in range(len(jobs))]
        by_act = [sum(1 for w_, _ in jobs[:n + 1] if w_ != "k") for n in range(len(jobs))]

        block = m.stack.enter_context(nc.Block())

        @block.sync
        def _(sp):
            xv = io["x"].rearrange("b s d -> (b s) d").rearrange("(t p) d -> p t d", p=P)
            for i in range(4):
                sp.dma_start(x[:, 4 * i:4 * i + 4], xv[:, 4 * i:4 * i + 4]).then_inc(x_in[i], 16)
            r0 = MAXLEN - (L - 1)
            rr = io["L0_attn_rel_pos_emb"]
            sp.dma_start(rel[:, 0:3], rr[r0:r0 + 3 * P].rearrange("(t p) d -> p t d", p=P)).then_inc(rel_in, 16)
            sp.dma_start(rel[0:P - 1, 3], rr[r0 + 3 * P:r0 + NR]).then_inc(rel_in, 16)
            sp.dma_start(w["r"][:], io["L0_attn_Wr"].rearrange("(c p) n -> p c n", p=P)).then_inc(wr_in, 16)
            for n in "qkv":
                sp.dma_start(w[n][:], io[f"L0_attn_W{n}"].rearrange("(c p) n -> p c n", p=P)).then_inc(wqkv_in, 16)

        @block.gpsimd
        def _(pool):
            nc.gpsimd.memset(ident[:], 0.0).then_inc(setup_step, 1)
            nc.gpsimd.memset(ones8[:], 1.0).then_inc(setup_step, 1)
            pool.wait_ge(setup_step, 2)
            nc.gpsimd.affine_select(out=ident[:], in_=ident[:], compare_op=ALU.not_equal, fill=1.0, base=0,
                                    pattern=[[-1, P]], channel_multiplier=1).then_inc(consts_ready, 1)
            nc.gpsimd.affine_select(out=ones8[:], in_=ones8[:], compare_op=ALU.is_ge, fill=0.0, base=0,
                                    pattern=[[-DH, 8]], channel_multiplier=1).then_inc(setup_step, 1)
            pool.wait_ge(setup_step, 3)
            nc.gpsimd.affine_select(out=mask8[:], in_=ones8[:], compare_op=ALU.is_ge, fill=0.0, base=DH - 1,
                                    pattern=[[DH, 8]], channel_multiplier=-1).then_inc(consts_ready, 1)
            for n, ready, at in (("r", wr_in, 16), ("k", wqkv_in, 48), ("q", wqkv_in, 48)):
                pool.wait_ge(ready, at)
                for c in range(DC):
                    src = w[n][:, c].rearrange("p (g h d) -> p h g d", g=GAM, h=HP)
                    for half in range(2):
                        nc.gpsimd.tensor_copy(w2[n][:, c, :, :, half], src).then_inc(w2_ready, 1)
            nc.gpsimd.memset(rf[:, :, NR:BANK], 0.0).then_inc(pad_ready, 1)
            nc.gpsimd.memset(zero[:], 0.0).then_inc(setup_step, 1)
            pool.wait_ge(setup_step, 4)
            flat = qs0[:].rearrange("p h s b g i -> p (h s b g i)")
            nc.gpsimd.tensor_copy(flat.bitcast(F32R), bc(zero[:], P, HP * 2 * B * GAM * IB)).then_inc(setup_step, 1)
            pool.wait_ge(setup_step, 5)

        @block.vector
        def _(dve):
            def normalize(src, dst, eps, first, turn, steps):
                for t in range(NT):
                    if first and t % 4 == 0:
                        dve.wait_ge(x_in[t // 4], 16)
                    i = nc.vector.bn_stats(st[:, t], src[:, t])
                i.then_inc(norm_step, 1)
                dve.wait_ge(norm_step, steps + 1)
                for t in range(NT):
                    i = nc.vector.bn_aggr(mv[:, t], st[:, t])
                i.then_inc(norm_step, 1)
                dve.wait_ge(norm_step, steps + 2)
                nc.vector.tensor_scalar_add(ve[:], mv[:, :, 1], eps).then_inc(var_ready, 1)
                dve.wait_ge(std_ready, turn)
                nc.vector.reciprocal(rs[:], sd[:]).then_inc(norm_step, 1)
                dve.wait_ge(norm_step, steps + 3)
                for t in range(NT):
                    i = nc.vector.tensor_scalar(dst[:, t], src[:, t], mv[:, t, 0:1], rs[:, t:t + 1], ALU.subtract, ALU.mult)
                    if not first:
                        i.then_inc(xn_ready, 1)
                if first:
                    i.then_inc(norm_step, 1)
                    dve.wait_ge(norm_step, steps + 4)

            normalize(x, z, 1e-5, True, 1, 0)
            normalize(z, x, 1e-6, False, 2, 4)
            link = Chain(dve, split_step)
            dve.wait_ge(consts_ready, 2)
            link(nc.vector.tensor_reduce(low[:], mask8[:, 1:8:2], X, ALU.add))
            link(nc.vector.tensor_scalar(sign[:], low[:], -2.0, 1.0, ALU.mult, ALU.add))
            dve.wait_ge(r_kept, HP)
            dve.wait_ge(pad_ready, 1)
            parts, full = rh, rf[:]
            link(nc.vector.tensor_single_scalar(parts.bitcast(U32), full.bitcast(U32), HIGH, op=ALU.bitwise_and))
            link(nc.vector.tensor_scalar(parts, parts, sign[:], None, ALU.mult))
            nc.vector.scalar_tensor_tensor(out=r2[:].bitcast(F32R), in0=full, scalar=low[:], in1=parts, op0=ALU.mult, op1=ALU.add)
            for n, (what, i) in enumerate(jobs):
                if what != "k":
                    continue
                dve.wait_ge(job_done, n + 1)
                bank, upper = ps[n % 4], kh[:, i % 2]
                tb, hp = divmod(i, HP)
                link(nc.vector.tensor_single_scalar(upper.bitcast(U32), bank[:].bitcast(U32), HIGH, op=ALU.bitwise_and))
                link(nc.vector.tensor_scalar(upper, upper, sign[:], None, ALU.mult))
                nc.vector.scalar_tensor_tensor(out=k2[:, hp, tb * BANK:(tb + 1) * BANK].bitcast(F32R), in0=bank[:], scalar=low[:], in1=upper,
                                               op0=ALU.mult, op1=ALU.add).then_inc(kept_dve, 1)

        @block.scalar
        def _(act):
            with nc.allow_non_contiguous_dma(reason="a few columns"):
                act.dma_start(gcol[:], io["L0_attn_gamma"].rearrange("(c p) -> p c", p=P)).then_inc(vec_in, 16)
                act.dma_start(bcol[:], io["L0_attn_beta"].rearrange("(c p) -> p c", p=P)).then_inc(vec_in, 16)
                for g in range(GAM):
                    for half in range(2):
                        for col, b in ((ucol, "u"), (vcol, "v")):
                            act.dma_start(col[32 * g + DH * half:32 * g + DH * (half + 1)],
                                          io[f"L0_attn_{b}_bias"][g * HP:(g + 1) * HP].rearrange("h d -> d h")).then_inc(vec_in, 16)
            for c in range(DC):
                act.wait_ge(rel_T, c + 1)
                nc.scalar.activation(relT[:, c, 0:NR], ps[c][:, 0:NR], ACT.Copy).then_inc(rel_copied, 1)
            act.wait_ge(var_ready, 1)
            nc.scalar.activation(sd[:], ve[:], ACT.Sqrt).then_inc(std_ready, 1)
            for hp in range(HP):
                act.wait_ge(r_done, hp + 1)
                nc.scalar.activation(rf[:, hp, 0:NR], ps[2 + hp % 2][:, 0:NR], ACT.Copy).then_inc(r_kept, 1)
            act.wait_ge(var_ready, 2)
            nc.scalar.activation(sd[:], ve[:], ACT.Sqrt).then_inc(std_ready, 1)
            act.wait_ge(vec_in, 16 * (2 + 4 * GAM))
            for n in range(NTB * DC):
                tb, c = divmod(n, DC)
                act.wait_ge(xT_done, n + 1)
                nc.scalar.activation(xnT[:, c, tb * BANK:(tb + 1) * BANK], ps[4 + n % 4][:], ACT.Identity,
                                     bias=bcol[:, c:c + 1], scale=gcol[:, c:c + 1]).then_inc(xnT_ready, 1)
            for n, (what, i) in enumerate(jobs):
                if what == "k":
                    continue
                act.wait_ge(job_done, n + 1)
                bank = ps[n % 4]
                if what == "v":
                    nc.scalar.activation(vt[:, 2 * i:2 * i + 2], bank[:].rearrange("p (t d) -> p t d", t=2), ACT.Copy).then_inc(kept_act, 1)
                else:
                    tb, hp = divmod(i, HP)
                    nc.scalar.activation(q2[:, hp, tb * BANK:(tb + 1) * BANK], bank[:], ACT.Copy).then_inc(kept_act, 1)

        @block.tensor
        def _(pe):
            pe.wait_ge(consts_ready, 2)
            pe.wait_ge(rel_in, 32)
            for c in range(DC):
                for t in range(4):
                    n = P if t < 3 else P - 1
                    i = nc.tensor.transpose(ps[c][:, t * P:t * P + n], rel[0:n, t, c * P:(c + 1) * P], ident[0:n, 0:n])
                i.then_inc(rel_T, 1)
            pe.wait_ge(rel_copied, DC)
            pe.wait_ge(w2_ready, 2 * DC)
            for hp in range(HP):
                if hp >= 2:
                    pe.wait_ge(r_kept, hp - 1)
                for c in range(DC):
                    i = nc.tensor.matmul(ps[2 + hp % 2][:, 0:NR], w2["r"][:, c, hp].rearrange("p g s d -> p (g s d)"), relT[:, c, 0:NR],
                                         start=c == 0, stop=c == DC - 1)
                i.then_inc(r_done, 1)
            for n in range(NTB * DC):
                tb, c = divmod(n, DC)
                if n >= 4:
                    pe.wait_ge(xnT_ready, n - 3)
                for t in range(4):
                    if c == 0:
                        pe.wait_ge(xn_ready, 4 * tb + t + 1)
                    i = nc.tensor.transpose(ps[4 + n % 4][:, t * P:(t + 1) * P], x[:, 4 * tb + t, c * P:(c + 1) * P], ident[:])
                i.then_inc(xT_done, 1)
            pe.wait_ge(wqkv_in, 48)
            pe.wait_ge(w2_ready, 6 * DC)
            pe.wait_ge(r_kept, HP)
            for n, (what, i) in enumerate(jobs):
                if n >= 4:
                    pe.wait_ge(kept_dve, by_dve[n - 4])
                    pe.wait_ge(kept_act, by_act[n - 4])
                pe.wait_ge(xnT_ready, DC * (i // (DC if what == "v" else HP) + 1))
                bank = ps[n % 4]
                if what == "v":
                    for t in range(2):
                        for c in range(DC):
                            tile = 2 * i + t
                            j = nc.tensor.matmul(bank[:, t * D:(t + 1) * D], xnT[:, c, tile * P:(tile + 1) * P], w["v"][:, c],
                                                 start=c == 0, stop=c == DC - 1)
                else:
                    tb, hp = divmod(i, HP)
                    for c in range(DC):
                        j = nc.tensor.matmul(bank[:], w2[what][:, c, hp].rearrange("p g s d -> p (g s d)"), xnT[:, c, tb * BANK:(tb + 1) * BANK],
                                             start=c == 0, stop=c == DC - 1)
                j.then_inc(job_done, 1)


def attention_phase(nc, ps, io, keep):
    q2, k2, vt, r2, qs0, ident, ucol, vcol, aT = (keep[n] for n in ("q2", "k2", "vt", "r2", "qs0", "ident", "ucol", "vcol", "aT"))
    LEAD = 12
    CH = 2
    RING = 4
    ROW = CH * WIN + IB
    NORM = 8, 12
    LATE_BIAS, LATE_UPPER, LATE_LOWER = 2, 5, 7
    LT, LV, LO = 3, 6, 13
    pos = nc.dram_tensor("position_scores", [RING, P * ROW], F32).ap()
    with Mem(nc) as m:
        bds = m.sb("bds", [P, RING, CH, L])
        bdp = m.sb("bdp", [P, 2, CH * WIN])
        qs = [qs0, m.sb("qs1", [P, HP, 2, B, GAM, IB])]
        qt, high = m.sb("qt", [P, 2, B, IB]), m.sb("high", [P, 2, B, IB])
        zero = m.sb("attention_zero", [P, 1])
        sc = m.sb("sc", [P, 4, L])
        pr = m.sb("pr", [P, 8, L])
        prT = m.sb("prT", [P, 4, BANK])
        nmax = m.sb("nmax", [P, U])
        rsum = m.sb("rsum", [P, U])
        rinv = m.sb("rinv", [P, U])
        osb = m.sb("osb", [P, B, HP, DH])
        ac_banks, bd_banks, pt_banks, o_banks = ps[0:2], ps[2:4], ps[4:6], ps[6:8]

        qt_ready, high_ready, split_ready, placed = m.sem("qt_ready"), m.sem("high_ready"), m.sem("split_ready"), m.sem("placed")
        ac_done, s_done, exp_done = m.sem("ac_done"), m.sem("s_done"), m.sem("exp_done")
        bd_done, bd_kept = m.sem("bd_done"), m.sem("bd_kept")
        pos_out = [m.sem(f"pos_out{i}") for i in range(RING)]
        pos_in = [m.sem(f"pos_in{i}") for i in range(RING)]
        pt_done, pt_kept, pv_done = m.sem("pt_done"), m.sem("pt_kept"), m.sem("pv_done")
        rinv_step, o_kept, ot_done, ot_kept = m.sem("rinv_step"), m.sem("o_kept"), m.sem("ot_done"), m.sem("ot_kept")

        NC = U // CH
        TURNS = NC // RING

        def place(ib, s, shift):
            s += shift
            ib, s = (ib - 1, s + U) if s < 0 else (ib + 1, s - U) if s >= U else (ib, s)
            return None if isinstance(ib, int) and not 0 <= ib < NIB else (ib, s)

        def past(ib, n):
            return not isinstance(ib, int) or ib >= n

        def order(group):
            ib, hp, kind = group
            return 2 * HP * ib + 2 * hp + kind

        def groups_of_step(ib, s, late):
            if isinstance(ib, int) and ib == 0 and s < 4:
                return [(0, 2 + s // 2, s % 2)]
            t = place(ib, s, -late)
            if t is None or t[1] % 4 or (isinstance(t[0], int) and t == (0, 0)):
                return []
            at = place(*t, U - 8 if t[1] % 8 == 0 else U - 4)
            return [(at[0], at[1] // B, int(t[1] % 8 == 0))] if at else []

        def placings(group):
            n = order(group)
            return n + 2 + (min((n + 1) // 2, HP) if isinstance(n, int) else HP)

        FIRST = [(0, hp, kind) for hp in range(2) for kind in range(2)]
        BY_DVE = [(0, 0, 1)]

        def block_queries(ap, ib):
            return ap.rearrange("p (b i) -> p b i", b=B)[:, :, bass.ds(IB * ib, IB)]

        def run_turns(eng, step):
            for s in range(U):
                step(0, s, True)
            with eng.Fori(1, NIB - 1) as ib:
                for s in range(U):
                    step(ib, s, True)
            for s in range(U):
                step(NIB - 1, s, True)
            for s in range(LO):
                step(NIB, s, False)

        block = m.stack.enter_context(nc.Block())

        @block.sync
        def _(sp):
            def send(ib, c):
                slot, turn = c % RING, TURNS * ib + c // RING
                sp.wait_ge(bd_kept, U * ib + CH * (c + 1))
                sp.nop(nofuse=True)
                if c >= RING or past(ib, 1):
                    sp.wait_ge(pos_in[slot], 16 * turn)
                    sp.nop(nofuse=True)
                sp.dma_start(bass.AP(pos.tensor, slot * P * ROW, [[IB * (ROW - 1), GAM], [ROW, IB], [1, CH * WIN]]),
                             bdp[:, c % 2]).then_inc(pos_out[slot], 16)

            def fetch(ib, c):
                slot, turn = c % RING, TURNS * ib + c // RING
                sp.wait_ge(pos_out[slot], 16 * turn + 16)
                sp.nop(nofuse=True)
                if c >= RING or past(ib, 1):
                    sp.wait_ge(s_done, U * ib + CH * (c + 1 - RING))
                    sp.nop(nofuse=True)
                sp.dma_start(bds[:, slot], bass.AP(pos.tensor, slot * P * ROW + IB - 1, [[ROW - 1, P], [WIN, CH], [1, L]])
                             ).then_inc(pos_in[slot], 16)

            send(0, 0)
            for c in range(1, NC):
                send(0, c)
                fetch(0, c - 1)
            with sp.Fori(1, NIB) as ib:
                for c in range(NC):
                    send(ib, c)
                    fetch(ib if c else ib - 1, (c - 1) % NC)
            fetch(NIB - 1, NC - 1)

        @block.gpsimd
        def _(pool):
            def lower_bits(group):
                ib, hp, kind = group
                n = order(group)
                pool.wait_ge(high_ready, n + 1)
                for g in range(GAM):
                    if g or past(ib, 1) or n:
                        pool.wait_ge(split_ready, GAM * n + g)
                    pool.nop(nofuse=True)
                    rows = slice(g * IB, (g + 1) * IB)
                    nc.gpsimd.tensor_tensor(out=qs[kind][rows, hp, 1, :, g].bitcast(F32R), in0=qt[rows, kind], in1=high[rows, kind], op=ALU.subtract
                                            ).then_inc(split_ready, 1)

            for hp in range(HP):
                for kind in range(2):
                    if (0, hp, kind) not in BY_DVE:
                        lower_bits((0, hp, kind))
            with pool.Fori(1, NIB) as ib:
                for hp in range(HP):
                    for kind in range(2):
                        lower_bits((ib, hp, kind))

        @block.vector
        def _(dve):
            def place_upper_bits(group, half):
                ib, hp, kind = group
                for g in (2 * half, 2 * half + 1):
                    rows = slice(g * IB, (g + 1) * IB)
                    i = nc.vector.tensor_copy(qs[kind][rows, hp, 0, :, g].bitcast(F32R), high[rows, kind])
                if half:
                    i.then_inc(placed, 1)

            def upper_bits(group):
                ib, hp, kind = group
                n = order(group)
                if kind and isinstance(ib, int) and ib == 0:
                    dve.wait_ge(placed, placings(group) - 2)
                    nc.vector.tensor_copy(qs[1][:, hp].rearrange("p s b g i -> p (s b g i)").bitcast(F32R),
                                          bc(zero[:], P, 2 * B * GAM * IB)).then_inc(placed, 1)
                    dve.wait_ge(placed, placings(group) - 1)
                dve.wait_ge(qt_ready, n + 1)
                if past(ib, 1):
                    dve.wait_ge((bd_done, ac_done)[kind], U * (ib - 1) + (hp + 1) * B)
                dve.nop(nofuse=True)
                nc.vector.tensor_single_scalar(high[:, kind].bitcast(U32), qt[:, kind].bitcast(U32), HIGH, op=ALU.bitwise_and).then_inc(high_ready, 1)
                dve.wait_ge(high_ready, n + 1)
                dve.nop(nofuse=True)
                place_upper_bits(group, 0)

            nc.vector.memset(zero[:], 0.0).then_inc(placed, 1)
            for group in FIRST:
                upper_bits(group)
                place_upper_bits(group, 1)
                if group in BY_DVE:
                    _, hp, kind = group
                    dve.wait_ge(split_ready, GAM * order(group))
                    for g in range(GAM):
                        rows = slice(g * IB, (g + 1) * IB)
                        nc.vector.tensor_tensor(out=qs[kind][rows, hp, 1, :, g].bitcast(F32R), in0=qt[rows, kind], in1=high[rows, kind],
                                                op=ALU.subtract).then_inc(split_ready, 1)

            def step(ib, s, scores):
                if scores:
                    c = s // CH
                    if s % CH == 0:
                        dve.wait_ge(pos_in[c % RING], 16 * (TURNS * ib + c // RING + 1))
                    dve.wait_ge(ac_done, U * ib + s + 1)
                    if s >= 4 or past(ib, 1):
                        dve.wait_ge(exp_done, U * ib + s - 3)
                    dve.nop(nofuse=True)
                    nc.vector.tensor_tensor_reduce(
                        out=sc[:, s % 4], in0=ac_banks[s % 2][:, 0:L], in1=bds[:, c % RING, s % CH],
                        scale=-1.0 / DH ** 0.5, scalar=3.0e38, op0=ALU.add, op1=ALU.min,
                        accum_out=nmax[:, s:s + 1]).then_inc(s_done, 1)
                    for group in groups_of_step(ib, s, LATE_UPPER):
                        upper_bits(group)
                    for group in groups_of_step(ib, s, LATE_LOWER):
                        place_upper_bits(group, 1)
                t = place(ib, s, -LT)
                if t and t[1] % 2:
                    tb, pair = t[0], t[1] // 2
                    dve.wait_ge(pt_done, U // 2 * tb + pair + 1)
                    if pair >= 4 or past(tb, 1):
                        dve.wait_ge(pv_done, U // 2 * tb + pair - 3)
                    nc.vector.tensor_copy(prT[:, pair % 4], pt_banks[pair % 2][:]).then_inc(pt_kept, 1)
                for half, lag in enumerate(NORM):
                    t = place(ib, s, -lag)
                    if t and t[1] % B == B - 1:
                        tb, hp = t[0], t[1] // B
                        part = slice(hp * B, (hp + 1) * B)
                        if half == 0:
                            dve.wait_ge(exp_done, U * tb + t[1] + 1)
                            nc.vector.reciprocal(rinv[:, part], rsum[:, part]).then_inc(rinv_step, 1)
                            dve.wait_ge(rinv_step, HP * tb + hp + 1)
                            dve.wait_ge(pv_done, U // 2 * tb + (t[1] + 1) // 2)
                            if hp == 0 and past(tb, 1):
                                dve.wait_ge(ot_done, tb)
                        bank = o_banks[hp % 2][:].rearrange("p (b g d) -> p b g d", b=B, g=GAM)
                        for g in (2 * half, 2 * half + 1):
                            rows = slice(g * IB, (g + 1) * IB)
                            i = nc.vector.tensor_tensor(out=osb[rows, :, hp], in0=bank[rows, :, g],
                                                        in1=bc(rinv[rows, part].unsqueeze(2), IB, B, DH), op=ALU.mult)
                        if half:
                            i.then_inc(o_kept, 1)

            run_turns(dve, step)

        @block.scalar
        def _(act):
            def keep_positions(ib, s):
                c = s // CH
                act.wait_ge(bd_done, U * ib + s + 1)
                if s % CH == 0 and (c >= 2 or past(ib, 1)):
                    act.wait_ge(pos_out[(c - 2) % RING], 16 * (TURNS * ib + (c - 2) // RING + 1))
                nc.scalar.activation(bdp[:, c % 2, s % CH * WIN:(s % CH + 1) * WIN], bd_banks[s % 2][:, 0:WIN], ACT.Copy).then_inc(bd_kept, 1)

            def add_bias(group):
                ib, hp, kind = group
                if past(ib, 1) or order(group) > 1:
                    act.wait_ge(split_ready, GAM * order(group) - GAM)
                    act.nop(nofuse=True)
                nc.scalar.activation(qt[:, kind], block_queries(q2[:, hp], ib), ACT.Identity, bias=(vcol, ucol)[kind][:, hp:hp + 1]).then_inc(qt_ready, 1)

            def step(ib, s, scores):
                if scores:
                    for group in groups_of_step(ib, s, LATE_BIAS):
                        add_bias(group)
                    act.wait_ge(s_done, U * ib + s + 1)
                    if s % 2 == 0 and (s >= 8 or past(ib, 1)):
                        act.wait_ge(pt_done, U // 2 * ib + s // 2 - 3)
                    nc.scalar.activation(pr[:, s % 8], sc[:, s % 4], ACT.Exp, bias=nmax[:, s:s + 1], scale=-1.0,
                                         accum_out=rsum[:, s:s + 1]).then_inc(exp_done, 1)
                    if place(ib, s, LEAD):
                        keep_positions(*place(ib, s, LEAD))
                if s == LO - 1 and past(ib, 1):
                    act.wait_ge(ot_done, ib)
                    nc.scalar.activation(aT[:, :, :, bass.ds(IB * ib - IB, IB)], o_banks[1][:].rearrange("p (a g i) -> p a g i", a=B // 2, g=GAM),
                                         ACT.Copy).then_inc(ot_kept, 1)

            for n, group in enumerate(FIRST):
                add_bias(group)
            for s in range(LEAD):
                keep_positions(0, s)
            run_turns(act, step)

        @block.tensor
        def _(pe):
            def position_scores(ib, s):
                hp, b = divmod(s, B)
                if b == 0:
                    pe.wait_ge(placed, placings((ib, hp, 0)))
                    pe.wait_ge(split_ready, GAM * order((ib, hp, 0)) + GAM)
                if s >= 2 or past(ib, 1):
                    pe.wait_ge(bd_kept, U * ib + s - 1)
                pe.nop(nofuse=True)
                for part in range(2):
                    i = nc.tensor.matmul(bd_banks[s % 2][:, 0:WIN], qs[0][:, hp, part, b].rearrange("p g i -> p (g i)").bitcast(F32R),
                                         r2[:, hp, bass.ds(L - IB - IB * ib, WIN)].bitcast(F32R), start=part == 0, stop=part == 1)
                i.then_inc(bd_done, 1)

            def content_scores(ib, s):
                hp, b = divmod(s, B)
                if b == 0:
                    pe.wait_ge(placed, placings((ib, hp, 1)))
                    pe.wait_ge(split_ready, GAM * order((ib, hp, 1)) + GAM)
                if s >= 2 or past(ib, 1):
                    pe.wait_ge(s_done, U * ib + s - 1)
                for part in range(2):
                    i = nc.tensor.matmul(ac_banks[s % 2][:, 0:L], qs[1][:, hp, part, b].rearrange("p g i -> p (g i)").bitcast(F32R),
                                         k2[:, hp, b * L:(b + 1) * L].bitcast(F32R), start=part == 0, stop=part == 1)
                i.then_inc(ac_done, 1)

            def transposes(ib, s):
                pe.wait_ge(exp_done, U * ib + s + 1)
                if s % 2 == 0 and (s >= 4 or past(ib, 1)):
                    pe.wait_ge(pt_kept, U // 2 * ib + s // 2 - 1)
                for jc in range(2):
                    i = nc.tensor.transpose(pt_banks[s // 2 % 2][:, s % 2 * L + jc * P:s % 2 * L + (jc + 1) * P],
                                            pr[:, s % 8, jc * P:(jc + 1) * P], ident[:])
                if s % 2:
                    i.then_inc(pt_done, 1)

            def values(ib, s):
                hp, b = divmod(s, B)
                if s % 2 == 0:
                    pe.wait_ge(pt_kept, U // 2 * ib + s // 2 + 1)
                if b == 0 and (hp >= 2 or past(ib, 1)):
                    if hp == 1:
                        pe.wait_ge(ot_kept, ib)
                    else:
                        pe.wait_ge(o_kept, HP * ib + hp - 1)
                for jc in range(2):
                    v = vt[:, 2 * b + jc].rearrange("p (g h d) -> p g h d", g=GAM, h=HP)[:, :, hp]
                    i = nc.tensor.matmul(o_banks[hp % 2][:, b * 64:(b + 1) * 64],
                                         prT[:, s // 2 % 4, s % 2 * L + jc * P:s % 2 * L + (jc + 1) * P], v,
                                         start=jc == 0, stop=jc == 1)
                if s % 2:
                    i.then_inc(pv_done, 1)

            def step(ib, s, scores):
                if scores:
                    content_scores(ib, s)
                    if place(ib, s, LEAD):
                        position_scores(*place(ib, s, LEAD))
                if place(ib, s, -LT):
                    transposes(*place(ib, s, -LT))
                if place(ib, s, -LV):
                    values(*place(ib, s, -LV))
                if s == LO - 1 and past(ib, 1):
                    pe.wait_ge(o_kept, HP * ib)
                    for a in range(B // 2):
                        i = nc.tensor.transpose(o_banks[1][:, a * P:(a + 1) * P], osb[:, 2 * a:2 * a + 2].rearrange("p b h d -> p (b h d)"), ident[:])
                    i.then_inc(ot_done, 1)

            for s in range(LEAD):
                position_scores(0, s)
            run_turns(pe, step)


MAGIC = 12582912.0
XW = ("d2v", "img", "txt", "att0", "att1", "f1", "f2")
XSHAPE = {"d2v": (256, 192), "img": (256, 256), "txt": (256, 256), "att0": (128, 256), "att1": (128, 256),
          "f1": (1024, 512), "f2": (256, 1024)}
RMAX = bass.bass_isa.ReduceOp.max
RADD = bass.bass_isa.ReduceOp.add


def chunks(n):
    return [(i, min(P, n - i)) for i in range(0, n, P)]


class Chain:

    def __init__(self, eng, sem):
        self.eng, self.sem, self.n = eng, sem, 0

    def __call__(self, ins):
        self.n += 1
        ins.then_inc(self.sem, 1)
        self.eng.wait_ge(self.sem, self.n)


def activation_scale(nc, link, am, isc, inv):
    link(nc.vector.tensor_scalar(isc, am, 1e-8, 1.0 / 127.0, ALU.max, ALU.mult))
    link(nc.vector.reciprocal(inv, isc))


def context_phase(nc, ps, io, keep):
    ident, qwT, ws, bias = keep["ident"], keep["qwT"], keep["ws"], keep["bias"]
    kvT, kvt, avg = keep["kvT"], keep["kvt"], keep["avg"]
    aT, x1 = keep["aT"], keep["x1"]
    NB = 4
    CW = 192
    NTB = T // BANK
    with Mem(nc) as m:
        wo = m.sb("wo", [P, GAM, D])
        bo = m.sb("bo", [P, D])
        wo_in, x_in = m.sem("wo_in"), m.sem("x1_in")
        y_done, xb_done, x1_done = m.sem("y_done"), m.sem("xb_done"), m.sem("x1_done")
        raw = {n: m.sb(f"raw_{n}", [P, XSHAPE[n][0] // P, XSHAPE[n][1]]) for n in XW}
        qn = {n: m.sb(f"qn_{n}", [P, XSHAPE[n][0] // P, XSHAPE[n][1]], BF16) for n in XW}
        identb = m.sb("identb", [P, P], BF16)
        cx = m.sb("cx", [P, NT, CW])
        cq = m.sb("cq", [P, NT, CW], BF16)
        cqT = m.sb("cqT", [P, 2, T], BF16)
        act_f = {"vis": m.sb("vis", [P, DC, T]), "img": m.sb("img", [P, DC, T])}
        act_q = m.sb("act_q", [P, DC, T], BF16)
        junk = act_q[:].rearrange("p c t -> p (c t)")
        sums, cnt, thr, nthr = (m.sb(n, [P, len(XW)]) for n in ("sums", "cnt", "thr", "nthr"))
        part = m.sb("part", [P, 8])
        loc, am, isc, inv = (m.sb(n, [P, 3]) for n in ("loc", "am", "isc", "inv"))
        sc = m.sb("sc_d", [P, 4])
        small_in = m.sem("w_in_small")
        w_in = {n: small_in if n in ("img", "txt", "att0", "att1") else m.sem(f"w_in_{n}") for n in XW}
        cx_in, bias_in = m.sem("cx_in"), m.sem("bias_in")
        dve_step, pool_step, cnt_ready, abs_summed, sums_ready, idb_ready = (
            m.sem(n) for n in ("dve_step", "pool_step", "cnt_ready", "abs_summed", "sums_ready", "idb_ready"))
        w_quant, loc_ready, am_ready, scale_ready = (m.sem(n) for n in ("w_quant", "loc_ready", "am_ready", "scale_ready"))
        c_quant, a_quant = m.sem("c_quant"), {n: m.sem(f"quant_{n}") for n in ("vis", "img")}
        bank_done, bank_kept = m.sem("bank_done"), m.sem("bank_kept")

        WB = {"d2v": 1, "img": 1, "txt": 1, "att0": 1, "att1": 1, "f1": 4, "f2": 2}
        J = {}
        n = 0
        J["d2v"] = n; n += 1
        J["ctx"] = n; n += 4
        J["vis"] = n; n += 8
        J["img"] = n; n += 1
        J["image"] = n; n += 8
        for w in ("att0", "att1"):
            J[w] = n; n += 1
        J["kv"] = n; n += 8
        J["kvt"] = n; n += 8
        for w in ("txt", "f1", "f2"):
            J[w] = n; n += WB[w]
        NJ = n
        block = m.stack.enter_context(nc.Block())

        @block.sync
        def _(sp):
            for half in range(2):
                sp.dma_start(wo[64 * half:64 * half + 64], io["L0_attn_Wo"].rearrange("(g q) n -> q g n", g=GAM)).then_inc(wo_in, 16)
            sp.dma_start(x1[:], io["x"].rearrange("b s d -> (b s) d").rearrange("(t p) d -> p t d", p=P)).then_inc(x_in, 16)
            sp.dma_start(bo[:], bc(io["L0_attn_bo"].unsqueeze(0), P, D)).then_inc(x_in, 16)
            for w in XW:
                if w == "img":
                    sp.dma_start(cx[:], io["ctx_768"].rearrange("b s d -> (b s) d").rearrange("(t p) d -> p t d", p=P)).then_inc(cx_in, 16)
                sp.dma_start(raw[w][:], io[f"L0_xattn_W_{w}"].rearrange("(c p) n -> p c n", p=P)).then_inc(w_in[w], 16)

        @block.gpsimd
        def _(pool):
            with nc.allow_non_contiguous_dma(reason="bias columns"):
                for w in XW:
                    pool.dma_start(bias[w][:], io[f"L0_xattn_b_{w}"].rearrange("(c p) -> p c", p=P)).then_inc(bias_in, 16)
            nc.gpsimd.tensor_copy(identb[:], ident[:]).then_inc(idb_ready, 1)
            for k, w in enumerate(XW):
                i = nc.gpsimd.memset(cnt[:, k:k + 1], 1.0 / (XSHAPE[w][0] * XSHAPE[w][1]))
            i.then_inc(cnt_ready, 1)
            pool.wait_ge(x_in, 32)
            for t in range(0, NT, 2):
                nc.gpsimd.tensor_tensor(out=x1[:, t:t + 2], in0=x1[:, t:t + 2], in1=bc(bo[:].unsqueeze(1), P, 2, D), op=ALU.add).then_inc(xb_done, 1)
            pool.wait_ge(abs_summed, len(XW))
            nc.gpsimd.partition_all_reduce(thr[:], sums[:], P, RADD).then_inc(sums_ready, 1)
            for a in range(3):
                pool.wait_ge(loc_ready, a + 1)
                nc.gpsimd.partition_all_reduce(am[:, a:a + 1], loc[:, a:a + 1], P, RMAX).then_inc(am_ready, 1)
            pool.wait_ge(bias_in, 16 * len(XW))

        @block.vector
        def _(dve):
            link = Chain(dve, dve_step)

            def keep_rows(pairs):
                for k in pairs:
                    dve.wait_ge(xb_done, k + 1)
                    dve.wait_ge(y_done, k + 1)
                    nc.vector.tensor_tensor(out=x1[:, 2 * k:2 * k + 2], in0=ps[NB + k % 4][:].rearrange("p (t d) -> p t d", t=2),
                                            in1=x1[:, 2 * k:2 * k + 2], op=ALU.add).then_inc(x1_done, 1)

            def row_stats(pairs):
                for k in pairs:
                    dve.wait_ge(x1_done, k + 1)
                    for t in (2 * k, 2 * k + 1):
                        i = nc.vector.bn_stats(keep["stats"][:, t], x1[:, t])
                return i

            dve.wait_ge(cx_in, 16)
            nc.vector.tensor_reduce(loc[:, 0:1], cx[:].rearrange("p t d -> p (t d)"), X, ALU.max, apply_absolute_value=True).then_inc(loc_ready, 1)
            keep_rows((0, 1, 2))
            dve.wait_ge(sums_ready, 1)
            dve.wait_ge(cnt_ready, 1)
            link(nc.vector.tensor_tensor(out=ws[:], in0=thr[:], in1=cnt[:], op=ALU.mult))
            link(nc.vector.tensor_scalar_max(ws[:], ws[:], 1e-5))
            link(nc.vector.tensor_scalar_mul(thr[:], ws[:], 0.5))
            link(nc.vector.tensor_scalar_mul(nthr[:], ws[:], -0.5))

            def ternary(w):
                k = XW.index(w)
                link(nc.vector.tensor_scalar(qn[w][:], raw[w][:], nthr[:, k:k + 1], None, ALU.is_lt))
                nc.vector.scalar_tensor_tensor(out=qn[w][:], in0=raw[w][:], scalar=thr[:, k:k + 1], in1=qn[w][:],
                                               op0=ALU.is_gt, op1=ALU.subtract).then_inc(w_quant, 1)

            ternary("d2v")
            row_stats((0, 1, 2))
            keep_rows((3,))
            dve.wait_ge(am_ready, 1)
            activation_scale(nc, link, am[:, 0:1], isc[:, 0:1], inv[:, 0:1])
            nc.vector.tensor_tensor(out=sc[:, 0:1], in0=isc[:, 0:1], in1=ws[:, 0:1], op=ALU.mult).then_inc(scale_ready, 1)
            for g in range(2):
                tiles = slice(8 * g, 8 * g + 8)
                link(nc.vector.tensor_scalar(cx[:, tiles], cx[:, tiles], inv[:, 0:1], MAGIC, ALU.mult, ALU.add))
                nc.vector.tensor_scalar(cq[:, tiles], cx[:, tiles], MAGIC, None, ALU.subtract).then_inc(c_quant, 1)
            ternary("img")
            keep_rows((4,))
            row_stats((3,))

            def measure(a, name, j0):
                for tb in range(NTB):
                    for oc in range(DC):
                        dve.wait_ge(bank_kept, J[j0] + tb * DC + oc + 1)
                        i = nc.vector.tensor_reduce(part[:, tb * DC + oc:tb * DC + oc + 1], act_f[name][:, oc, tb * BANK:(tb + 1) * BANK],
                                                    X, ALU.max, apply_absolute_value=True)
                link(i)
                nc.vector.tensor_reduce(loc[:, a:a + 1], part[:], X, ALU.max).then_inc(loc_ready, 1)

            def quantize(a, name):
                src = act_f[name]
                for tb in range(NTB):
                    cols = slice(tb * BANK, (tb + 1) * BANK)
                    link(nc.vector.tensor_scalar(src[:, :, cols], src[:, :, cols], inv[:, a:a + 1], MAGIC, ALU.mult, ALU.add))
                    nc.vector.tensor_scalar(act_q[:, :, cols], src[:, :, cols], MAGIC, None, ALU.subtract).then_inc(a_quant[name], 1)

            measure(1, "vis", "vis")
            ternary("att0")
            ternary("att1")
            row_stats((4,))
            keep_rows((5,))
            dve.wait_ge(am_ready, 2)
            activation_scale(nc, link, am[:, 1:2], isc[:, 1:2], inv[:, 1:2])
            nc.vector.tensor_tensor(out=sc[:, 1:2], in0=isc[:, 1:2], in1=ws[:, 1:2], op=ALU.mult).then_inc(scale_ready, 1)
            quantize(1, "vis")
            keep_rows((6,))
            row_stats((5,))
            measure(2, "img", "image")
            link(nc.vector.reduce_sum(avg[:], act_f["img"][:].rearrange("p c (b s) -> p c b s", b=B), X))
            nc.vector.tensor_scalar_mul(avg[:], avg[:], 1.0 / L)
            row_stats((6,))
            keep_rows((7,))
            dve.wait_ge(am_ready, 3)
            activation_scale(nc, link, am[:, 2:3], isc[:, 2:3], inv[:, 2:3])
            nc.vector.tensor_scalar(sc[:, 2:4], ws[:, 3:5], isc[:, 2:3], None, ALU.mult).then_inc(scale_ready, 1)
            dve.wait_ge(bank_kept, J["image"] + 8)
            dve.wait_ge(bank_done, J["image"] + 8)
            quantize(2, "img")
            ternary("txt")
            row_stats((7,))
            ternary("f1")
            ternary("f2")

        def keep_weight(w):
            rows, cols = XSHAPE[w]
            blocks = [(ic, oc) for ic in range(len(chunks(cols))) for oc in range(rows // P)]
            per = -(-len(blocks) // WB[w])
            return [blocks[i:i + per] for i in range(0, len(blocks), per)]

        @block.scalar
        def _(act):
            for k, w in enumerate(XW):
                act.wait_ge(w_in[w], 64 if w_in[w] is small_in else 16)
                n = XSHAPE[w][0] // P * XSHAPE[w][1]
                if k:
                    act.wait_ge(abs_summed, k)
                nc.scalar.activation(junk[:, 0:n], raw[w][:].rearrange("p c n -> p (c n)"), ACT.Abs,
                                     accum_out=sums[:, k:k + 1]).then_inc(abs_summed, 1)
            act.wait_ge(bias_in, 16 * len(XW))

            def weight(w):
                for q, blocks in enumerate(keep_weight(w)):
                    j = J[w] + q
                    act.wait_ge(bank_done, j + 1)
                    (i0, o0) = blocks[0]
                    bank = ps[j % NB][:].bitcast(BF16)
                    rows = min(c[1] for c in chunks(XSHAPE[w][1]))
                    if rows == P:
                        o = qwT[w][:].rearrange("p i n -> p (i n)")
                        s = (i0 * (XSHAPE[w][0] // P) + o0) * P
                        nc.scalar.activation(o[:, s:s + len(blocks) * P], bank[:, 0:len(blocks) * P], ACT.Copy).then_inc(bank_kept, 1)
                    else:
                        half = len(blocks) // 2 * P
                        nc.scalar.activation(qwT[w][:, 0], bank[:, 0:half], ACT.Copy)
                        nc.scalar.activation(qwT[w][0:rows, 1], bank[0:rows, half:2 * half], ACT.Copy).then_inc(bank_kept, 1)

            weight("d2v")
            for c, (c0, cn) in enumerate(chunks(CW)):
                for g in range(2):
                    j = J["ctx"] + 2 * c + g
                    act.wait_ge(bank_done, j + 1)
                    nc.scalar.activation(cqT[0:cn, c, g * 1024:(g + 1) * 1024], ps[j % NB][0:cn, :].bitcast(BF16), ACT.Copy).then_inc(bank_kept, 1)

            def linear(j0, a, out, w):
                act.wait_ge(scale_ready, a + 1)
                for tb in range(NTB):
                    for oc in range(DC):
                        j = J[j0] + tb * DC + oc
                        act.wait_ge(bank_done, j + 1)
                        nc.scalar.activation(out[:, oc, tb * BANK:(tb + 1) * BANK], ps[j % NB][:], ACT.Identity,
                                             scale=sc[:, a:a + 1], bias=bias[w][:, oc:oc + 1]).then_inc(bank_kept, 1)

            linear("vis", 0, act_f["vis"], "d2v")
            weight("img")
            linear("image", 1, act_f["img"], "img")
            weight("att0")
            weight("att1")
            act.wait_ge(scale_ready, 3)
            for tb in range(NTB):
                for a in range(2):
                    j = J["kv"] + 2 * tb + a
                    act.wait_ge(bank_done, j + 1)
                    nc.scalar.activation(kvT[:, a, tb * BANK:(tb + 1) * BANK], ps[j % NB][:], ACT.Identity,
                                         scale=sc[:, 2 + a:3 + a], bias=bias[f"att{a}"][:, 0:1]).then_inc(bank_kept, 1)
            for tb in range(NTB):
                for a in range(2):
                    j = J["kvt"] + 2 * tb + a
                    act.wait_ge(bank_done, j + 1)
                    nc.scalar.activation(kvt[:, a, 4 * tb:4 * tb + 4], ps[j % NB][:].rearrange("p (t o) -> p t o", t=4), ACT.Copy).then_inc(bank_kept, 1)
            for w in ("txt", "f1", "f2"):
                weight(w)

        @block.tensor
        def _(pe):
            def bank(j):
                if j >= NB:
                    pe.wait_ge(bank_kept, j - NB + 1)
                return ps[j % NB]

            def weight(w, order):
                pe.wait_ge(w_quant, order)
                for q, blocks in enumerate(keep_weight(w)):
                    out = bank(J[w] + q)[:].bitcast(BF16)
                    for k, (ic, oc) in enumerate(blocks):
                        c0, cn = chunks(XSHAPE[w][1])[ic]
                        i = nc.tensor.transpose(out[0:cn, k * P:(k + 1) * P], qn[w][:, oc, c0:c0 + cn], identb[:])
                    i.then_inc(bank_done, 1)

            def project(pairs):
                for k in pairs:
                    if k >= 4:
                        pe.wait_ge(x1_done, k - 3)
                    rows = slice(64 * (k % 2), 64 * (k % 2) + 64)
                    for ic in range(2):
                        for g in range(GAM):
                            i = nc.tensor.matmul(ps[NB + k % 4][:, ic * D:(ic + 1) * D], aT[rows, k // 2, g, ic * P:(ic + 1) * P],
                                                 wo[rows, g], start=g == 0, stop=g == GAM - 1)
                    i.then_inc(y_done, 1)

            pe.wait_ge(wo_in, 32)
            project((0, 1, 2, 3))
            pe.wait_ge(idb_ready, 1)
            weight("d2v", 1)
            for c, (c0, cn) in enumerate(chunks(CW)):
                for g in range(2):
                    pe.wait_ge(c_quant, g + 1)
                    out = bank(J["ctx"] + 2 * c + g)[:].bitcast(BF16)
                    for t in range(8):
                        i = nc.tensor.transpose(out[0:cn, t * P:(t + 1) * P], cq[:, 8 * g + t, c0:c0 + cn], identb[:])
                    i.then_inc(bank_done, 1)
            pe.wait_ge(bank_kept, J["ctx"] + 4)

            def linear(j0, w, src, widths, ready):
                for tb in range(NTB):
                    if ready is not None:
                        pe.wait_ge(ready, tb + 1)
                    for oc in range(XSHAPE[w][0] // P):
                        o = bank(J[j0] + tb * DC + oc)
                        for c, (c0, cn) in enumerate(widths):
                            i = nc.tensor.matmul(o[:], qwT[w][0:cn, c, oc * P:(oc + 1) * P], src[0:cn, c, tb * BANK:(tb + 1) * BANK],
                                                 start=c == 0, stop=c == len(widths) - 1)
                        i.then_inc(bank_done, 1)

            project((4,))
            linear("vis", "d2v", cqT, chunks(CW), None)
            weight("img", 2)
            pe.wait_ge(bank_kept, J["img"] + 1)
            project((5, 6))
            linear("image", "img", act_q, chunks(D), a_quant["vis"])
            weight("att0", 3)
            weight("att1", 4)
            project((7,))
            pe.wait_ge(bank_kept, J["att1"] + 1)
            for tb in range(NTB):
                pe.wait_ge(a_quant["img"], tb + 1)
                for a in range(2):
                    o = bank(J["kv"] + 2 * tb + a)
                    for c in range(DC):
                        i = nc.tensor.matmul(o[:], qwT[f"att{a}"][:, c], act_q[:, c, tb * BANK:(tb + 1) * BANK], start=c == 0, stop=c == DC - 1)
                    i.then_inc(bank_done, 1)
            for tb in range(NTB):
                for a in range(2):
                    pe.wait_ge(bank_kept, J["kv"] + 2 * tb + a + 1)
                    o = bank(J["kvt"] + 2 * tb + a)
                    for t in range(4):
                        s = tb * BANK + t * P
                        i = nc.tensor.transpose(o[:, t * P:(t + 1) * P], kvT[:, a, s:s + P], ident[:])
                    i.then_inc(bank_done, 1)
            for k, w in enumerate(("txt", "f1", "f2")):
                weight(w, 5 + k)


def cross_phase(nc, ps, io, keep):
    ident, qwT, ws, bias, x1 = (keep[n] for n in ("ident", "qwT", "ws", "bias", "x1"))
    kvT, kvt, fused = keep["kvT"], keep["kvt"], keep["fused"]
    NTB = T // BANK
    with Mem(nc) as m:
        z = m.sb("z_c", [P, NT, D])
        zq = m.sb("zq", [P, NT, D], BF16)
        zqT = m.sb("zqT", [P, DC, T], BF16)
        identb = m.sb("identb_c", [P, P], BF16)
        fsum = m.sb("fsum", [P, 2, T])
        pr = m.sb("pr_c", [P, 4, 2, L])
        prT = m.sb("prT_c", [P, 2, BANK])
        mv = m.sb("mv_c", [P, NT, 2])
        ve, sd, rs = (m.sb(n, [P, NT]) for n in ("ve_c", "sd_c", "rs_c"))
        loc, am, isc, inv, sc = (m.sb(n, [P, 1]) for n in ("loc_c", "am_c", "isc_c", "inv_c", "sc_c"))
        nmax, rsum, rinv = (m.sb(n, [P, 32]) for n in ("nmax_c", "rsum_c", "rinv_c"))
        part = m.sb("part_c", [P, NT])
        dve_step, idb_ready, var_ready, std_ready, loc_ready, am_ready, scale_ready, z_quant = (
            m.sem(f"c_{n}") for n in ("dve_step", "idb_ready", "var_ready", "std_ready", "loc_ready", "am_ready", "scale_ready", "z_quant"))
        zT_done, zT_kept, txt_done, txt_kept, fsum_ready = (m.sem(f"c_{n}") for n in ("zT_done", "zT_kept", "txt_done", "txt_kept", "fsum_ready"))
        fold_ready, rinv_ready = m.sem("fold_ready"), m.sem("rinv_ready")
        s_done, max_ready, exp_done, pr_ready, pt_done, pt_kept, pv_done, pv_kept = (
            m.sem(f"c_{n}") for n in ("s_done", "max_ready", "exp_done", "pr_ready", "pt_done", "pt_kept", "pv_done", "pv_kept"))
        block = m.stack.enter_context(nc.Block())
        UN = 2 * B
        SCALE = 1.0 / D ** 0.5

        @block.gpsimd
        def _(pool):
            nc.gpsimd.tensor_copy(identb[:], ident[:]).then_inc(idb_ready, 1)
            pool.wait_ge(loc_ready, 1)
            nc.gpsimd.partition_all_reduce(am[:], loc[:], P, RMAX).then_inc(am_ready, 1)
            for b in range(B):
                pool.wait_ge(pv_kept, b + 1)
                cols = slice(b * L, (b + 1) * L)
                nc.gpsimd.tensor_tensor(out=fsum[:, 1, cols], in0=fused[:, 0, cols], in1=fused[:, 1, cols], op=ALU.add).then_inc(fold_ready, 1)

        @block.vector
        def _(dve):
            link = Chain(dve, dve_step)
            for t in range(NT):
                i = nc.vector.bn_aggr(mv[:, t], keep["stats"][:, t])
            link(i)
            nc.vector.tensor_scalar_add(ve[:], mv[:, :, 1], 1e-5).then_inc(var_ready, 1)
            dve.wait_ge(std_ready, 1)
            link(nc.vector.reciprocal(rs[:], sd[:]))
            for t in range(NT):
                i = nc.vector.tensor_scalar(z[:, t], x1[:, t], mv[:, t, 0:1], rs[:, t:t + 1], ALU.subtract, ALU.mult)
            link(i)
            nc.vector.tensor_reduce(loc[:], z[:].rearrange("p t d -> p (t d)"), X, ALU.max, apply_absolute_value=True).then_inc(loc_ready, 1)
            dve.wait_ge(am_ready, 1)
            activation_scale(nc, link, am[:], isc[:], inv[:])
            nc.vector.tensor_tensor(out=sc[:], in0=isc[:], in1=ws[:, 2:3], op=ALU.mult).then_inc(scale_ready, 1)
            for g in range(4):
                tiles = slice(4 * g, 4 * g + 4)
                link(nc.vector.tensor_scalar(z[:, tiles], z[:, tiles], inv[:], MAGIC, ALU.mult, ALU.add))
                nc.vector.tensor_scalar(zq[:, tiles], z[:, tiles], MAGIC, None, ALU.subtract).then_inc(z_quant, 1)

            for tb in range(NTB):
                dve.wait_ge(txt_kept, 2 * tb + 2)
                cols = slice(tb * BANK, (tb + 1) * BANK)
                nc.vector.tensor_tensor(out=fsum[:, 0, cols], in0=fused[:, 0, cols], in1=fused[:, 1, cols], op=ALU.add).then_inc(fsum_ready, 1)
            for n in range(UN + 3):
                if n < UN:
                    dve.wait_ge(s_done, n + 1)
                    link(nc.vector.tensor_reduce(nmax[:, 2 * n:2 * n + 2], ps[n % 2][:].rearrange("p (a j) -> p a j", a=2), X, ALU.max,
                                                 negate=True))
                    nc.vector.tensor_scalar_mul(nmax[:, 2 * n:2 * n + 2], nmax[:, 2 * n:2 * n + 2], SCALE).then_inc(max_ready, 1)
                k = n - 1
                if 0 <= k < UN:
                    dve.wait_ge(exp_done, k + 1)
                    nc.vector.reciprocal(rinv[:, 2 * k:2 * k + 2], rsum[:, 2 * k:2 * k + 2]).then_inc(rinv_ready, 1)
                k = n - 3
                if 0 <= k < UN:
                    layer, b = divmod(k, B)
                    cols = slice(b * L, (b + 1) * L)
                    dve.wait_ge(pv_done, k + 1)
                    if layer:
                        if b:
                            dve.wait_ge(pv_kept, k)
                            nc.vector.tensor_reduce(keep["most"][:, b - 1:b], fused[:, :, (b - 1) * L:b * L], XY, ALU.max, apply_absolute_value=True)
                    for c in range(DC):
                        i = nc.vector.scalar_tensor_tensor(out=fused[:, c, cols], in0=ps[4 + k % 2][:, 0:L], scalar=0.1,
                                                           in1=fused[:, c, cols], op0=ALU.mult, op1=ALU.add)
                    i.then_inc(pv_kept, 1)
            dve.wait_ge(pv_kept, UN)
            nc.vector.tensor_reduce(keep["most"][:, B - 1:B], fused[:, :, (B - 1) * L:B * L], XY, ALU.max, apply_absolute_value=True)

        @block.scalar
        def _(act):
            act.wait_ge(var_ready, 1)
            nc.scalar.activation(sd[:], ve[:], ACT.Sqrt).then_inc(std_ready, 1)
            for n in range(4):
                g, c = divmod(n, 2)
                act.wait_ge(zT_done, n + 1)
                nc.scalar.activation(zqT[:, c, g * 1024:(g + 1) * 1024], ps[n][:].bitcast(BF16), ACT.Copy).then_inc(zT_kept, 1)
            act.wait_ge(scale_ready, 1)
            for n in range(8):
                tb, oc = divmod(n, DC)
                act.wait_ge(txt_done, n + 1)
                nc.scalar.activation(fused[:, oc, tb * BANK:(tb + 1) * BANK], ps[4 + n % 4][:], ACT.Identity,
                                     scale=sc[:], bias=bias["txt"][:, oc:oc + 1]).then_inc(txt_kept, 1)
            for n in range(UN + 3):
                if n < UN:
                    act.wait_ge(max_ready, n + 1)
                    if n >= 4:
                        act.wait_ge(pt_done, n - 3)
                    for a in range(2):
                        i = nc.scalar.activation(pr[:, n % 4, a], ps[n % 2][:, a * L:(a + 1) * L], ACT.Exp,
                                                 bias=nmax[:, 2 * n + a:2 * n + a + 1], scale=SCALE, accum_out=rsum[:, 2 * n + a:2 * n + a + 1])
                    i.then_inc(exp_done, 1)
                k = n - 1
                if 0 <= k < UN:
                    act.wait_ge(rinv_ready, k + 1)
                    for a in range(2):
                        i = nc.scalar.activation(pr[:, k % 4, a], pr[:, k % 4, a], ACT.Copy, scale=rinv[:, 2 * k + a:2 * k + a + 1])
                    i.then_inc(pr_ready, 1)
                k = n - 2
                if 0 <= k < UN:
                    act.wait_ge(pt_done, k + 1)
                    if k >= 2:
                        act.wait_ge(pv_done, k - 1)
                    nc.scalar.activation(prT[:, k % 2], ps[2 + k % 2][:], ACT.Copy).then_inc(pt_kept, 1)

        @block.tensor
        def _(pe):
            pe.wait_ge(idb_ready, 1)
            for n in range(4):
                g, c = divmod(n, 2)
                pe.wait_ge(z_quant, 2 * g + 2)
                for t in range(8):
                    i = nc.tensor.transpose(ps[n][:].bitcast(BF16)[:, t * P:(t + 1) * P], zq[:, 8 * g + t, c * P:(c + 1) * P], identb[:])
                i.then_inc(zT_done, 1)
            for n in range(8):
                tb, oc = divmod(n, DC)
                pe.wait_ge(zT_kept, 2 * (tb // 2) + 2)
                if n >= 4:
                    pe.wait_ge(txt_kept, n - 3)
                for c in range(DC):
                    i = nc.tensor.matmul(ps[4 + n % 4][:], qwT["txt"][:, c, oc * P:(oc + 1) * P], zqT[:, c, tb * BANK:(tb + 1) * BANK],
                                         start=c == 0, stop=c == DC - 1)
                i.then_inc(txt_done, 1)
            pe.wait_ge(txt_kept, 8)
            for n in range(UN + 3):
                if n < UN:
                    layer, b = divmod(n, B)
                    if layer:
                        pe.wait_ge(fold_ready, b + 1)
                    else:
                        pe.wait_ge(fsum_ready, b // 2 + 1)
                    if n >= 2:
                        pe.wait_ge(exp_done, n - 1)
                    for a in range(2):
                        s = b * L + a * P
                        i = nc.tensor.matmul(ps[n % 2][:, a * L:(a + 1) * L], fsum[:, layer, s:s + P], kvT[:, layer, b * L:(b + 1) * L],
                                             start=True, stop=True)
                    i.then_inc(s_done, 1)
                k = n - 2
                if 0 <= k < UN:
                    pe.wait_ge(pr_ready, k + 1)
                    if k >= 2:
                        pe.wait_ge(pt_kept, k - 1)
                    for a in range(2):
                        for jc in range(2):
                            i = nc.tensor.transpose(ps[2 + k % 2][:, jc * L + a * P:jc * L + (a + 1) * P], pr[:, k % 4, a, jc * P:(jc + 1) * P], ident[:])
                    i.then_inc(pt_done, 1)
                k = n - 3
                if 0 <= k < UN:
                    layer, b = divmod(k, B)
                    pe.wait_ge(pt_kept, k + 1)
                    if k >= 2:
                        pe.wait_ge(pv_kept, k - 1)
                    for jc in range(2):
                        i = nc.tensor.matmul(ps[4 + k % 2][:, 0:L], kvt[:, layer, 2 * b + jc], prT[:, k % 2, jc * L:(jc + 1) * L],
                                             start=jc == 0, stop=jc == 1)
                    i.then_inc(pv_done, 1)


def feed_phase(nc, ps, io, keep):
    ident, qwT, ws, bias, x1 = (keep[n] for n in ("ident", "qwT", "ws", "bias", "x1"))
    fused, avg = keep["fused"], keep["avg"]
    NTB = T // BANK
    FC = 8
    with Mem(nc) as m:
        h = m.sb("h", [P, FC, T])
        hq = m.sb("hq", [P, FC, T], BF16)
        qf = m.sb("qf", [P, DC, T], BF16)
        oT = m.sb("oT", [P, DC, T])
        qavg = m.sb("qavg", [P, DC, B], BF16)
        avm = m.sb("avm", [P, DC, B])
        part = m.sb("part_f", [P, 40])
        loc, am, isc, inv, sc = (m.sb(n, [P, 2]) for n in ("loc_f", "am_f", "isc_f", "inv_f", "sc_f"))
        dve_step, loc_ready, am_ready, scale_ready, f_quant, h_quant = (
            m.sem(f"f_{n}") for n in ("dve_step", "loc_ready", "am_ready", "scale_ready", "f_quant", "h_quant"))
        h_done, h_kept, o_done, o_kept, t_done, t_kept = (m.sem(f"f_{n}") for n in ("h_done", "h_kept", "o_done", "o_kept", "t_done", "t_kept"))
        block = m.stack.enter_context(nc.Block())

        @block.gpsimd
        def _(pool):
            for a in range(2):
                pool.wait_ge(loc_ready, a + 1)
                nc.gpsimd.partition_all_reduce(am[:, a:a + 1], loc[:, a:a + 1], P, RMAX).then_inc(am_ready, 1)

        @block.vector
        def _(dve):
            link = Chain(dve, dve_step)
            nc.vector.tensor_reduce(part[:, 0:1], keep["most"][:], X, ALU.max)
            link(nc.vector.tensor_reduce(part[:, 1:2], avg[:].rearrange("p c b -> p (c b)"), X, ALU.max, apply_absolute_value=True))
            nc.vector.tensor_reduce(loc[:, 0:1], part[:, 0:2], X, ALU.max).then_inc(loc_ready, 1)
            dve.wait_ge(am_ready, 1)
            activation_scale(nc, link, am[:, 0:1], isc[:, 0:1], inv[:, 0:1])
            nc.vector.tensor_tensor(out=sc[:, 0:1], in0=isc[:, 0:1], in1=ws[:, 5:6], op=ALU.mult).then_inc(scale_ready, 1)
            link(nc.vector.tensor_scalar(avm[:], avg[:], inv[:, 0:1], MAGIC, ALU.mult, ALU.add))
            nc.vector.tensor_scalar(qavg[:], avm[:], MAGIC, None, ALU.subtract)
            for tb in range(NTB):
                cols = slice(tb * BANK, (tb + 1) * BANK)
                link(nc.vector.tensor_scalar(fused[:, :, cols], fused[:, :, cols], inv[:, 0:1], MAGIC, ALU.mult, ALU.add))
                nc.vector.tensor_scalar(qf[:, :, cols], fused[:, :, cols], MAGIC, None, ALU.subtract).then_inc(f_quant, 1)
            for n in range(NTB * FC):
                tb, fc = divmod(n, FC)
                dve.wait_ge(h_kept, n + 1)
                i = nc.vector.reduce_max(part[:, 2 + n:3 + n], h[:, fc, tb * BANK:(tb + 1) * BANK], X)
            link(i)
            nc.vector.reduce_max(loc[:, 1:2], part[:, 2:2 + NTB * FC], X).then_inc(loc_ready, 1)
            dve.wait_ge(am_ready, 2)
            activation_scale(nc, link, am[:, 1:2], isc[:, 1:2], inv[:, 1:2])
            nc.vector.tensor_tensor(out=sc[:, 1:2], in0=isc[:, 1:2], in1=ws[:, 6:7], op=ALU.mult).then_inc(scale_ready, 1)
            for tb in range(NTB):
                cols = slice(tb * BANK, (tb + 1) * BANK)
                link(nc.vector.tensor_scalar(h[:, :, cols], h[:, :, cols], inv[:, 1:2], MAGIC, ALU.mult, ALU.add))
                nc.vector.tensor_scalar(hq[:, :, cols], h[:, :, cols], MAGIC, None, ALU.subtract).then_inc(h_quant, 1)
            for n in range(NT // 2):
                dve.wait_ge(t_done, n + 1)
                nc.vector.tensor_tensor(out=x1[:, 2 * n:2 * n + 2], in0=ps[n % 4][:].rearrange("p (t d) -> p t d", t=2),
                                        in1=x1[:, 2 * n:2 * n + 2], op=ALU.add).then_inc(t_kept, 1)

        @block.scalar
        def _(act):
            act.wait_ge(scale_ready, 1)
            for n in range(NTB * FC):
                tb, fc = divmod(n, FC)
                act.wait_ge(h_done, n + 1)
                nc.scalar.activation(h[:, fc, tb * BANK:(tb + 1) * BANK], ps[n % 8][:], ACT.Relu,
                                     scale=sc[:, 0:1], bias=bias["f1"][:, fc:fc + 1]).then_inc(h_kept, 1)
            act.wait_ge(scale_ready, 2)
            for n in range(NTB * DC):
                tb, oc = divmod(n, DC)
                act.wait_ge(o_done, n + 1)
                nc.scalar.activation(oT[:, oc, tb * BANK:(tb + 1) * BANK], ps[4 + n % 4][:], ACT.Identity,
                                     scale=sc[:, 1:2], bias=bias["f2"][:, oc:oc + 1]).then_inc(o_kept, 1)

        @block.tensor
        def _(pe):
            for n in range(NTB * FC):
                tb, fc = divmod(n, FC)
                pe.wait_ge(f_quant, tb + 1)
                if n >= 8:
                    pe.wait_ge(h_kept, n - 7)
                for c in range(DC):
                    nc.tensor.matmul(ps[n % 8][:], qwT["f1"][:, c, fc * P:(fc + 1) * P], qf[:, c, tb * BANK:(tb + 1) * BANK],
                                     start=c == 0, stop=False)
                for c in range(DC):
                    i = nc.tensor.matmul(ps[n % 8][:], qwT["f1"][:, DC + c, fc * P:(fc + 1) * P],
                                         bc(qavg[:, c, 2 * tb:2 * tb + 2].unsqueeze(2), P, 2, L), start=False, stop=c == DC - 1)
                i.then_inc(h_done, 1)
            pe.wait_ge(h_kept, NTB * FC)
            for tb in range(NTB):
                pe.wait_ge(h_quant, tb + 1)
                for oc in range(DC):
                    n = tb * DC + oc
                    if n >= 4:
                        pe.wait_ge(o_kept, n - 3)
                    for fc in range(FC):
                        i = nc.tensor.matmul(ps[4 + n % 4][:], qwT["f2"][:, fc, oc * P:(oc + 1) * P], hq[:, fc, tb * BANK:(tb + 1) * BANK],
                                             start=fc == 0, stop=fc == FC - 1)
                    i.then_inc(o_done, 1)
                pe.wait_ge(o_kept, 2 * tb + 2)
                for k in (2 * tb, 2 * tb + 1):
                    if k >= 4:
                        pe.wait_ge(t_kept, k - 3)
                    for t in range(2):
                        for c in range(DC):
                            s = (2 * k + t) * P
                            i = nc.tensor.transpose(ps[k % 4][:, t * D + c * P:t * D + (c + 1) * P], oT[:, c, s:s + P], ident[:])
                    i.then_inc(t_done, 1)


NE, FF = 8, 1024
FFC = FF // P
SLOTS = T // P + NE - 1
I32 = mybir.dt.int32


def route_phase(nc, ps, io, keep):
    ident, x2, slot, tile_e = (keep[n] for n in ("ident", "x1", "slot", "tile_e"))
    w1T, w2T, stage, rows = keep["w1T"], keep["w2T"], keep["stage"], keep["rows"]
    with Mem(nc) as m:
        y = m.sb("y", [P, NT, D])
        yT = m.sb("yT", [P, DC, T])
        st = m.sb("st_e", [P, NT, 6])
        mv = m.sb("mv_e", [P, NT, 2])
        ve, sd, rs = (m.sb(n, [P, NT]) for n in ("ve_e", "sd_e", "rs_e"))
        wr = m.sb("router", [NE, D])
        wrT = m.sb("routerT", [P, DC, NE])
        br = m.sb("br", [P, NE])
        lg, eq, hot = (m.sb(n, [P, NT, NE]) for n in ("lg", "eq", "hot"))
        hotb = m.sb("hotb", [P, NT, NE], BF16)
        tri, ones = m.sb("tri", [P, P], BF16), m.sb("ones", [P, P], BF16)
        zero = m.sb("zero", [P, 1, D])
        iota8 = m.sb("iota8", [P, NE])
        iotat = m.sb("iotat", [1, SLOTS])
        best, first, slotf = (m.sb(n, [P, NT]) for n in ("best", "first", "slotf"))
        cnt, tiles, ends, base = (m.sb(n, [P, NE]) for n in ("cnt_e", "tiles", "ends", "base"))
        cnti = m.sb("cnti", [P, NE], I32)
        cmp = m.sb("cmp", [1, SLOTS, NE - 1])
        tef = m.sb("tef", [1, SLOTS])
        w1_in, w2_in = [m.sem("w1_in0"), m.sem("w1_in1")], [m.sem("w2_in0"), m.sem("w2_in1")]
        wr_in, br_in, zero_sent, row_sent = (m.sem(n) for n in ("wr_in_e", "br_in", "zero_sent", "row_sent"))
        pool_step, consts_ready, dve_step, var_ready, std_ready, y_ready = (
            m.sem(f"e_{n}") for n in ("pool_step", "consts_ready", "dve_step", "var_ready", "std_ready", "y_ready"))
        wT_done, wT_kept, yT_done, yT_kept, wrT_done, wrT_kept, lg_done, hot_ready, pos_done, slot_ready = (
            m.sem(f"e_{n}") for n in ("wT_done", "wT_kept", "yT_done", "yT_kept", "wrT_done", "wrT_kept", "lg_done", "hot_ready", "pos_done", "slot_ready"))
        w_banks = ps[0:4]
        y_banks, lg_bank, pos_bank = ps[4:6], ps[6], ps[7]
        stages = [stage, yT[:].rearrange("p c t -> p (c t)")]
        s1 = [x[:, 0:FFC * D].rearrange("p (f d) -> p f d", d=D) for x in stages]
        s2 = [x[:, FFC * D:2 * FFC * D].rearrange("p (c f) -> p c f", f=FF) for x in stages]
        block = m.stack.enter_context(nc.Block())

        @block.sync
        def _(sp):
            sp.dma_start(wr[:], io["L0_ffn_Wr"]).then_inc(wr_in, 16)
            sp.dma_start(br[:], bc(io["L0_ffn_br"].unsqueeze(0), P, NE)).then_inc(br_in, 16)
            w1 = io["L0_ffn_W1"].rearrange("e (f p) d -> p (e f) d", p=P)
            w2 = io["L0_ffn_W2"].rearrange("e (c p) f -> p (e c) f", p=P)

            def load(e, place, w1_used, w2_used):
                if w2_used is not None:
                    sp.wait_ge(wT_done, w1_used)
                    sp.nop(nofuse=True)
                sp.dma_start(s1[place], w1[:, bass.ds(e * FFC, FFC)]).then_inc(w1_in[place], 16)
                if w2_used is not None:
                    sp.wait_ge(wT_done, w2_used)
                    sp.nop(nofuse=True)
                sp.dma_start(s2[place], w2[:, bass.ds(e * DC, DC)]).then_inc(w2_in[place], 16)

            load(0, 0, None, None)
            load(1, 0, 4, 8)
            sp.wait_ge(lg_done, 1)
            load(2, 1, None, None)
            load(3, 0, 12, 16)
            with sp.Fori(2, NE // 2) as j:
                load(2 * j, 1, 16 * j - 12, 16 * j - 8)
                load(2 * j + 1, 0, 16 * j - 4, 16 * j)
            sp.wait_ge(zero_sent, 16)
            sp.wait_ge(row_sent, 16 * NT)

        @block.gpsimd
        def _(pool):
            nc.gpsimd.memset(zero[:], 0.0).then_inc(pool_step, 1)
            pool.wait_ge(pool_step, 1)
            pool.dma_start(rows.rearrange("(k p) d -> p k d", p=P), bc(zero[:], P, SLOTS, D)).then_inc(zero_sent, 16)
            nc.gpsimd.memset(ones[:], 1.0).then_inc(pool_step, 1)
            pool.wait_ge(pool_step, 2)
            nc.gpsimd.affine_select(out=tri[:], in_=ones[:], compare_op=ALU.is_gt, fill=0.0, base=0,
                                    pattern=[[1, P]], channel_multiplier=-1).then_inc(consts_ready, 1)
            nc.gpsimd.iota(iota8[:], pattern=[[1, NE]], base=-NE, channel_multiplier=0,
                           allow_small_or_imprecise_dtypes=True).then_inc(consts_ready, 1)
            nc.gpsimd.iota(iotat[:], pattern=[[1, SLOTS]], base=0, channel_multiplier=0,
                           allow_small_or_imprecise_dtypes=True).then_inc(consts_ready, 1)
            pool.wait_ge(zero_sent, 16)
            pool.wait_ge(slot_ready, 1)
            for t in range(NT):
                pool.indirect_dma_start(out=rows, out_offset=bass.IndirectOffsetOnAxis(ap=slot[:, t:t + 1], axis=0),
                                        in_=y[:, t], in_offset=None).then_inc(row_sent, 16)

        @block.vector
        def _(dve):
            link = Chain(dve, dve_step)
            for t in range(NT):
                i = nc.vector.bn_stats(st[:, t], x2[:, t])
            link(i)
            for t in range(NT):
                i = nc.vector.bn_aggr(mv[:, t], st[:, t])
            link(i)
            nc.vector.tensor_scalar_add(ve[:], mv[:, :, 1], 1e-5).then_inc(var_ready, 1)
            dve.wait_ge(std_ready, 1)
            link(nc.vector.reciprocal(rs[:], sd[:]))
            for t in range(NT):
                nc.vector.tensor_scalar(y[:, t], x2[:, t], mv[:, t, 0:1], rs[:, t:t + 1], ALU.subtract, ALU.mult).then_inc(y_ready, 1)
            dve.wait_ge(wrT_done, 1)
            nc.vector.tensor_copy(wrT[:].rearrange("p c e -> p (c e)"), lg_bank[:, 0:DC * NE]).then_inc(wrT_kept, 1)
            for n in range(8):
                tb, c = divmod(n, DC)
                dve.wait_ge(yT_done, n + 1)
                nc.vector.tensor_copy(yT[:, c, tb * BANK:(tb + 1) * BANK], y_banks[n % 2][:]).then_inc(yT_kept, 1)
            dve.wait_ge(consts_ready, 3)
            dve.wait_ge(br_in, 16)
            dve.wait_ge(lg_done, 1)
            link(nc.vector.tensor_tensor(out=lg[:], in0=lg_bank[:, 0:NT * NE].rearrange("p (t e) -> p t e", e=NE),
                                         in1=bc(br[:].unsqueeze(1), P, NT, NE), op=ALU.add))
            link(nc.vector.tensor_reduce(best[:], lg[:], X, ALU.max))
            link(nc.vector.tensor_tensor(out=eq[:], in0=lg[:], in1=bc(best[:].unsqueeze(2), P, NT, NE), op=ALU.is_ge))
            link(nc.vector.tensor_tensor(out=eq[:], in0=eq[:], in1=bc(iota8[:].unsqueeze(1), P, NT, NE), op=ALU.mult))
            link(nc.vector.tensor_reduce(first[:], eq[:], X, ALU.min))
            link(nc.vector.tensor_tensor(out=hot[:], in0=bc(iota8[:].unsqueeze(1), P, NT, NE),
                                         in1=bc(first[:].unsqueeze(2), P, NT, NE), op=ALU.is_equal))
            nc.vector.tensor_copy(hotb[:], hot[:]).then_inc(hot_ready, 1)
            dve.wait_ge(pos_done, 1)
            link(nc.vector.tensor_scalar_add(cnt[:], pos_bank[:, NT * NE:(NT + 1) * NE], float(P - 1)))
            link(nc.vector.tensor_copy(cnti[:], cnt[:]))
            link(nc.vector.tensor_single_scalar(cnti[:], cnti[:], 7, op=ALU.logical_shift_right))
            link(nc.vector.tensor_copy(tiles[:], cnti[:]))
            link(nc.vector.tensor_copy(ends[:, 0:1], tiles[:, 0:1]))
            for e in range(1, NE):
                link(nc.vector.tensor_tensor(out=ends[:, e:e + 1], in0=ends[:, e - 1:e], in1=tiles[:, e:e + 1], op=ALU.add))
            link(nc.vector.tensor_tensor(out=base[:], in0=ends[:], in1=tiles[:], op=ALU.subtract))
            link(nc.vector.tensor_scalar_mul(base[:], base[:], float(P)))
            link(nc.vector.tensor_tensor(out=eq[:], in0=pos_bank[:, 0:NT * NE].rearrange("p (t e) -> p t e", e=NE),
                                         in1=bc(base[:].unsqueeze(1), P, NT, NE), op=ALU.add))
            link(nc.vector.tensor_tensor(out=eq[:], in0=eq[:], in1=hot[:], op=ALU.mult))
            link(nc.vector.tensor_reduce(slotf[:], eq[:], X, ALU.add))
            nc.vector.tensor_copy(slot[:], slotf[:]).then_inc(slot_ready, 1)
            link(nc.vector.tensor_tensor(out=cmp[:], in0=bc(iotat[:].unsqueeze(2), 1, SLOTS, NE - 1),
                                         in1=bc(ends[0:1, 0:NE - 1].unsqueeze(1), 1, SLOTS, NE - 1), op=ALU.is_ge))
            link(nc.vector.tensor_reduce(tef[:], cmp[:], X, ALU.add))
            link(nc.vector.tensor_copy(tile_e[:], tef[:]))

        @block.scalar
        def _(act):
            act.wait_ge(var_ready, 1)
            nc.scalar.activation(sd[:], ve[:], ACT.Sqrt).then_inc(std_ready, 1)
            with act.Fori(0, NE) as e:
                for n in range(8):
                    act.wait_ge(wT_done, 8 * e + n + 1)
                    if n < 4:
                        c, half = divmod(n, 2)
                        dst = w1T[:].rearrange("p (e c f) -> p e c f", e=NE, c=DC)[:, bass.ds(e, 1), c, half * BANK:(half + 1) * BANK]
                    else:
                        dst = w2T[:].rearrange("p (e q j) -> p e q j", e=NE, q=4)[:, bass.ds(e, 1), n - 4]
                    nc.scalar.activation(dst, w_banks[n % 4][:].unsqueeze(1), ACT.Copy).then_inc(wT_kept, 1)

        @block.tensor
        def _(pe):
            def weights(e, place, loads):
                for n in range(8):
                    if n == 0:
                        pe.wait_ge(w1_in[place], 16 * loads)
                    if n == 4:
                        pe.wait_ge(w2_in[place], 16 * loads)
                    if n >= 4 or not isinstance(e, int) or e:
                        pe.wait_ge(wT_kept, 8 * e + n - 3)
                    for k in range(4):
                        if n < 4:
                            c, half = divmod(n, 2)
                            src = s1[place][:, 4 * half + k, c * P:(c + 1) * P]
                        else:
                            fc, c = divmod(4 * (n - 4) + k, DC)
                            src = s2[place][:, c, fc * P:(fc + 1) * P]
                        i = nc.tensor.transpose(w_banks[n % 4][:, k * P:(k + 1) * P], src, ident[:])
                    i.then_inc(wT_done, 1)

            weights(0, 0, 1)
            pe.wait_ge(wr_in, 16)
            for c in range(DC):
                i = nc.tensor.transpose(lg_bank[:, c * NE:(c + 1) * NE], wr[:, c * P:(c + 1) * P], ident[0:NE, 0:NE])
            i.then_inc(wrT_done, 1)
            for n in range(8):
                tb, c = divmod(n, DC)
                pe.wait_ge(y_ready, 4 * tb + 4)
                if n >= 2:
                    pe.wait_ge(yT_kept, n - 1)
                for t in range(4):
                    i = nc.tensor.transpose(y_banks[n % 2][:, t * P:(t + 1) * P], y[:, 4 * tb + t, c * P:(c + 1) * P], ident[:])
                i.then_inc(yT_done, 1)
            pe.wait_ge(wrT_kept, 1)
            pe.wait_ge(yT_kept, 8)
            for t in range(NT):
                for c in range(DC):
                    i = nc.tensor.matmul(lg_bank[:, t * NE:(t + 1) * NE], yT[:, c, t * P:(t + 1) * P], wrT[:, c], start=c == 0, stop=c == DC - 1)
            i.then_inc(lg_done, 1)
            weights(1, 0, 2)
            pe.wait_ge(hot_ready, 1)
            nc.tensor.matmul(pos_bank[:, 0:NT * NE], tri[:], hotb[:].rearrange("p t e -> p (t e)"), start=True, stop=False)
            for t in range(NT - 1):
                nc.tensor.matmul(pos_bank[:, (t + 1) * NE:NT * NE].rearrange("p (t e) -> p t e", e=NE), ones[:],
                                 bc(hotb[:, t:t + 1], P, NT - 1 - t, NE), start=False, stop=t == NT - 2)
            for t in range(NT):
                i = nc.tensor.matmul(pos_bank[:, NT * NE:(NT + 1) * NE], ones[:], hotb[:, t], start=t == 0, stop=t == NT - 1)
            i.then_inc(pos_done, 1)
            with pe.Fori(1, NE // 2) as j:
                weights(2 * j, 1, j)
                weights(2 * j + 1, 0, j + 2)


def expert_phase(nc, ps, io, keep):
    ident, tile_e, w1T, w2T = (keep[n] for n in ("ident", "tile_e", "w1T", "w2T"))
    rows, outs = keep["rows"], keep["outs"]
    with Mem(nc) as m:
        b1T = m.sb("b1T", [P, NE * FFC])
        b1n = m.sb("b1n", [NE * FFC, P])
        b2 = m.sb("b2", [P, NE * D])
        yt = m.sb("yt", [P, 2, D])
        yTt = m.sb("yTt", [P, 2, DC, P])
        hs = m.sb("hs", [P, FF])
        hT = m.sb("hT", [P, 2, FFC, P])
        ot = m.sb("ot", [P, 2, D])
        b1_in, b2_in, y_in = m.sem("b1_in"), m.sem("b2_in"), [m.sem("y_in0"), m.sem("y_in1")]
        b1T_done, b1T_kept, yT_done, yT_kept, h_done, h_kept, hT_done, hT_kept, o_done, o_kept = (
            m.sem(f"x_{n}") for n in ("b1T_done", "b1T_kept", "yT_done", "yT_kept", "h_done", "h_kept", "hT_done", "hT_kept", "o_done", "o_kept"))
        o_sent = [m.sem("o_sent0"), m.sem("o_sent1")]
        yT_bank, h_banks, hT_banks, o_bank = ps[0], ps[1:3], ps[3:5], ps[5]
        N2 = (SLOTS - 1) // 2
        assert SLOTS % 2
        rv = rows.rearrange("(k p) d -> k p d", p=P)
        ov = outs.rearrange("(k p) d -> k p d", p=P)

        def past(j, c, n):
            return not isinstance(j, int) or 2 * j + c >= n

        block = m.stack.enter_context(nc.Block())

        @block.sync
        def _(sp):
            sp.dma_start(b1n[:], io["L0_ffn_b1"].rearrange("e (c p) -> (e c) p", p=P)).then_inc(b1_in, 16)
            sp.dma_start(b2[:], bc(io["L0_ffn_b2"].rearrange("e d -> (e d)").unsqueeze(0), P, NE * D)).then_inc(b2_in, 16)

            def fetch(j, c):
                if past(j, c, 2):
                    sp.wait_ge(yT_done, 2 * j + c - 1)
                sp.dma_start(yt[:, c % 2], rv[bass.ds(2 * j + c, 1)].rearrange("k p d -> p (k d)")).then_inc(y_in[c % 2], 16)

            def store(j, c):
                sp.wait_ge(o_kept, 2 * j + c + 1)
                sp.dma_start(ov[bass.ds(2 * j + c, 1)].rearrange("k p d -> p (k d)"), ot[:, c % 2]).then_inc(o_sent[c % 2], 16)

            fetch(0, 0)
            fetch(0, 1)
            fetch(0, 2)

            def turn(j):
                fetch(j, 3)
                store(j, 0)
                fetch(j, 4)
                store(j, 1)

            turn(0)
            with sp.Fori(1, N2 - 1) as j:
                turn(j)
            for c in range(3):
                store(N2 - 1, c)
            sp.wait_ge(o_sent[0], 16 * (N2 + 1))
            sp.wait_ge(o_sent[1], 16 * N2)

        @block.vector
        def _(dve):
            dve.wait_ge(b1T_done, 1)
            nc.vector.tensor_copy(b1T[:], o_bank[:, 0:NE * FFC]).then_inc(b1T_kept, 1)
            dve.wait_ge(b2_in, 16)

            def keep_yT(j, c):
                dve.wait_ge(yT_done, 2 * j + c + 1)
                if past(j, c, 2):
                    dve.wait_ge(h_done, 2 * j + c - 1)
                nc.vector.tensor_copy(yTt[:, c % 2], yT_bank[:, 0:DC * P].rearrange("p (c t) -> p c t", c=DC)).then_inc(yT_kept, 1)

            def keep_h(j, c):
                dve.wait_ge(h_done, 2 * j + c + 1)
                if past(j, c, 1):
                    dve.wait_ge(hT_done, 2 * j + c)
                nc.vector.tensor_copy(hs[:, 0:BANK], h_banks[0][:])
                nc.vector.tensor_copy(hs[:, BANK:FF], h_banks[1][:]).then_inc(h_kept, 1)

            def keep_o(j, c):
                e = dve.value_load(tile_e[0:1, bass.ds(2 * j + c, 1)], min_val=0, max_val=NE - 1)
                dve.wait_ge(o_done, 2 * j + c + 1)
                if past(j, c, 2):
                    dve.wait_ge(o_sent[c % 2], 16 * (j + c // 2))
                nc.vector.tensor_tensor(out=ot[:, c % 2], in0=o_bank[:, 0:D], in1=b2[:, bass.ds(e * D, D)], op=ALU.add).then_inc(o_kept, 1)

            keep_yT(0, 0)
            keep_yT(0, 1)
            keep_h(0, 0)

            def turn(j, c, last):
                if not last:
                    keep_yT(j, c + 1)
                keep_h(j, c)
                keep_o(j, c - 1)

            turn(0, 1, False)
            turn(0, 2, False)
            with dve.Fori(1, N2 - 1) as j:
                turn(j, 1, False)
                turn(j, 2, False)
            turn(N2 - 1, 1, False)
            turn(N2 - 1, 2, True)
            keep_o(N2 - 1, 2)

        @block.scalar
        def _(act):
            act.wait_ge(b1T_kept, 1)

            def relu(j, c):
                e = act.value_load(tile_e[0:1, bass.ds(2 * j + c, 1)], min_val=0, max_val=NE - 1)
                act.wait_ge(hT_done, 2 * j + c + 1)
                if past(j, c, 2):
                    act.wait_ge(o_done, 2 * j + c - 1)
                for fc in range(FFC):
                    i = nc.scalar.activation(hT[:, c % 2, fc], hT_banks[fc // 4][:, fc % 4 * P:(fc % 4 + 1) * P], ACT.Relu,
                                             bias=b1T[:, bass.ds(e * FFC + fc, 1)])
                i.then_inc(hT_kept, 1)

            for c in range(3):
                relu(0, c)
            with act.Fori(1, N2) as j:
                relu(j, 1)
                relu(j, 2)

        @block.tensor
        def _(pe):
            pe.wait_ge(b1_in, 16)
            nc.tensor.transpose(o_bank[:, 0:NE * FFC], b1n[:], ident[0:NE * FFC, 0:NE * FFC]).then_inc(b1T_done, 1)
            pe.wait_ge(b1T_kept, 1)

            def turn_y(j, c):
                pe.wait_ge(y_in[c % 2], 16 * (j + c // 2 + 1))
                if past(j, c, 1):
                    pe.wait_ge(yT_kept, 2 * j + c)
                for k in range(DC):
                    i = nc.tensor.transpose(yT_bank[:, k * P:(k + 1) * P], yt[:, c % 2, k * P:(k + 1) * P], ident[:])
                i.then_inc(yT_done, 1)

            def layer1(j, c):
                e = pe.value_load(tile_e[0:1, bass.ds(2 * j + c, 1)], min_val=0, max_val=NE - 1)
                pe.wait_ge(yT_kept, 2 * j + c + 1)
                if past(j, c, 1):
                    pe.wait_ge(h_kept, 2 * j + c)
                for half in range(2):
                    for k in range(DC):
                        i = nc.tensor.matmul(h_banks[half][:], yTt[:, c % 2, k], w1T[:, bass.ds(e * (DC * FF) + k * FF + half * BANK, BANK)],
                                             start=k == 0, stop=k == DC - 1)
                i.then_inc(h_done, 1)

            def turn_h(j, c):
                pe.wait_ge(h_kept, 2 * j + c + 1)
                if past(j, c, 1):
                    pe.wait_ge(hT_kept, 2 * j + c)
                for fc in range(FFC):
                    i = nc.tensor.transpose(hT_banks[fc // 4][:, fc % 4 * P:(fc % 4 + 1) * P], hs[:, fc * P:(fc + 1) * P], ident[:])
                i.then_inc(hT_done, 1)

            def layer2(j, c):
                e = pe.value_load(tile_e[0:1, bass.ds(2 * j + c, 1)], min_val=0, max_val=NE - 1)
                pe.wait_ge(hT_kept, 2 * j + c + 1)
                if past(j, c, 1):
                    pe.wait_ge(o_kept, 2 * j + c)
                for fc in range(FFC):
                    i = nc.tensor.matmul(o_bank[:, 0:D], hT[:, c % 2, fc], w2T[:, bass.ds(e * (FFC * D) + fc * D, D)],
                                         start=fc == 0, stop=fc == FFC - 1)
                i.then_inc(o_done, 1)

            turn_y(0, 0)
            turn_y(0, 1)
            layer1(0, 0)
            turn_h(0, 0)

            def turn(j, c, last):
                if not last:
                    turn_y(j, c + 1)
                layer1(j, c)
                layer2(j, c - 1)
                turn_h(j, c)

            turn(0, 1, False)
            turn(0, 2, False)
            with pe.Fori(1, N2 - 1) as j:
                turn(j, 1, False)
                turn(j, 2, False)
            turn(N2 - 1, 1, False)
            turn(N2 - 1, 2, True)
            layer2(N2 - 1, 2)


def final_phase(nc, ps, io, keep, out):
    x2, slot, outs = keep["x1"], keep["slot"], keep["outs"]
    with Mem(nc) as m:
        g = m.sb("g", [P, NT, D])
        row_in = [m.sem(f"row_in{k}") for k in range(4)]
        sum_ready, out_sent = m.sem("sum_ready"), m.sem("out_sent")
        block = m.stack.enter_context(nc.Block())

        @block.gpsimd
        def _(pool):
            for t in range(NT):
                pool.indirect_dma_start(out=g[:, t], out_offset=None, in_=outs,
                                        in_offset=bass.IndirectOffsetOnAxis(ap=slot[:, t:t + 1], axis=0)).then_inc(row_in[t // 4], 16)

        @block.vector
        def _(dve):
            for k in range(4):
                dve.wait_ge(row_in[k], 64)
                nc.vector.tensor_tensor(out=g[:, 4 * k:4 * k + 4], in0=g[:, 4 * k:4 * k + 4], in1=x2[:, 4 * k:4 * k + 4], op=ALU.add).then_inc(sum_ready, 1)

        @block.sync
        def _(sp):
            ov = out.rearrange("b s d -> (b s) d").rearrange("(t p) d -> p t d", p=P)
            for k in range(4):
                sp.wait_ge(sum_ready, k + 1)
                sp.dma_start(ov[:, 4 * k:4 * k + 4], g[:, 4 * k:4 * k + 4]).then_inc(out_sent, 16)
            sp.wait_ge(out_sent, 64)


def build(nc, io, out):
    with ExitStack() as sems, Mem(nc) as top:
        Mem.sems = sems
        ps = [top.stack.enter_context(nc.psum_tensor(f"bank{i}", [P, BANK], F32)) for i in range(8)]
        keep = {"ident": top.sb("ident", [P, P]), "aT": top.sb("aT", [P, B // 2, GAM, L])}
        with Mem(nc) as m2:
            for n in ("q2", "k2"):
                keep[n] = m2.sb(n, [P, HP, T])
            for n in ("ucol", "vcol"):
                keep[n] = m2.sb(n, [P, HP])
            keep["vt"] = m2.sb("vt", [P, NT, D])
            keep["r2"] = m2.sb("r2", [P, HP, BANK])
            keep["qs0"] = m2.sb("qs0", [P, HP, 2, B, GAM, IB])
            project_phase(nc, ps, io, keep)
            attention_phase(nc, ps, io, keep)
        keep["x1"] = top.sb("x1", [P, NT, D])
        with Mem(nc) as m:
            keep["qwT"] = {w: m.sb(f"qwT_{w}", [P, len(chunks(XSHAPE[w][1])), XSHAPE[w][0]], BF16) for w in XW}
            keep["ws"] = m.sb("ws", [P, len(XW)])
            keep["bias"] = {w: m.sb(f"bias_{w}", [P, XSHAPE[w][0] // P]) for w in XW}
            keep["avg"] = m.sb("avg", [P, DC, B])
            keep["stats"] = m.sb("stats", [P, NT, 6])
            keep["most"] = m.sb("most", [P, B])
            keep["fused"] = keep["aT"][:].rearrange("p a g i -> p (a g i)").rearrange("p (c t) -> p c t", c=DC)
            with Mem(nc) as m2:
                keep["kvT"] = m2.sb("kvT", [P, 2, T])
                keep["kvt"] = m2.sb("kvt", [P, 2, NT, P])
                context_phase(nc, ps, io, keep)
                cross_phase(nc, ps, io, keep)
            feed_phase(nc, ps, io, keep)
        with Mem(nc) as m:
            keep["slot"] = m.sb("slot", [P, NT], U32)
            keep["tile_e"] = m.sb("tile_e", [1, SLOTS], I32)
            keep["rows"] = nc.dram_tensor("expert_rows", [SLOTS * P, D], F32).ap()
            keep["outs"] = nc.dram_tensor("expert_outs", [SLOTS * P, D], F32).ap()
            with Mem(nc) as m2:
                keep["w1T"] = m2.sb("w1T", [P, NE * DC * FF])
                keep["w2T"] = m2.sb("w2T", [P, NE * FFC * D])
                keep["stage"] = keep["aT"][:].rearrange("p a g i -> p (a g i)")
                route_phase(nc, ps, io, keep)
                expert_phase(nc, ps, io, keep)
            final_phase(nc, ps, io, keep, out)


_INS = ("x", "ctx_768") + tuple(f"L0_attn_{n}" for n in ("gamma", "beta", "Wq", "Wk", "Wv", "Wr", "u_bias", "v_bias", "Wo", "bo", "rel_pos_emb")) \
    + tuple(f"L0_xattn_{k}_{n}" for n in XW for k in ("W", "b")) \
    + tuple(f"L0_ffn_{n}" for n in ("Wr", "br", "W1", "b1", "W2", "b2"))


def kernel(**inputs):
    import numpy as _np
    import concourse.bacc as _bacc
    from concourse import mybir as _mybir
    from concourse.bass_utils import run_bass_kernel_spmd as _run

    nc = _bacc.Bacc("TRN2", target_bir_lowering=False, num_devices=1)
    arrays, io = {}, {}
    for name in _INS:
        a = _np.ascontiguousarray(inputs[name])
        arrays[f"in_{name}_dram"] = a
        io[name] = nc.dram_tensor(f"in_{name}_dram", a.shape, _mybir.dt.from_np(a.dtype), kind="ExternalInput").ap()
    out = nc.dram_tensor("out_0_dram", (B, L, D), F32, kind="ExternalOutput").ap()
    build(nc, io, out)
    r = _run(nc, [arrays], core_ids=[0])
    return r.results[0]["out_0_dram"]
```
